# Optimizing a Trainium2 kernel written in Bass

```python
import numpy as np
import jax
import jax.numpy as jnp

def _softmax(x, axis=-1):
    return jax.nn.softmax(x, axis=axis)

def _gelu(x):
    return jax.nn.gelu(x, approximate=True)

def _silu(x):
    return jax.nn.silu(x)

def _sigmoid(x):
    return jax.nn.sigmoid(x)

def _layernorm(x, axis=-1, eps=1e-05):
    m = jnp.mean(x, axis=axis, keepdims=True)
    v = jnp.var(x, axis=axis, keepdims=True)
    return (x - m) / jnp.sqrt(v + eps)

def _scatter_add(tgt, idx, src, axis=0):
    return tgt.at[idx].add(src)

def _segment_sum(src, seg, n):
    return jax.ops.segment_sum(src, seg, n)
kernel_name = 'mk_seq_postln_d4_jaxref_r8_7c9b19'

def setup_inputs(seed: int=0):
    np.random.seed(seed)
    _w = jnp.asarray

    def _L0_attn_setup():
        import jax, jax.numpy as jnp
        import numpy as np
        EMBED_DIM = 128
        NUM_HEADS = 16
        HEAD_DIM = EMBED_DIM // NUM_HEADS
        ROPE_BASE = 10000.0

        def rotate_half(x):
            d = x.shape[-1] // 2
            x1, x2 = (x[..., :d], x[..., d:])
            return jnp.concatenate((-x2, x1), axis=-1)
        key = jax.random.key(seed)
        k_x, k_wqkv, k_bqkv, k_wo, k_bo = jax.random.split(key, 5)
        C = EMBED_DIM
        x = jax.random.normal(k_x, (4, 256, C), dtype=jnp.float32)
        s = 1.0 / np.sqrt(C)
        W_qkv = jax.random.uniform(k_wqkv, (C, 3 * C), minval=-s, maxval=s, dtype=jnp.float32)
        b_qkv = jax.random.uniform(k_bqkv, (3 * C,), minval=-s, maxval=s, dtype=jnp.float32)
        W_out = jax.random.uniform(k_wo, (C, C), minval=-s, maxval=s, dtype=jnp.float32)
        b_out = jax.random.uniform(k_bo, (C,), minval=-s, maxval=s, dtype=jnp.float32)
        return {'x': x, 'W_qkv': W_qkv, 'b_qkv': b_qkv, 'W_out': W_out, 'b_out': b_out}
    _L0_attn_in = _L0_attn_setup()

    def _L0_ffn_setup():
        import jax, jax.numpy as jnp
        import numpy as np
        D_MODEL = 128
        key = jax.random.key(seed)
        k_x, k_w, k_a1, k_a2 = jax.random.split(key, 4)
        x = jax.random.normal(k_x, (4, 256, D_MODEL), dtype=jnp.float32)
        weight = jax.random.normal(k_w, (D_MODEL, D_MODEL), dtype=jnp.float32) * 0.02
        aux_weight1 = jax.random.normal(k_a1, (D_MODEL, D_MODEL), dtype=jnp.float32) * 0.02
        aux_weight2 = jax.random.normal(k_a2, (D_MODEL, D_MODEL), dtype=jnp.float32) * 0.02
        bias = jnp.zeros((D_MODEL,), dtype=jnp.float32)
        return {'x': x, 'weight': weight, 'aux_weight1': aux_weight1, 'aux_weight2': aux_weight2, 'bias': bias}
    _L0_ffn_in = _L0_ffn_setup()

    def _L1_attn_setup():
        import jax, jax.numpy as jnp
        import numpy as np
        D_MODEL = 128
        N_HEADS = 16
        HEAD_DIM = D_MODEL // N_HEADS
        WINDOW = 64
        PREFIX = 16
        B = 2
        S = 512

        def _windowed_global_attention(q, k, v):
            Bb, H, S_, Dh = q.shape
            W, P = (WINDOW, PREFIX)
            C = S_ // W
            scale = 1.0 / np.sqrt(Dh).astype(np.float32)
            qc = q.reshape(Bb, H, C, W, Dh)
            kp = jnp.pad(k, ((0, 0), (0, 0), (W, 0), (0, 0)))
            vp = jnp.pad(v, ((0, 0), (0, 0), (W, 0), (0, 0)))
            tail_idx = jnp.arange(C)[:, None] * W + jnp.arange(2 * W)[None, :]
            kt = kp[:, :, tail_idx, :]
            vt = vp[:, :, tail_idx, :]
            kg = k[:, :, :P, :]
            vg = v[:, :, :P, :]
            sg = jnp.einsum('bhcqd,bhkd->bhcqk', qc, kg) * scale
            st = jnp.einsum('bhcqd,bhckd->bhcqk', qc, kt) * scale
            q_pos = jnp.arange(C)[:, None] * W + jnp.arange(W)[None, :]
            kt_pos = jnp.arange(C)[:, None] * W - W + jnp.arange(2 * W)[None, :]
            mg = jnp.arange(P)[None, None, :] <= q_pos[:, :, None]
            diff = q_pos[:, :, None] - kt_pos[:, None, :]
            mt = (diff >= 0) & (diff < W) & (kt_pos[:, None, :] >= P)
            neg = jnp.asarray(-1000000000.0, sg.dtype)
            scores = jnp.concatenate([jnp.where(mg[None, None], sg, neg), jnp.where(mt[None, None], st, neg)], axis=-1)
            attn = jax.nn.softmax(scores, axis=-1)
            vcat = jnp.concatenate([jnp.broadcast_to(vg[:, :, None], (Bb, H, C, P, Dh)), vt], axis=3)
            out = jnp.einsum('bhcqk,bhckd->bhcqd', attn, vcat)
            return out.reshape(Bb, H, S_, Dh)
        key = jax.random.key(seed)
        k1, k2, k3 = jax.random.split(key, 3)
        x = jax.random.normal(k1, (B, S, D_MODEL), dtype=jnp.float32)
        w_qkv = jax.random.normal(k2, (3 * D_MODEL, D_MODEL), dtype=jnp.float32) * 0.02
        w_out = jax.random.normal(k3, (D_MODEL, D_MODEL), dtype=jnp.float32) * 0.02
        return {'x': x, 'w_qkv': w_qkv, 'w_out': w_out}
    _L1_attn_in = _L1_attn_setup()

    def _L1_ffn_setup():
        import jax, jax.numpy as jnp
        import numpy as np
        H = 128
        I = 256
        E = 32
        B, S = (4, 256)

        def _grouped_mm(a, w, group_sizes):
            return jax.lax.ragged_dot(a, w, group_sizes)

        def _swiglu(x, gw, uw, dw):
            return jax.nn.silu(x @ gw) * (x @ uw) @ dw
        key = jax.random.key(seed)
        ks = jax.random.split(key, 8)
        scale = 0.02
        inp = {'hidden_states': jax.random.normal(ks[0], (B, S, H), dtype=jnp.float32), 'gate_w': jax.random.normal(ks[1], (H, E), dtype=jnp.float32) * scale, 'shared_gate_w': jax.random.normal(ks[2], (H, I), dtype=jnp.float32) * scale, 'shared_up_w': jax.random.normal(ks[3], (H, I), dtype=jnp.float32) * scale, 'shared_down_w': jax.random.normal(ks[4], (I, H), dtype=jnp.float32) * scale, 'routed_gate_w': jax.random.normal(ks[5], (E, H, I), dtype=jnp.float32) * scale, 'routed_up_w': jax.random.normal(ks[6], (E, H, I), dtype=jnp.float32) * scale, 'routed_down_w': jax.random.normal(ks[7], (E, I, H), dtype=jnp.float32) * scale}
        return inp
    _L1_ffn_in = _L1_ffn_setup()

    def _L2_attn_setup():
        import jax, jax.numpy as jnp
        import numpy as np
        DIM = 128
        DIM_HEAD = 64
        HEADS = 8
        INNER = DIM_HEAD * HEADS
        SCALE = DIM_HEAD ** (-0.5)
        COS_SCALE = 1.0

        def layer_norm(x, w, b, eps=1e-05):
            mu = jnp.mean(x, axis=-1, keepdims=True)
            var = jnp.var(x, axis=-1, keepdims=True)
            return (x - mu) * jax.lax.rsqrt(var + eps) * w + b
        key = jax.random.key(seed)
        ks = jax.random.split(key, 6)
        x = jax.random.normal(ks[0], (4, 256, DIM), dtype=jnp.float32)
        Wq = jax.random.normal(ks[1], (DIM, INNER), dtype=jnp.float32) * DIM ** (-0.5)
        Wkv = jax.random.normal(ks[2], (DIM, 2 * DIM_HEAD), dtype=jnp.float32) * DIM ** (-0.5)
        Wo = jax.random.normal(ks[3], (INNER, DIM), dtype=jnp.float32) * INNER ** (-0.5)
        norm_w = jnp.ones((DIM,), jnp.float32)
        norm_b = jnp.zeros((DIM,), jnp.float32)
        out_norm_w = jnp.ones((DIM,), jnp.float32)
        out_norm_b = jnp.zeros((DIM,), jnp.float32)
        return {'x': x, 'Wq': Wq, 'Wkv': Wkv, 'Wo': Wo, 'norm_w': norm_w, 'norm_b': norm_b, 'out_norm_w': out_norm_w, 'out_norm_b': out_norm_b}
    _L2_attn_in = _L2_attn_setup()

    def _L2_ffn_setup():
        import jax, jax.numpy as jnp
        import numpy as np
        TOP_K = 2
        key = jax.random.key(seed)
        k1, k2, k3, k4 = jax.random.split(key, 4)
        B, T, D, H, E = (2, 256, 128, 256, 8)
        x = jax.random.normal(k1, (B, T, D), dtype=jnp.float32)
        w12 = jax.random.normal(k2, (E, 2 * H, D), dtype=jnp.float32) * D ** (-0.5)
        w3 = jax.random.normal(k3, (E, D, H), dtype=jnp.float32) * H ** (-0.5)
        gate_w = jax.random.normal(k4, (E, D), dtype=jnp.float32) * D ** (-0.5)
        return {'x': x, 'w12': w12, 'w3': w3, 'gate_w': gate_w}
    _L2_ffn_in = _L2_ffn_setup()

    def _L3_attn_setup():
        import jax, jax.numpy as jnp
        import numpy as np
        HEAD_SIZE = 64
        key = jax.random.key(seed)
        ks = jax.random.split(key, 5)
        B, N, D, H, E, O = (2, 256, 128, 16, HEAD_SIZE, 128)
        return {'query': jax.random.normal(ks[0], (B, N, D), dtype=jnp.float32), 'Wq': jax.random.normal(ks[1], (H, D, E), dtype=jnp.float32) / np.sqrt(D), 'Wk': jax.random.normal(ks[2], (H, D, E), dtype=jnp.float32) / np.sqrt(D), 'Wv': jax.random.normal(ks[3], (H, D, E), dtype=jnp.float32) / np.sqrt(D), 'Wp': jax.random.normal(ks[4], (H * E, O), dtype=jnp.float32) / np.sqrt(H * E), 'bp': jnp.zeros((O,), dtype=jnp.float32)}
    _L3_attn_in = _L3_attn_setup()

    def _L3_ffn_setup():
        import jax, jax.numpy as jnp
        import numpy as np
        D_IN, D_HID = (128, 512)

        def _ternary(key, shape):
            return jax.random.randint(key, shape, -1, 2).astype(jnp.float32)

        def _tlin(x, w, s):
            return jnp.einsum('bsi,oi->bso', x, w) * s
        key = jax.random.key(seed)
        ks = jax.random.split(key, 12)
        inv = lambda fan: 1.0 / np.sqrt(fan).astype(np.float32)
        return {'x': jax.random.normal(ks[0], (4, 256, D_IN), dtype=jnp.float32), 'w1_w': _ternary(ks[1], (D_HID, D_IN)), 'w1_s': jax.random.uniform(ks[2], (D_HID,), dtype=jnp.float32) * inv(D_IN), 'w2_w': _ternary(ks[3], (D_HID, D_IN)), 'w2_s': jax.random.uniform(ks[4], (D_HID,), dtype=jnp.float32) * inv(D_IN), 'h1_w': _ternary(ks[5], (D_HID, D_HID)), 'h1_s': jax.random.uniform(ks[6], (D_HID,), dtype=jnp.float32) * inv(D_HID), 'h2_w': _ternary(ks[7], (D_HID, D_HID)), 'h2_s': jax.random.uniform(ks[8], (D_HID,), dtype=jnp.float32) * inv(D_HID), 'w3_w': _ternary(ks[9], (D_IN, D_HID)), 'w3_s': jax.random.uniform(ks[10], (D_IN,), dtype=jnp.float32) * inv(D_HID)}
    _L3_ffn_in = _L3_ffn_setup()
    _d = {'L0_attn_x': _L0_attn_in['x'], 'L0_attn_W_qkv': _L0_attn_in['W_qkv'], 'L0_attn_b_qkv': _L0_attn_in['b_qkv'], 'L0_attn_W_out': _L0_attn_in['W_out'], 'L0_attn_b_out': _L0_attn_in['b_out'], 'L0_ffn_weight': _L0_ffn_in['weight'], 'L0_ffn_aux_weight1': _L0_ffn_in['aux_weight1'], 'L0_ffn_aux_weight2': _L0_ffn_in['aux_weight2'], 'L0_ffn_bias': _L0_ffn_in['bias'], 'L1_attn_w_qkv': _L1_attn_in['w_qkv'], 'L1_attn_w_out': _L1_attn_in['w_out'], 'L1_ffn_gate_w': _L1_ffn_in['gate_w'], 'L1_ffn_shared_gate_w': _L1_ffn_in['shared_gate_w'], 'L1_ffn_shared_up_w': _L1_ffn_in['shared_up_w'], 'L1_ffn_shared_down_w': _L1_ffn_in['shared_down_w'], 'L1_ffn_routed_gate_w': _L1_ffn_in['routed_gate_w'], 'L1_ffn_routed_up_w': _L1_ffn_in['routed_up_w'], 'L1_ffn_routed_down_w': _L1_ffn_in['routed_down_w'], 'L2_attn_Wq': _L2_attn_in['Wq'], 'L2_attn_Wkv': _L2_attn_in['Wkv'], 'L2_attn_Wo': _L2_attn_in['Wo'], 'L2_attn_norm_w': _L2_attn_in['norm_w'], 'L2_attn_norm_b': _L2_attn_in['norm_b'], 'L2_attn_out_norm_w': _L2_attn_in['out_norm_w'], 'L2_attn_out_norm_b': _L2_attn_in['out_norm_b'], 'L2_ffn_w12': _L2_ffn_in['w12'], 'L2_ffn_w3': _L2_ffn_in['w3'], 'L2_ffn_gate_w': _L2_ffn_in['gate_w'], 'L3_attn_Wq': _L3_attn_in['Wq'], 'L3_attn_Wk': _L3_attn_in['Wk'], 'L3_attn_Wv': _L3_attn_in['Wv'], 'L3_attn_Wp': _L3_attn_in['Wp'], 'L3_attn_bp': _L3_attn_in['bp'], 'L3_ffn_w1_w': _L3_ffn_in['w1_w'], 'L3_ffn_w1_s': _L3_ffn_in['w1_s'], 'L3_ffn_w2_w': _L3_ffn_in['w2_w'], 'L3_ffn_w2_s': _L3_ffn_in['w2_s'], 'L3_ffn_h1_w': _L3_ffn_in['h1_w'], 'L3_ffn_h1_s': _L3_ffn_in['h1_s'], 'L3_ffn_h2_w': _L3_ffn_in['h2_w'], 'L3_ffn_h2_s': _L3_ffn_in['h2_s'], 'L3_ffn_w3_w': _L3_ffn_in['w3_w'], 'L3_ffn_w3_s': _L3_ffn_in['w3_s']}
    _x0 = _d['L0_attn_x']
    _d['L0_attn_x'] = jax.random.normal(jax.random.fold_in(jax.random.key(seed), 1), (2, 1024, 128), dtype=_x0.dtype)
    del _x0
    return _d

def reference(L0_attn_x, L0_attn_W_qkv, L0_attn_b_qkv, L0_attn_W_out, L0_attn_b_out, L0_ffn_weight, L0_ffn_aux_weight1, L0_ffn_aux_weight2, L0_ffn_bias, L1_attn_w_qkv, L1_attn_w_out, L1_ffn_gate_w, L1_ffn_shared_gate_w, L1_ffn_shared_up_w, L1_ffn_shared_down_w, L1_ffn_routed_gate_w, L1_ffn_routed_up_w, L1_ffn_routed_down_w, L2_attn_Wq, L2_attn_Wkv, L2_attn_Wo, L2_attn_norm_w, L2_attn_norm_b, L2_attn_out_norm_w, L2_attn_out_norm_b, L2_ffn_w12, L2_ffn_w3, L2_ffn_gate_w, L3_attn_Wq, L3_attn_Wk, L3_attn_Wv, L3_attn_Wp, L3_attn_bp, L3_ffn_w1_w, L3_ffn_w1_s, L3_ffn_w2_w, L3_ffn_w2_s, L3_ffn_h1_w, L3_ffn_h1_s, L3_ffn_h2_w, L3_ffn_h2_s, L3_ffn_w3_w, L3_ffn_w3_s):

    def _L0_attn_ref(x, W_qkv, b_qkv, W_out, b_out):
        import jax, jax.numpy as jnp
        import numpy as np
        EMBED_DIM = 128
        NUM_HEADS = 16
        HEAD_DIM = EMBED_DIM // NUM_HEADS
        ROPE_BASE = 10000.0

        def rotate_half(x):
            d = x.shape[-1] // 2
            x1, x2 = (x[..., :d], x[..., d:])
            return jnp.concatenate((-x2, x1), axis=-1)
        B, T, C = x.shape
        H, Dh = (NUM_HEADS, HEAD_DIM)
        qkv = (x @ W_qkv + b_qkv).reshape(B, T, 3, H, Dh).transpose(2, 0, 3, 1, 4)
        q, k, v = (qkv[0], qkv[1], qkv[2])
        inv_freq = 1.0 / ROPE_BASE ** (jnp.arange(0, Dh, 2, dtype=jnp.float32) / Dh)
        freqs = jnp.arange(T, dtype=jnp.float32)[:, None] * inv_freq[None, :]
        emb = jnp.concatenate((freqs, freqs), axis=-1)
        cos, sin = (jnp.cos(emb), jnp.sin(emb))
        q = q * cos + rotate_half(q) * sin
        k = k * cos + rotate_half(k) * sin
        scale = 1.0 / np.sqrt(Dh)
        attn = jax.nn.softmax(jnp.einsum('bhqd,bhkd->bhqk', q, k) * scale, axis=-1)
        out = jnp.einsum('bhqk,bhkd->bhqd', attn, v)
        out = out.transpose(0, 2, 1, 3).reshape(B, T, C)
        return out @ W_out + b_out

    def _L0_ffn_ref(x, weight, aux_weight1, aux_weight2, bias):
        import jax, jax.numpy as jnp
        import numpy as np
        D_MODEL = 128
        h = jnp.einsum('btc,cd->btd', x, weight)
        h = jnp.einsum('btc,cd->btd', h, aux_weight1)
        h = jnp.einsum('btc,cd->btd', h, aux_weight2)
        return jnp.tanh(h + bias)

    def _L1_attn_ref(x, w_qkv, w_out):
        import jax, jax.numpy as jnp
        import numpy as np
        D_MODEL = 128
        N_HEADS = 16
        HEAD_DIM = D_MODEL // N_HEADS
        WINDOW = 64
        PREFIX = 16
        B = 2
        S = 512

        def _windowed_global_attention(q, k, v):
            Bb, H, S_, Dh = q.shape
            W, P = (WINDOW, PREFIX)
            C = S_ // W
            scale = 1.0 / np.sqrt(Dh).astype(np.float32)
            qc = q.reshape(Bb, H, C, W, Dh)
            kp = jnp.pad(k, ((0, 0), (0, 0), (W, 0), (0, 0)))
            vp = jnp.pad(v, ((0, 0), (0, 0), (W, 0), (0, 0)))
            tail_idx = jnp.arange(C)[:, None] * W + jnp.arange(2 * W)[None, :]
            kt = kp[:, :, tail_idx, :]
            vt = vp[:, :, tail_idx, :]
            kg = k[:, :, :P, :]
            vg = v[:, :, :P, :]
            sg = jnp.einsum('bhcqd,bhkd->bhcqk', qc, kg) * scale
            st = jnp.einsum('bhcqd,bhckd->bhcqk', qc, kt) * scale
            q_pos = jnp.arange(C)[:, None] * W + jnp.arange(W)[None, :]
            kt_pos = jnp.arange(C)[:, None] * W - W + jnp.arange(2 * W)[None, :]
            mg = jnp.arange(P)[None, None, :] <= q_pos[:, :, None]
            diff = q_pos[:, :, None] - kt_pos[:, None, :]
            mt = (diff >= 0) & (diff < W) & (kt_pos[:, None, :] >= P)
            neg = jnp.asarray(-1000000000.0, sg.dtype)
            scores = jnp.concatenate([jnp.where(mg[None, None], sg, neg), jnp.where(mt[None, None], st, neg)], axis=-1)
            attn = jax.nn.softmax(scores, axis=-1)
            vcat = jnp.concatenate([jnp.broadcast_to(vg[:, :, None], (Bb, H, C, P, Dh)), vt], axis=3)
            out = jnp.einsum('bhcqk,bhckd->bhcqd', attn, vcat)
            return out.reshape(Bb, H, S_, Dh)
        Bb, S_, Dm = x.shape
        qkv = x @ w_qkv.T
        q, k, v = jnp.split(qkv, 3, axis=-1)

        def heads(t):
            return t.reshape(Bb, S_, N_HEADS, HEAD_DIM).transpose(0, 2, 1, 3)
        q, k, v = (heads(q), heads(k), heads(v))
        o = _windowed_global_attention(q, k, v)
        o = o.transpose(0, 2, 1, 3).reshape(Bb, S_, Dm)
        return o @ w_out.T

    def _L1_ffn_ref(hidden_states, gate_w, shared_gate_w, shared_up_w, shared_down_w, routed_gate_w, routed_up_w, routed_down_w):
        import jax, jax.numpy as jnp
        import numpy as np
        H = 128
        I = 256
        E = 32
        B, S = (4, 256)

        def _grouped_mm(a, w, group_sizes):
            return jax.lax.ragged_dot(a, w, group_sizes)

        def _swiglu(x, gw, uw, dw):
            return jax.nn.silu(x @ gw) * (x @ uw) @ dw
        b, s, h = hidden_states.shape
        x = hidden_states.reshape(-1, h)
        shared_out = _swiglu(x, shared_gate_w, shared_up_w, shared_down_w)
        logits = x @ gate_w
        topk_ids = jnp.argmax(logits, axis=-1)
        topk_val = jnp.max(logits, axis=-1)
        scores = jax.nn.sigmoid(topk_val)[:, None]
        xs = x * scores
        tokens_per_expert = jnp.zeros((E,), jnp.int32).at[topk_ids].add(1)
        order = jnp.argsort(topk_ids)
        sorted_x = xs[order]
        g = _grouped_mm(sorted_x, routed_gate_w, tokens_per_expert)
        u = _grouped_mm(sorted_x, routed_up_w, tokens_per_expert)
        d = _grouped_mm(jax.nn.silu(g) * u, routed_down_w, tokens_per_expert)
        inv = jnp.argsort(order)
        routed_out = d[inv]
        return (shared_out + routed_out).reshape(b, s, h)

    def _L2_attn_ref(x, Wq, Wkv, Wo, norm_w, norm_b, out_norm_w, out_norm_b):
        import jax, jax.numpy as jnp
        import numpy as np
        DIM = 128
        DIM_HEAD = 64
        HEADS = 8
        INNER = DIM_HEAD * HEADS
        SCALE = DIM_HEAD ** (-0.5)
        COS_SCALE = 1.0

        def layer_norm(x, w, b, eps=1e-05):
            mu = jnp.mean(x, axis=-1, keepdims=True)
            var = jnp.var(x, axis=-1, keepdims=True)
            return (x - mu) * jax.lax.rsqrt(var + eps) * w + b
        b, n, _ = x.shape
        xn = layer_norm(x, norm_w, norm_b)
        q = xn @ Wq
        kv = xn @ Wkv
        k, v = (kv[..., :DIM_HEAD], kv[..., DIM_HEAD:])
        q = q.reshape(b, n, HEADS, DIM_HEAD).transpose(0, 2, 1, 3) * SCALE
        sim = jnp.einsum('bhid,bjd->bhij', q, k) * COS_SCALE
        attn = jax.nn.softmax(sim.astype(jnp.float32), axis=-1).astype(sim.dtype)
        out = jnp.einsum('bhij,bjd->bhid', attn, v)
        out = out.transpose(0, 2, 1, 3).reshape(b, n, INNER)
        out = out @ Wo
        return layer_norm(out, out_norm_w, out_norm_b)

    def _L2_ffn_ref(x, w12, w3, gate_w):
        import jax, jax.numpy as jnp
        import numpy as np
        TOP_K = 2
        E = gate_w.shape[0]
        H = w3.shape[-1]
        scores = jnp.einsum('btd,ed->bte', x, gate_w)
        topk_scores, topk_idx = jax.lax.top_k(scores, TOP_K)
        topk_probs = jax.nn.softmax(topk_scores, axis=-1)
        total_probs = jnp.sum(jax.nn.one_hot(topk_idx, E, dtype=topk_probs.dtype) * topk_probs[..., None], axis=-2)
        h12 = jnp.einsum('btd,ehd->bteh', x, w12)
        h1, h2 = (h12[..., :H], h12[..., H:])
        hidden = jax.nn.silu(h1) * h2
        expert_out = jnp.einsum('bteh,edh->bted', hidden, w3)
        y = jnp.sum(total_probs[..., None] * expert_out, axis=-2)
        return y

    def _L3_attn_ref(query, Wq, Wk, Wv, Wp, bp):
        import jax, jax.numpy as jnp
        import numpy as np
        HEAD_SIZE = 64
        B, N, D = query.shape
        H, _, E = Wq.shape
        scale = 1.0 / jnp.sqrt(jnp.asarray(E, query.dtype))
        q = jnp.einsum('bnd,hde->bhne', query, Wq) * scale
        k = jnp.einsum('bmd,hde->bhme', query, Wk)
        v = jnp.einsum('bmd,hde->bhme', query, Wv)
        logits = jnp.einsum('bhne,bhme->bhnm', q, k)
        attn = jax.nn.softmax(logits, axis=-1)
        out = jnp.einsum('bhnm,bhme->bnhe', attn, v)
        out = jnp.swapaxes(out, -1, -2).reshape(B, N, E * H)
        return jnp.dot(out, Wp) + bp

    def _L3_ffn_ref(x, w1_w, w1_s, w2_w, w2_s, h1_w, h1_s, h2_w, h2_s, w3_w, w3_s):
        import jax, jax.numpy as jnp
        import numpy as np
        D_IN, D_HID = (128, 512)

        def _ternary(key, shape):
            return jax.random.randint(key, shape, -1, 2).astype(jnp.float32)

        def _tlin(x, w, s):
            return jnp.einsum('bsi,oi->bso', x, w) * s
        h = jax.nn.silu(_tlin(x, w1_w, w1_s)) * _tlin(x, w2_w, w2_s)
        h = jax.nn.gelu(_tlin(h, h1_w, h1_s), approximate=False)
        h = jax.nn.gelu(_tlin(h, h2_w, h2_s), approximate=False)
        return _tlin(h, w3_w, w3_s)
    x = L0_attn_x
    x = _layernorm(x + _L0_attn_ref(x, L0_attn_W_qkv, L0_attn_b_qkv, L0_attn_W_out, L0_attn_b_out), axis=-1)
    x = _layernorm(x + _L0_ffn_ref(x, L0_ffn_weight, L0_ffn_aux_weight1, L0_ffn_aux_weight2, L0_ffn_bias), axis=-1)
    x = _layernorm(x + _L1_attn_ref(x, L1_attn_w_qkv, L1_attn_w_out), axis=-1)
    x = _layernorm(x + _L1_ffn_ref(x, L1_ffn_gate_w, L1_ffn_shared_gate_w, L1_ffn_shared_up_w, L1_ffn_shared_down_w, L1_ffn_routed_gate_w, L1_ffn_routed_up_w, L1_ffn_routed_down_w), axis=-1)
    x = _layernorm(x + _L2_attn_ref(x, L2_attn_Wq, L2_attn_Wkv, L2_attn_Wo, L2_attn_norm_w, L2_attn_norm_b, L2_attn_out_norm_w, L2_attn_out_norm_b), axis=-1)
    x = _layernorm(x + _L2_ffn_ref(x, L2_ffn_w12, L2_ffn_w3, L2_ffn_gate_w), axis=-1)
    x = _layernorm(x + _L3_attn_ref(x, L3_attn_Wq, L3_attn_Wk, L3_attn_Wv, L3_attn_Wp, L3_attn_bp), axis=-1)
    x = _layernorm(x + _L3_ffn_ref(x, L3_ffn_w1_w, L3_ffn_w1_s, L3_ffn_w2_w, L3_ffn_w2_s, L3_ffn_h1_w, L3_ffn_h1_s, L3_ffn_h2_w, L3_ffn_h2_s, L3_ffn_w3_w, L3_ffn_w3_s), axis=-1)
    return x

_drawn_inputs = setup_inputs


def setup_inputs(seed=0):
    import zlib

    import numpy as np

    out = dict(_drawn_inputs(seed))
    spreads = {'L0_ffn_bias': (0.0, 0.1),
     'L2_attn_norm_w': (1.0, 0.2),
     'L2_attn_norm_b': (0.0, 0.1),
     'L2_attn_out_norm_w': (1.0, 0.2),
     'L2_attn_out_norm_b': (0.0, 0.1),
     'L3_attn_bp': (0.0, 0.1)}
    factors = {'L1_ffn_gate_w': 5.017,
     'L1_ffn_shared_gate_w': 3.88,
     'L1_ffn_shared_up_w': 3.664,
     'L1_ffn_shared_down_w': 3.782,
     'L1_ffn_routed_gate_w': 6.806,
     'L1_ffn_routed_up_w': 6.507,
     'L1_ffn_routed_down_w': 5.817,
     'L3_ffn_w1_w': 8.0,
     'L3_ffn_w1_s': 8.0,
     'L3_ffn_w2_w': 8.0,
     'L3_ffn_w2_s': 8.0,
     'L3_ffn_h1_w': 8.0,
     'L3_ffn_h1_s': 8.0,
     'L3_ffn_h2_w': 8.0,
     'L3_ffn_h2_s': 8.0,
     'L3_ffn_w3_w': 8.0,
     'L3_ffn_w3_s': 8.0}
    for name, (base, spread) in spreads.items():
        noise = np.random.default_rng([zlib.crc32(name.encode()), seed]).standard_normal(out[name].shape)
        drawn = base * np.exp(spread * noise) if base else spread * noise
        out[name] = jnp.asarray(drawn.astype(out[name].dtype))
    for name, factor in factors.items():
        out[name] = (out[name] * factor).astype(out[name].dtype)
    return out
```

```python
import numpy as np
from contextlib import ExitStack

import concourse.bass as bass
from concourse import mybir

F32 = mybir.dt.float32
F32R = mybir.dt.float32r
BF16 = mybir.dt.bfloat16
ALU = mybir.AluOpType
ACT = mybir.ActivationFunctionType
AX = mybir.AxisListType

P = 128
BATCH = 2
SEQ = 1024
C = 128
TOKENS = BATCH * SEQ
TILES = TOKENS // P
QB = SEQ // P
HALF = 512
CHUNKS = TOKENS // HALF
EPS = 1e-5
MASKED = -1e9
WINDOW = 64
PREFIX = 16


class Stage:

    def __init__(self, nc, name):
        self.nc, self.name = nc, name
        self.ctx, self.sems = ExitStack(), []

    def __enter__(self):
        return self

    def sb(self, name, shape, dt=F32):
        return self.ctx.enter_context(self.nc.sbuf_tensor(f"{self.name}_{name}", shape, dt))

    def ps(self, name, shape):
        return self.ctx.enter_context(self.nc.psum_tensor(f"{self.name}_{name}", shape, F32))

    def sem(self, name):
        self.sems.append(self.nc.alloc_semaphore(f"{self.name}_{name}"))
        return self.sems[-1]

    def begin(self):
        self.guard = self.nc.Block()
        return self.guard.__enter__()

    def __exit__(self, *e):
        if e[0] is not None:
            return False
        self.guard.__exit__(None, None, None)
        self.nc.clear_and_free_semaphores(self.sems)
        self.nc.all_engine_barrier()
        self.ctx.close()
        return False


class Persistent:

    def __init__(self, nc, ctx):
        def sb(name, shape, dt=F32):
            return ctx.enter_context(nc.sbuf_tensor(name, shape, dt))
        self.x_rows = sb("x_rows", [P, TILES, C])
        self.x_cols = sb("x_cols", [C, TOKENS])
        self.acc = sb("acc", [P, TILES, C])
        self.ident = sb("identity", [P, P])
        self.ones_row = sb("ones_row", [1, P])


def span(start, n):
    return slice(start, start + n) if isinstance(start, int) else bass.ds(start, n)


def tile_bcast(row_bc):
    return row_bc[:, :].unsqueeze(1).to_broadcast([P, TILES, C])



def load_stage(nc, per, x, ident):
    with Stage(nc, "load") as st:
        tr = st.ps("tr", [P, CHUNKS, HALF])
        x_in, id_in = st.sem("x_in"), st.sem("id_in")
        transposed, ones_set, copied = st.sem("transposed"), st.sem("ones_set"), st.sem("copied")
        block = st.begin()

        @block.sync
        def _(sp):
            sp.dma_start(per.ident[:, :], ident).then_inc(id_in, 16)
            xv = x.rearrange("b (q p) c -> p (b q) c", p=P)
            sp.dma_start(per.x_rows[:, :, :], xv).then_inc(x_in, 16)

        @block.vector
        def _(dve):
            nc.vector.memset(per.ones_row[:, :], 1.0).then_inc(ones_set, 1)

        @block.tensor
        def _(pe):
            pe.wait_ge(id_in, 16)
            pe.wait_ge(x_in, 16)
            for t in range(TILES):
                nc.tensor.transpose(tr[:, t // 4, (t % 4) * P:(t % 4 + 1) * P], per.x_rows[:, t, :],
                                    per.ident[:, :]).then_inc(transposed, 1)

        @block.scalar
        def _(act):
            for c in range(CHUNKS):
                act.wait_ge(transposed, 4 * c + 4)
                nc.scalar.activation(per.x_cols[:, c * HALF:(c + 1) * HALF], tr[:, c, :],
                                     ACT.Copy).then_inc(copied, 1)


def norm_stage(nc, per, name, src, dst, bias=None, affine=None, plus=None, to_cols=True):
    with Stage(nc, name) as st:
        stats = st.sb("stats", [P, TILES, 6])
        moments = st.sb("moments", [P, TILES, 2])
        var = st.sb("var", [P, TILES])
        power = st.sb("power", [P, TILES])
        rstd = st.sb("rstd", [P, TILES])
        rows_bc = st.sb("rows_bc", [P, 3, C])
        tr = st.ps("tr", [P, CHUNKS, HALF])
        rows_in = st.sem("rows_in")
        biased, stats_done = st.sem("biased"), st.sem("stats_done")
        moments_ready, rstd_ready = st.sem("moments_ready"), st.sem("rstd_ready")
        var_ready, power_set = st.sem("var_ready"), st.sem("power_set")
        normed, scaled = st.sem("normed"), st.sem("scaled")
        transposed, copied = st.sem("transposed"), st.sem("copied")
        block = st.begin()
        rows = [r for r in ([bias] if bias is not None else []) + list(affine or [])]

        @block.sync
        def _(sp):
            for k, r in enumerate(rows):
                sp.dma_start(rows_bc[:, k, :],
                             r.rearrange("(a c) -> a c", a=1).partition_broadcast(P)
                             .rearrange("p a c -> p (a c)")).then_inc(rows_in, 16)

        @block.vector
        def _(dve):
            if rows:
                dve.wait_ge(rows_in, 16 * len(rows))
            if bias is not None:
                nc.vector.tensor_tensor(src[:, :, :], src[:, :, :], tile_bcast(rows_bc[:, 0, :]),
                                        ALU.add).then_inc(biased, 1)
                dve.wait_ge(biased, 1)
            for t in range(TILES):
                nc.vector.bn_stats(stats[:, t, :], src[:, t, :]).then_inc(stats_done, 1)
            for t in range(TILES):
                dve.wait_ge(stats_done, t + 1)
                nc.vector.bn_aggr(moments[:, t, :], stats[:, t, :]).then_inc(moments_ready, 1)
            dve.wait_ge(moments_ready, TILES)
            nc.vector.tensor_scalar(var[:, :], moments[:, :, 1], EPS, None, ALU.add).then_inc(var_ready, 1)
            dve.wait_ge(rstd_ready, 1)
            for t in range(TILES):
                nc.vector.tensor_scalar(dst[:, t, :], src[:, t, :], moments[:, t, 0:1],
                                        rstd[:, t:t + 1], ALU.subtract, ALU.mult).then_inc(normed, 1)
            if affine is not None:
                k = len(rows) - 2
                dve.wait_ge(normed, TILES)
                nc.vector.tensor_tensor(dst[:, :, :], dst[:, :, :], tile_bcast(rows_bc[:, k, :]),
                                        ALU.mult).then_inc(scaled, 1)
                dve.wait_ge(scaled, 1)
                nc.vector.tensor_tensor(dst[:, :, :], dst[:, :, :], tile_bcast(rows_bc[:, k + 1, :]),
                                        ALU.add).then_inc(scaled, 1)
                if plus is not None:
                    dve.wait_ge(scaled, 2)
                    nc.vector.tensor_tensor(dst[:, :, :], dst[:, :, :], plus[:, :, :],
                                            ALU.add).then_inc(scaled, 1)

        @block.gpsimd
        def _(pool):
            nc.gpsimd.memset(power[:, :], -0.5).then_inc(power_set, 1)
            pool.wait_ge(power_set, 1)
            pool.wait_ge(var_ready, 1)
            nc.gpsimd.tensor_tensor(rstd[:, :], var[:, :], power[:, :], ALU.pow).then_inc(rstd_ready, 1)

        if to_cols:
            @block.tensor
            def _(pe):
                if affine is not None:
                    pe.wait_ge(scaled, 2)
                for t in range(TILES):
                    pe.wait_ge(normed, t + 1)
                    nc.tensor.transpose(tr[:, t // 4, (t % 4) * P:(t % 4 + 1) * P], dst[:, t, :],
                                        per.ident[:, :]).then_inc(transposed, 1)

            @block.scalar
            def _(act):
                for c in range(CHUNKS):
                    act.wait_ge(transposed, 4 * c + 4)
                    nc.scalar.activation(per.x_cols[:, c * HALF:(c + 1) * HALF], tr[:, c, :],
                                         ACT.Copy).then_inc(copied, 1)


def store_stage(nc, per, out):
    with Stage(nc, "store") as st:
        stored = st.sem("stored")
        block = st.begin()

        @block.sync
        def _(sp):
            sp.dma_start(out.rearrange("b (q p) c -> p (b q) c", p=P),
                         per.x_rows[:, :, :]).then_inc(stored, 16)
            sp.wait_ge(stored, 16)



D8 = 8
H8 = 16


class SmallHeads:

    def __init__(self, nc, st):
        self.stacks = {x: nc.dram_tensor(f"{st.name}_stack_{x}", (H8 * 4 * D8, TOKENS), F32).ap() for x in "qk"}
        self.v_rows = st.sb("v_rows", [P, TILES, H8 * (D8 + 1)])
        self.w_out = st.sb("w_out_flipped", [C, C])


def small_qkv_stage(nc, per, name, heads, w_in, w_out, bias, rope):
    w_transposed = w_out is not None
    with Stage(nc, name) as st:
        w_raw = st.sb("w_raw", [P, 4, P])
        w = st.sb("w", [P, 3, P])
        acc_ps = st.ps("acc_ps", [P, 4, HALF])
        rot_ps = st.ps("rot_ps", [P, 4, HALF])
        parts = {n: st.sb(n, [P, TOKENS], F32R) for n in ("qh", "ql", "kh", "kl")}
        flat = st.sb("flat", [P, 2, HALF])
        t_cos = st.sb("t_cos", [P, 2, HALF])
        t_sin = st.sb("t_sin", [P, 2, HALF])
        roped = st.sb("roped", [P, 2, HALF])
        b_cols = st.sb("b_cols", [P, 2])
        b_row = st.sb("b_row", [1, C])
        rot = st.sb("rot", [P, P])
        cos = st.sb("cos", [P, SEQ])
        sin = st.sb("sin", [P, SEQ])
        loaded, w_flipped, w_ready = st.sem("loaded"), st.sem("w_flipped"), st.sem("w_ready")
        proj_done, flat_ready, rot_done = st.sem("proj_done"), st.sem("flat_ready"), st.sem("rot_done")
        cos_done, sin_done, roped_ready = st.sem("cos_done"), st.sem("sin_done"), st.sem("roped_ready")
        high_ready, low_ready, stacked = st.sem("high_ready"), st.sem("low_ready"), st.sem("stacked")
        v_done, v_copied, ones_set = st.sem("v_done"), st.sem("v_copied"), st.sem("ones_set")
        n_loads = 1 + w_transposed + (3 if bias is not None else 0) + (3 if rope is not None else 0)
        steps = [(x, c) for x in range(2) for c in range(CHUNKS)]
        block = st.begin()

        @block.sync
        def _(sp):
            if w_transposed:
                sp.dma_start(w_raw[:, 0:3, :], w_in.rearrange("(a o) i -> o a i", a=3)).then_inc(loaded, 16)
                sp.dma_start(w_raw[:, 3, :], w_out).then_inc(loaded, 16)
            else:
                sp.dma_start(w[:, :, :], w_in.rearrange("i (a o) -> i a o", a=3)).then_inc(loaded, 16)
            if bias is not None:
                for x in range(2):
                    sp.dma_start(b_cols[:, x:x + 1],
                                 bias[x * C:(x + 1) * C].rearrange("(p a) -> p a", a=1)).then_inc(loaded, 16)
                sp.dma_start(b_row[:, :], bias[2 * C:3 * C].rearrange("(a c) -> a c", a=1)).then_inc(loaded, 16)
            if rope is not None:
                for dst, src in zip((rot, cos, sin), rope):
                    sp.dma_start(dst[:, :], src).then_inc(loaded, 16)
            for n, (x, c) in enumerate(steps):
                cols = slice(c * HALF, (c + 1) * HALF)
                stack = heads.stacks["qk"[x]].rearrange("(h r d) t -> h r d t", r=4, d=D8)
                sp.wait_ge(low_ready, n + 1)
                for r, part in enumerate(("hhll", "hlhl")[x]):
                    sp.dma_start(stack[:, r, :, cols],
                                 parts["qk"[x] + part][:, cols].bitcast(F32)).then_inc(stacked, 16)
            sp.wait_ge(stacked, 16 * 4 * len(steps))

        @block.tensor
        def _(pe):
            pe.wait_ge(loaded, 16 * n_loads)
            if w_transposed:
                for a in range(4):
                    nc.tensor.transpose(acc_ps[:, 0, a * P:(a + 1) * P], w_raw[:, a, :],
                                        per.ident[:, :]).then_inc(w_flipped, 1)
                pe.wait_ge(w_ready, 2)

            def rotate(n):
                pe.wait_ge(flat_ready, n + 1)
                if n >= 4:
                    pe.wait_ge(sin_done, n - 3)
                nc.tensor.matmul(rot_ps[:, n % 4, :], rot[:, :], flat[:, n % 2, :],
                                 start=True, stop=True).then_inc(rot_done, 1)

            for n, (x, c) in enumerate(steps):
                if n >= 4:
                    pe.wait_ge(flat_ready if rope is not None else low_ready, n - 3)
                nc.tensor.matmul(acc_ps[:, n % 4, :], w[:, x, :], per.x_cols[:, c * HALF:(c + 1) * HALF],
                                 start=True, stop=True).then_inc(proj_done, 1)
                if rope is not None and n >= 1:
                    rotate(n - 1)
            if rope is not None:
                rotate(len(steps) - 1)
            pe.wait_ge(flat_ready if rope is not None else low_ready, len(steps))
            for t in range(TILES):
                if bias is not None:
                    nc.tensor.matmul(acc_ps[:, t // 4, (t % 4) * P:(t % 4 + 1) * P], per.ones_row[:, :],
                                     b_row[:, :], start=True, stop=False)
                nc.tensor.matmul(acc_ps[:, t // 4, (t % 4) * P:(t % 4 + 1) * P],
                                 per.x_cols[:, t * P:(t + 1) * P], w[:, 2, :],
                                 start=bias is None, stop=True).then_inc(v_done, 1)

        @block.scalar
        def _(act):
            if w_transposed:
                act.wait_ge(w_flipped, 4)
                nc.scalar.activation(heads.w_out[:, :], acc_ps[:, 0, 3 * P:4 * P], ACT.Copy).then_inc(w_ready, 1)
                nc.scalar.activation(w[:, :, :], acc_ps[:, 0, 0:3 * P].rearrange("p (a o) -> p a o", a=3),
                                     ACT.Copy).then_inc(w_ready, 1)
            if rope is not None:
                for n, (x, c) in enumerate(steps):
                    act.wait_ge(proj_done, n + 1)
                    if n >= 2:
                        act.wait_ge(rot_done, n - 1)
                        act.wait_ge(cos_done, n - 1)
                    nc.scalar.activation(flat[:, n % 2, :], acc_ps[:, n % 4, :], ACT.Identity,
                                         bias=b_cols[:, x:x + 1]).then_inc(flat_ready, 1)
            act.wait_ge(ones_set, 1)
            for c in range(CHUNKS):
                act.wait_ge(v_done, 4 * c + 4)
                nc.scalar.activation(
                    heads.v_rows[:, 4 * c:4 * c + 4, :].rearrange("p t (h d) -> p t h d", d=D8 + 1)[:, :, :, 0:D8],
                    acc_ps[:, c, :].rearrange("p (t h d) -> p t h d", t=4, d=D8), ACT.Copy).then_inc(v_copied, 1)

        @block.gpsimd
        def _(pool):
            nc.gpsimd.memset(heads.v_rows[:, :, :], 1.0).then_inc(ones_set, 1)
            if rope is not None:
                for n, (x, c) in enumerate(steps):
                    pool.wait_ge(flat_ready, n + 1)
                    if n >= 2:
                        pool.wait_ge(roped_ready, n - 1)
                    at = (c % 2) * HALF
                    nc.gpsimd.tensor_tensor(t_cos[:, n % 2, :], flat[:, n % 2, :], cos[:, at:at + HALF],
                                            ALU.mult).then_inc(cos_done, 1)

        @block.vector
        def _(dve):
            for n, (x, c) in enumerate(steps):
                high, low = [parts["qk"[x] + s][:, c * HALF:(c + 1) * HALF] for s in "hl"]
                if rope is not None:
                    at = (c % 2) * HALF
                    dve.wait_ge(rot_done, n + 1)
                    nc.vector.tensor_tensor(t_sin[:, n % 2, :], rot_ps[:, n % 4, :], sin[:, at:at + HALF],
                                            ALU.mult).then_inc(sin_done, 1)
                    dve.wait_ge(sin_done, n + 1)
                    dve.wait_ge(cos_done, n + 1)
                    nc.vector.tensor_tensor(roped[:, n % 2, :], t_cos[:, n % 2, :], t_sin[:, n % 2, :],
                                            ALU.add).then_inc(roped_ready, 1)
                    dve.wait_ge(roped_ready, n + 1)
                    value = roped[:, n % 2, :]
                else:
                    dve.wait_ge(proj_done, n + 1)
                    value = acc_ps[:, n % 4, :]
                nc.vector.tensor_copy(high, value).then_inc(high_ready, 1)
                dve.wait_ge(high_ready, n + 1)
                nc.vector.tensor_tensor(low, value, high.bitcast(F32), ALU.subtract).then_inc(low_ready, 1)



class Jobs:

    def __init__(self, steps, q_uses, r_uses, m_uses, prologue_uses):
        self.steps, self.q, self.r, self.m = steps, q_uses, r_uses, m_uses
        self.per = q_uses + r_uses + m_uses
        self.pre = prologue_uses
        self.u0 = prologue_uses + q_uses + m_uses

    def first(self, i, b):
        return isinstance(i, int) and i == 0 and b == 0

    def use(self, i, b, k):
        fixed = self.u0 + self.per * b + k - (0 if self.first(i, b) else self.r)
        return i * (2 * self.per) + fixed, fixed % 2

    def job(self, i, b, each=1, plus=0):
        return i * (2 * each) + (each * b + plus)


def attention_stage(nc, per, name, kind, n_heads, dim, scale, w_o, *, heads=None, weights=None,
                    masks=None, x_init=True, windowed=False):
    small = kind == "small"
    rows = 2 * 2 * D8 if small else 2 * dim
    steps = 3 if windowed else QB
    q_uses = {"small": 0, "mqa": 2, "full": 5}[kind]
    m_uses = (QB if windowed else 2 * QB) + 1
    r_uses = 3
    pre_uses = 6 if kind == "mqa" else 0
    J = Jobs(steps, q_uses, r_uses, m_uses, pre_uses)
    OUT = C + 1
    last_i = n_heads - 1
    max_at = 64 if small else dim
    k_rows = max_at + 1 if small else P
    m_rows = max_at if small else P
    v_used = dim + 1
    v_width = 64 if small else dim + 1
    with Stage(nc, name) as st:
        keys = [st.sb(f"keys{b}", [k_rows, SEQ], F32R) for b in range(2)]
        queries = [st.sb(f"queries{b}", [k_rows, SEQ], F32R) for b in range(2)]
        if not small:
            keys_b = [st.sb(f"keys_b{b}", [dim + 1, SEQ], F32R) for b in range(2)]
            queries_b = [st.sb(f"queries_b{b}", [dim + 1, SEQ], F32R) for b in range(2)]
            w_qk = st.sb("w_qk", [P, 4, dim])
            w_v = st.sb("w_v", [P, dim])
        values = [st.sb(f"values{b}", [P, QB, v_width]) for b in range(2)]
        probs = [st.sb(f"probs{b}", [P, SEQ]) for b in range(2)]
        out_cols = [st.sb(f"out_cols{b}", [v_width, SEQ]) for b in range(2)]
        w_out = st.sb("w_out_heads", [v_width, n_heads * OUT])
        part_max = st.sb("part_max", [P, QB, 2])
        neg_max = st.sb("neg_max", [P, QB], F32R)
        max_rows = st.sb("max_rows", [QB, P])
        w_head = [st.sb(f"w_head{b}", [v_width, OUT]) for b in range(2)]
        recip = st.sb("recip", [P, 2, QB])
        work = st.ps("work", [P, 2, HALF])
        scores = st.ps("scores", [P, 2, SEQ])
        outs = st.ps("outs", [P, SEQ])
        if windowed:
            mask_in = st.sb("mask_in", [P, 3, SEQ])
            mask_t = st.sb("mask_t", [P, 3, SEQ], BF16)
            mask_q_in = st.sb("mask_q_in", [P, 2, 272])
            mask_q = st.sb("mask_q", [P, 2, 272], BF16)
            ident_b = st.sb("ident_b", [P, P], BF16)

        work_filled, work_drained = st.sem("work_filled"), st.sem("work_drained")
        scores_ready, exp_done = st.sem("scores_ready"), st.sem("exp_done")
        values_done, out_saved, acc_set = st.sem("values_done"), st.sem("out_saved"), st.sem("acc_set")
        split_done, recip_done = st.sem("split_done"), st.sem("recip_done")
        max_joined, max_loaded = st.sem("max_joined"), st.sem("max_loaded")
        operands_in, values_in, keys_b_ready = st.sem("operands_in"), st.sem("values_in"), st.sem("keys_b_ready")
        consts_in, consts_set, w_out_in = st.sem("consts_in"), st.sem("consts_set"), st.sem("w_out_in")
        masks_ready, w_head_ready = st.sem("masks_ready"), st.sem("w_head_ready")
        block = st.begin()

        def iterations(eng, body):
            body(0)
            if last_i > 1:
                with eng.Fori(1, last_i) as i:
                    body(i)
            body(last_i)

        def is_last(i, b):
            return isinstance(i, int) and i == last_i and b == 1

        def after(i, b):
            return (i, 1) if b == 0 else (i + 1, 0)

        def at_least(eng, sem, value):
            if not isinstance(value, int) or value > 0:
                eng.wait_ge(sem, value)

        N_OPERANDS = 2
        n_consts = 3 + 2 * (4 if small else 2)

        @block.sync
        def _(sp):
            if windowed:
                sp.dma_start(mask_in[:, :, :], masks[0]).then_inc(consts_in, 16)
                sp.dma_start(mask_q_in[:, :, :], masks[1]).then_inc(consts_in, 16)

            def operands(i, b):
                if small:
                    cols = slice(b * SEQ, (b + 1) * SEQ)
                    for dst, x in ((keys[b], "k"), (queries[b], "q")):
                        sp.dma_start(dst[0:rows, :].bitcast(F32),
                                     heads.stacks[x][span(i * rows, rows), cols]).then_inc(operands_in, 16)

            def maxima(i, b, use):
                sp.wait_ge(work_drained, use + 1)
                row = (queries if small else queries_b)[b][max_at:max_at + 1, :]
                sp.dma_start(row.bitcast(F32), max_rows[:, :]).then_inc(max_loaded, 16)

            operands(0, 0)
            maxima(0, 0, J.pre + J.q + J.m - 1)

            def slot(i, b):
                if is_last(i, b):
                    return
                ni, nb = after(i, b)
                if small:
                    at_least(sp, scores_ready, J.job(i, b, steps))
                    operands(ni, nb)
                m0 = J.q + (0 if J.first(i, b) else J.r)
                maxima(ni, nb, J.use(i, b, m0 + J.m - 1)[0])

            iterations(sp, lambda i: (slot(i, 0), slot(i, 1)))

        @block.gpsimd
        def _(pool):
            def head_projections(i):
                for k in range(2):
                    pool.dma_start(w_qk[:, k, :], weights[0](i)).then_inc(operands_in, 16)
                if kind == "full":
                    for k in range(2):
                        pool.dma_start(w_qk[:, 2 + k, :], weights[1](i)).then_inc(operands_in, 16)
                    pool.dma_start(w_v[:, :], weights[2](i)).then_inc(operands_in, 16)

            if kind == "mqa":
                for k in range(2):
                    pool.dma_start(w_qk[:, 2 + k, :], weights[1](0)).then_inc(consts_in, 16)
                pool.dma_start(w_v[:, :], weights[2](0)).then_inc(consts_in, 16)
            if not small:
                head_projections(0)
            wv = w_out[:, :].rearrange("p (h c) -> p h c", c=OUT)
            nc.gpsimd.memset(w_out[:, :], 0.0).then_inc(consts_set, 1)
            pool.wait_ge(consts_set, 1)
            nc.gpsimd.memset(wv[:, :, C:OUT], 1.0).then_inc(consts_set, 1)
            pool.wait_ge(consts_set, 2)
            nc.gpsimd.affine_select(out=wv[:, :, C:OUT], in_=wv[:, :, C:OUT], compare_op=ALU.is_equal, fill=0.0,
                                    base=-dim, pattern=[[0, n_heads], [0, 1]],
                                    channel_multiplier=1).then_inc(consts_set, 1)
            done = 3
            for b in range(2):
                fills = [((keys if small else keys_b)[b][max_at:max_at + 1, :].bitcast(F32), 1.0)]
                if small:
                    fills += [(x[rows:max_at, :].bitcast(F32), 0.0) for x in (keys[b], queries[b])]
                    fills += [(values[b][:, :, :], 0.0)]
                else:
                    fills += [(values[b][:, :, dim:dim + 1], 1.0)]
                for where, value in fills:
                    pool.wait_ge(consts_set, done)
                    nc.gpsimd.memset(where, value).then_inc(consts_set, 1)
                    done += 1
            assert done == n_consts
            pool.wait_ge(consts_set, n_consts)
            if small and windowed:
                for h in range(n_heads):
                    pool.dma_start(wv[0:dim, h, 0:C], w_o[h * dim:(h + 1) * dim, :]).then_inc(w_out_in, 16)
            else:
                pool.dma_start(wv[0:dim, :, 0:C], w_o).then_inc(w_out_in, 16)
            if x_init:
                nc.gpsimd.tensor_copy(per.acc[:, :, :], per.x_rows[:, :, :]).then_inc(acc_set, 1)
            else:
                nc.gpsimd.memset(per.acc[:, :, :], 0.0).then_inc(acc_set, 1)

            def following_projections(i):
                if isinstance(i, int) and i == last_i:
                    return
                pool.wait_ge(work_filled, J.use(i, 0, J.q - 1)[0] + 1)
                head_projections(i + 1)

            if not small:
                iterations(pool, following_projections)

        @block.tensor
        def _(pe):
            def fill(use):
                at_least(pe, work_drained, use - 1)

            def key_value_uses(b, u, k_only_from=0):
                for h in range(2):
                    fill(u + h)
                    nc.tensor.matmul(work[:, (u + h) % 2, :], w_qk[:, 2:4, :].rearrange("p a d -> p (a d)"),
                                     per.x_cols[:, b * SEQ + h * HALF:b * SEQ + (h + 1) * HALF],
                                     start=True, stop=True).then_inc(work_filled, 1)
                value_use(b, u + 2, (u + 2) % 2)

            def value_use(b, u, bank):
                fill(u)
                for t in range(QB):
                    last = nc.tensor.matmul(work[:, bank, t * dim:(t + 1) * dim],
                                            per.x_cols[:, b * SEQ + t * P:b * SEQ + (t + 1) * P], w_v[:, :],
                                            start=True, stop=True)
                last.then_inc(work_filled, 1)

            def project(b, use_of):
                if kind == "small":
                    return
                for k in range(2):
                    u, bank = use_of(k)
                    fill(u)
                    nc.tensor.matmul(work[:, bank, :], w_qk[:, 0:2, :].rearrange("p a d -> p (a d)"),
                                     per.x_cols[:, b * SEQ + k * HALF:b * SEQ + (k + 1) * HALF],
                                     start=True, stop=True).then_inc(work_filled, 1)
                if kind == "full":
                    for k in range(2):
                        u, bank = use_of(2 + k)
                        fill(u)
                        nc.tensor.matmul(work[:, bank, :], w_qk[:, 2:4, :].rearrange("p a d -> p (a d)"),
                                         per.x_cols[:, b * SEQ + k * HALF:b * SEQ + (k + 1) * HALF],
                                         start=True, stop=True).then_inc(work_filled, 1)
                    u, bank = use_of(4)
                    value_use(b, u, bank)

            def max_use(b, k, u, bank):
                fill(u)
                if windowed:
                    lo = 0 if k else P
                    nc.tensor.matmul(work[:, bank, lo:272], ident_b[:, :], mask_q[:, min(k, 1), lo:272],
                                     start=True, stop=False, skip_group_check=True)
                    q = queries[b][0:m_rows, k * P:(k + 1) * P]
                    nc.tensor.matmul(work[:, bank, lo:2 * P], q, keys[b][0:m_rows, max(k - 1, 0) * P:(k + 1) * P],
                                     start=False, stop=False, skip_group_check=True)
                    nc.tensor.matmul(work[:, bank, 2 * P:272], q, keys[b][0:m_rows, 0:PREFIX],
                                     start=False, stop=True, skip_group_check=True).then_inc(work_filled, 1)
                else:
                    q, h = k // 2, k % 2
                    nc.tensor.matmul(work[:, bank, :], queries[b][0:m_rows, q * P:(q + 1) * P],
                                     keys[b][0:m_rows, h * HALF:(h + 1) * HALF],
                                     start=True, stop=True).then_inc(work_filled, 1)

            def max_rows_use(u, bank, job_count):
                fill(u)
                pe.wait_ge(max_joined, job_count)
                nc.tensor.transpose(work[0:QB, bank, 0:P], neg_max[:, :].bitcast(F32),
                                    per.ident[:, :]).then_inc(work_filled, 1)

            def score_step(i, b, k):
                g = steps * b + k
                bank = g % 2
                at_least(pe, exp_done, J.job(i, b, steps, k - 1))
                if windowed:
                    last = window_scores(b, k, bank)
                else:
                    for h in range(2):
                        cols = slice(h * HALF, (h + 1) * HALF)
                        last = nc.tensor.matmul(scores[:, bank, cols], keys[b][:, k * P:(k + 1) * P],
                                                queries[b][:, cols], start=True, stop=small)
                        if not small:
                            last = nc.tensor.matmul(scores[:, bank, cols], keys_b[b][:, k * P:(k + 1) * P],
                                                    queries_b[b][:, cols], start=False, stop=True)
                last.then_inc(scores_ready, 1)

            def window_scores(b, k, bank):
                if k == 0:
                    for h in range(2):
                        cols = slice(h * HALF, (h + 1) * HALF)
                        nc.tensor.matmul(scores[0:PREFIX, bank, cols], ident_b[:, 0:PREFIX], mask_t[:, 0, cols],
                                         start=True, stop=False, skip_group_check=True)
                        last = nc.tensor.matmul(scores[0:PREFIX, bank, cols], keys[b][:, 0:PREFIX],
                                                queries[b][:, cols], start=False, stop=True, skip_group_check=True)
                    return last
                for h in range(2):
                    first = k - 1 if h == 0 else 0
                    cols = slice(h * HALF + first * P, (h + 1) * HALF)
                    nc.tensor.matmul(scores[:, bank, cols], ident_b[:, :], mask_t[:, k, cols],
                                     start=True, stop=False, skip_group_check=True)
                    for q in range(4 * h + first, 4 * h + 4):
                        kb = q - (k - 1)
                        last = nc.tensor.matmul(scores[:, bank, q * P:(q + 1) * P], keys[b][:, kb * P:(kb + 1) * P],
                                                queries[b][:, q * P:(q + 1) * P], start=False,
                                                stop=q == 4 * h + 3, skip_group_check=True)
                return last

            def value_step(i, b, k):
                pbuf = (steps * b + k) % 2
                pe.wait_ge(exp_done, J.job(i, b, steps, k + 1))
                if k == 0:
                    at_least(pe, out_saved, J.job(i, b))
                v = values[b]
                if windowed:
                    for h in range(2):
                        cols = slice(h * HALF, (h + 1) * HALF)
                        if k == 0:
                            last = nc.tensor.matmul(outs[0:v_width, cols], v[0:PREFIX, 0, :], probs[pbuf][0:PREFIX, cols],
                                                    start=True, stop=False, skip_group_check=True)
                            continue
                        for q in range(4 * h + (k - 1 if h == 0 else 0), 4 * h + 4):
                            last = nc.tensor.matmul(outs[0:v_width, q * P:(q + 1) * P], v[:, q - (k - 1), :],
                                                    probs[pbuf][:, q * P:(q + 1) * P], start=False,
                                                    stop=k == 2 and q == 4 * h + 3, skip_group_check=True)
                else:
                    for h in range(2):
                        cols = slice(h * HALF, (h + 1) * HALF)
                        last = nc.tensor.matmul(outs[0:v_width, cols], v[:, k, :], probs[pbuf][:, cols],
                                                start=k == 0, stop=k == steps - 1)
                last.then_inc(values_done, 1)

            def output_product(i, b, use_of):
                pe.wait_ge(out_saved, J.job(i, b, 1, 1))
                pe.wait_ge(w_head_ready, J.job(i, b, 1, 1))
                for k in range(3):
                    u, bank = use_of(k)
                    fill(u)
                    for j in range(3 * k, min(3 * k + 3, QB)):
                        last = nc.tensor.matmul(work[:, bank, (j - 3 * k) * OUT:(j - 3 * k + 1) * OUT],
                                                out_cols[b][:, j * P:(j + 1) * P], w_head[b][:, :], start=True, stop=True)
                    last.then_inc(work_filled, 1)

            pe.wait_ge(consts_set, n_consts)
            if small:
                pe.wait_ge(operands_in, 16 * N_OPERANDS)
            elif kind == "mqa":
                pe.wait_ge(consts_in, 16 * 3)
                for b in range(2):
                    key_value_uses(b, 3 * b)
                pe.wait_ge(operands_in, 16 * 2)
            else:
                pe.wait_ge(operands_in, 16 * 5)
            if windowed:
                pe.wait_ge(masks_ready, 3)
            project(0, lambda k: (J.pre + k, (J.pre + k) % 2))
            m_start = J.pre + J.q
            at_least(pe, work_drained, m_start)
            for k in range(J.m - 1):
                max_use(0, k, m_start + k, (m_start + k) % 2)
            max_rows_use(m_start + J.m - 1, (m_start + J.m - 1) % 2, 1)

            def slot(i, b):
                last_slot = is_last(i, b)
                first_slot = J.first(i, b)
                nq = 0 if last_slot else J.q
                ni, nb = after(i, b)
                pi, pb = (i, 0) if b else (i - 1, 1)
                m0 = J.q + (0 if first_slot else J.r)
                pe.wait_ge(max_loaded, J.job(i, b, 16, 16))
                if small:
                    pe.wait_ge(values_in, J.job(i, b, 1, 1))
                elif kind == "full":
                    pe.wait_ge(keys_b_ready, J.job(i, b, 1, 1))
                elif first_slot:
                    pe.wait_ge(keys_b_ready, 2)
                todo = list(range(J.m - 1))
                middle = max(steps - 3, 1)
                share = -(-len(todo) // middle)
                for k in range(steps):
                    score_step(i, b, k)
                    if k:
                        value_step(i, b, k - 1)
                    if k == 0 and not last_slot:
                        if small:
                            pe.wait_ge(operands_in, J.job(i, b, 16 * N_OPERANDS, 2 * 16 * N_OPERANDS))
                        elif nb == 0:
                            n_w = 2 if kind == "mqa" else 5
                            pe.wait_ge(operands_in, i * (16 * n_w) + 2 * 16 * n_w)
                        project(nb, lambda k: J.use(i, b, k))
                    if k == (0 if windowed else 1) and not first_slot:
                        output_product(pi, pb, lambda k: J.use(i, b, nq + k))
                    if not last_slot and ((windowed and k == 1) or (not windowed and 2 <= k < steps - 1)):
                        if todo and todo[0] == 0:
                            pe.wait_ge(work_drained, J.use(i, b, m0)[0])
                        for j in todo[:share]:
                            max_use(nb, j, *J.use(i, b, m0 + j))
                        todo = todo[share:]
                    if not last_slot and k == steps - 1:
                        max_rows_use(*J.use(i, b, m0 + J.m - 1), J.job(i, b, 1, 2))
                value_step(i, b, steps - 1)

            iterations(pe, lambda i: (slot(i, 0), slot(i, 1)))
            output_product(last_i, 1, lambda k: J.use(last_i, 1, J.r + k))

        @block.scalar
        def _(act):
            def save(i, b):
                act.wait_ge(values_done, J.job(i, b, steps, steps))
                nc.scalar.activation(out_cols[b][:, :], outs[0:v_width, :], ACT.Copy).then_inc(out_saved, 1)

            def high_keys(b, use):
                act.wait_ge(work_drained, use + 1)
                nc.scalar.activation(keys_b[b][0:dim, :], keys[b][0:dim, :].bitcast(F32),
                                     ACT.Copy).then_inc(keys_b_ready, 1)

            if kind == "mqa":
                for b in range(2):
                    high_keys(b, 3 * b + 1)
            if kind == "full":
                high_keys(0, J.pre + 3)

            def slot(i, b):
                for k in range(steps):
                    buf = (steps * b + k) % 2
                    act.wait_ge(scores_ready, J.job(i, b, steps, k + 1))
                    at_least(act, values_done, J.job(i, b, steps, k - 1))
                    if windowed and k == 0:
                        where = (slice(0, PREFIX), slice(0, SEQ))
                    elif windowed and k == 2:
                        where = (slice(0, P), slice(P, SEQ))
                    else:
                        where = (slice(0, P), slice(0, SEQ))
                    nc.scalar.activation(probs[buf][where[0], where[1]], scores[where[0], buf, where[1]],
                                         ACT.Exp, scale=scale).then_inc(exp_done, 1)
                    if k == 0 and not J.first(i, b):
                        save(*((i, 0) if b else (i - 1, 1)))
                    if k == 3 and kind == "full" and not is_last(i, b):
                        high_keys(1 - b, J.use(i, b, 3)[0])

            iterations(act, lambda i: (slot(i, 0), slot(i, 1)))
            save(last_i, 1)

        @block.vector
        def _(dve):
            if windowed:
                dve.wait_ge(consts_in, 32)
                nc.vector.tensor_copy(mask_t[:, :, :], mask_in[:, :, :]).then_inc(masks_ready, 1)
                nc.vector.tensor_copy(mask_q[:, :, :], mask_q_in[:, :, :]).then_inc(masks_ready, 1)
                nc.vector.tensor_copy(ident_b[:, :], per.ident[:, :]).then_inc(masks_ready, 1)

            splits = {"small": 0, "mqa": 2, "full": 4}[kind]
            pre_splits = 4 if kind == "mqa" else 0

            def split_query(b, h, u, bank, s):
                cols = slice(h * HALF, (h + 1) * HALF)
                dve.wait_ge(work_filled, u + 1)
                nc.vector.tensor_copy(queries[b][:, cols], work[:, bank, :]).then_inc(split_done, 1)
                dve.wait_ge(split_done, s + 1)
                nc.vector.tensor_tensor(queries_b[b][0:dim, cols], work[0:dim, bank, :],
                                        queries[b][0:dim, cols].bitcast(F32), ALU.subtract).then_inc(work_drained, 1)

            def split_key(b, h, u, bank, s):
                cols = slice(h * HALF, (h + 1) * HALF)
                dve.wait_ge(work_filled, u + 1)
                nc.vector.tensor_copy(keys[b][:, cols], work[:, bank, :]).then_inc(split_done, 1)
                dve.wait_ge(split_done, s + 1)
                nc.vector.tensor_tensor(keys[b][dim:2 * dim, cols], work[dim:2 * dim, bank, :],
                                        keys[b][dim:2 * dim, cols].bitcast(F32), ALU.subtract).then_inc(work_drained, 1)

            def copy_values(b, u, bank):
                dve.wait_ge(work_filled, u + 1)
                nc.vector.tensor_copy(values[b][:, :, 0:dim],
                                      work[:, bank, :].rearrange("p (t d) -> p t d", d=dim)).then_inc(work_drained, 1)

            def project(b, use_of, s0):
                if small:
                    return
                for k in range(2):
                    split_query(b, k, *use_of(k), s0 + k)
                if kind == "full":
                    for k in range(2):
                        split_key(b, k, *use_of(2 + k), s0 + 2 + k)
                    copy_values(b, *use_of(4))

            def max_use(k, u, bank):
                dve.wait_ge(work_filled, u + 1)
                if windowed:
                    nc.vector.tensor_reduce(part_max[:, k, 0:1], work[:, bank, (0 if k else P):272], AX.X,
                                            ALU.max).then_inc(work_drained, 1)
                else:
                    nc.vector.tensor_reduce(part_max[:, k // 2, k % 2:k % 2 + 1], work[:, bank, :], AX.X,
                                            ALU.max).then_inc(work_drained, 1)

            def join_max(u, bank, dma_value):
                dve.wait_ge(work_drained, u)
                if windowed:
                    nc.vector.tensor_scalar(neg_max[:, :], part_max[:, :, 0], -1.0, None,
                                            ALU.mult).then_inc(max_joined, 1)
                else:
                    nc.vector.tensor_reduce(neg_max[:, :], part_max[:, :, :], AX.X, ALU.max,
                                            negate=True).then_inc(max_joined, 1)
                dve.wait_ge(work_filled, u + 1)
                at_least(dve, max_loaded, dma_value)
                nc.vector.tensor_copy(max_rows[:, :], work[0:QB, bank, 0:P]).then_inc(work_drained, 1)

            def output_product(b, use_of, r0):
                for k in range(3):
                    u, bank = use_of(k)
                    n = min(3, QB - 3 * k)
                    dve.wait_ge(work_filled, u + 1)
                    at = work[:, bank, 0:n * OUT].rearrange("p (j c) -> p j c", c=OUT)
                    nc.vector.reciprocal(recip[:, b, 3 * k:3 * k + n], at[:, :, C]).then_inc(recip_done, 1)
                    dve.wait_ge(recip_done, r0 + k + 1)
                    for j in range(n):
                        t = b * QB + 3 * k + j
                        last = nc.vector.scalar_tensor_tensor(per.acc[:, t, :], at[:, j, 0:C],
                                                              recip[:, b, 3 * k + j:3 * k + j + 1], per.acc[:, t, :],
                                                              ALU.mult, ALU.add)
                    last.then_inc(work_drained, 1)

            def head_weights(i, b):
                nc.vector.tensor_scalar(w_head[b][:, :], w_out[:, span(i * OUT, OUT)], 1.0, None,
                                        ALU.mult).then_inc(w_head_ready, 1)

            def head_values(i, b):
                nc.vector.tensor_scalar(values[b][:, :, 0:v_used],
                                        heads.v_rows[:, b * QB:(b + 1) * QB, span(i * v_used, v_used)], 1.0, None,
                                        ALU.mult).then_inc(values_in, 1)

            dve.wait_ge(consts_set, n_consts)
            dve.wait_ge(w_out_in, 16 * n_heads if windowed else 16)
            if small:
                head_values(0, 0)
            if kind == "mqa":
                for b in range(2):
                    for h in range(2):
                        split_key(b, h, 3 * b + h, (3 * b + h) % 2, 2 * b + h)
                    copy_values(b, 3 * b + 2, (3 * b + 2) % 2)
            project(0, lambda k: (J.pre + k, (J.pre + k) % 2), pre_splits)
            m_start = J.pre + J.q
            for k in range(J.m - 1):
                max_use(k, m_start + k, (m_start + k) % 2)
            join_max(m_start + J.m - 1, (m_start + J.m - 1) % 2, 0)

            def slot(i, b):
                last_slot, first_slot = is_last(i, b), J.first(i, b)
                nq = 0 if last_slot else J.q
                ni, nb = after(i, b)
                m0 = J.q + (0 if first_slot else J.r)
                at_least(dve, values_done, J.job(i, b, steps))
                head_weights(i, b)
                if not last_slot:
                    if small:
                        head_values(ni, nb)
                    project(nb, lambda k: J.use(i, b, k), J.job(i, b, splits, splits + pre_splits))
                if not first_slot:
                    output_product(1 - b, lambda k: J.use(i, b, nq + k), J.job(i, b, 3, -3))
                if not last_slot:
                    for k in range(J.m - 1):
                        max_use(k, *J.use(i, b, m0 + k))
                    join_max(*J.use(i, b, m0 + J.m - 1), J.job(i, b, 16, 16))

            dve.wait_ge(acc_set, 1)
            iterations(dve, lambda i: (slot(i, 0), slot(i, 1)))
            output_product(1, lambda k: J.use(last_i, 1, J.r + k), 3 * (2 * n_heads - 1))



def layer0_ffn(nc, per, t):
    with Stage(nc, "L0_ffn") as st:
        w = st.sb("w", [C, C])
        a1 = st.sb("a1", [C, C])
        a2 = st.sb("a2", [C, C])
        b_row = st.sb("b_row", [1, C])
        w_t = st.sb("w_t", [C, C])
        a1_t = st.sb("a1_t", [C, C])
        a12 = st.sb("a12", [C, C])
        wa = st.sb("wa", [C, C])
        act_out = st.sb("act_out", [P, TILES, C])
        small_ps = st.ps("small_ps", [P, 4, HALF])
        out_ps = st.ps("out_ps", [P, CHUNKS, HALF])
        loaded = st.sem("loaded")
        product, copied = st.sem("product"), st.sem("copied")
        rows_done, tanh_done, added = st.sem("rows_done"), st.sem("tanh_done"), st.sem("added")
        block = st.begin()

        @block.sync
        def _(sp):
            for dst, name in ((w, "weight"), (a1, "aux_weight1"), (a2, "aux_weight2")):
                sp.dma_start(dst[:, :], t["L0_ffn_" + name]).then_inc(loaded, 16)
            sp.dma_start(b_row[:, :], t["L0_ffn_bias"].rearrange("(a c) -> a c", a=1)).then_inc(loaded, 16)

        @block.tensor
        def _(pe):
            pe.wait_ge(loaded, 64)
            nc.tensor.transpose(small_ps[:, 0, 0:C], w[:, :], per.ident[:, :]).then_inc(product, 1)
            nc.tensor.transpose(small_ps[:, 1, 0:C], a1[:, :], per.ident[:, :]).then_inc(product, 1)
            pe.wait_ge(copied, 2)
            nc.tensor.matmul(small_ps[:, 2, 0:C], a1_t[:, :], a2[:, :], start=True, stop=True).then_inc(product, 1)
            pe.wait_ge(copied, 3)
            nc.tensor.matmul(small_ps[:, 3, 0:C], w_t[:, :], a12[:, :], start=True, stop=True).then_inc(product, 1)
            pe.wait_ge(copied, 4)
            for k in range(TILES):
                cols = slice((k % 4) * C, (k % 4 + 1) * C)
                nc.tensor.matmul(out_ps[:, k // 4, cols], per.ones_row[:, :], b_row[:, :], start=True, stop=False)
                nc.tensor.matmul(out_ps[:, k // 4, cols], per.x_cols[:, k * P:(k + 1) * P], wa[:, :],
                                 start=False, stop=True).then_inc(rows_done, 1)

        @block.scalar
        def _(act):
            for k, dst in enumerate((w_t, a1_t, a12, wa)):
                act.wait_ge(product, k + 1)
                nc.scalar.activation(dst[:, :], small_ps[:, k, 0:C], ACT.Copy).then_inc(copied, 1)
            for c in range(CHUNKS):
                act.wait_ge(rows_done, 4 * c + 4)
                nc.scalar.activation(act_out[:, 4 * c:4 * c + 4, :],
                                     out_ps[:, c, :].rearrange("p (t c) -> p t c", c=C), ACT.Tanh).then_inc(tanh_done, 1)

        @block.vector
        def _(dve):
            for c in range(CHUNKS):
                dve.wait_ge(tanh_done, c + 1)
                part = slice(4 * c, 4 * c + 4)
                nc.vector.tensor_tensor(per.acc[:, part, :], per.x_rows[:, part, :], act_out[:, part, :],
                                        ALU.add).then_inc(added, 1)
    norm_stage(nc, per, "L0_norm1", per.acc, per.x_rows)


def one_hot_of_max(nc, dve, st, name, scores, n, one_hot, scratch, eq, top, rev, step, at):
    def wide(a):
        return a[:, :].unsqueeze(2).to_broadcast([P, TILES, n])
    nc.vector.tensor_reduce(top[:, :], scores[:, :, :], AX.X, ALU.max).then_inc(step, 1)
    dve.wait_ge(step, at + 1)
    nc.vector.tensor_tensor(eq[:, :, :], scores[:, :, :], wide(top), ALU.is_equal).then_inc(step, 1)
    dve.wait_ge(step, at + 2)
    nc.vector.tensor_tensor(eq[:, :, :], eq[:, :, :], rev[:, 0:n].unsqueeze(1).to_broadcast([P, TILES, n]),
                            ALU.mult).then_inc(step, 1)
    dve.wait_ge(step, at + 3)
    nc.vector.tensor_reduce(scratch[:, :], eq[:, :, :], AX.X, ALU.max).then_inc(step, 1)
    dve.wait_ge(step, at + 4)
    nc.vector.tensor_tensor(one_hot[:, :, :], eq[:, :, :], wide(scratch), ALU.is_equal).then_inc(step, 1)
    dve.wait_ge(step, at + 5)
    return at + 5


def layer1_ffn(nc, per, t):
    n_e = 32
    with ExitStack() as ctx:
        held = Held(nc, ctx, "L1_routed")
        pick = held.sb("pick", [P, TILES, n_e])
        scaled_cols = held.sb("scaled_cols", [C, TOKENS])
        with Stage(nc, "L1_router") as st:
            w = st.sb("w", [C, n_e])
            rev = st.sb("rev", [P, n_e])
            logits = st.sb("logits", [P, TILES, n_e])
            eq = st.sb("eq", [P, TILES, n_e])
            top = st.sb("top", [P, TILES])
            scratch = st.sb("scratch", [P, TILES])
            score = st.sb("score", [P, TILES])
            scaled = st.sb("scaled", [P, TILES, C])
            logit_ps = st.ps("logit_ps", [P, HALF])
            tr = st.ps("tr", [P, CHUNKS, HALF])
            loaded, logits_done, logits_ready = st.sem("loaded"), st.sem("logits_done"), st.sem("logits_ready")
            step, score_ready = st.sem("step"), st.sem("score_ready")
            scaled_ready, transposed, copied = st.sem("scaled_ready"), st.sem("transposed"), st.sem("copied")
            acc_set = st.sem("acc_set")
            block = st.begin()

            @block.sync
            def _(sp):
                sp.dma_start(w[:, :], t["L1_ffn_gate_w"]).then_inc(loaded, 16)
                sp.dma_start(rev[:, :], t["reversed"]).then_inc(loaded, 16)

            @block.tensor
            def _(pe):
                pe.wait_ge(loaded, 32)
                for k in range(TILES):
                    nc.tensor.matmul(logit_ps[:, k * n_e:(k + 1) * n_e], per.x_cols[:, k * P:(k + 1) * P], w[:, :],
                                     start=True, stop=True).then_inc(logits_done, 1)
                for k in range(TILES):
                    pe.wait_ge(scaled_ready, k + 1)
                    nc.tensor.transpose(tr[:, k // 4, (k % 4) * P:(k % 4 + 1) * P], scaled[:, k, :],
                                        per.ident[:, :]).then_inc(transposed, 1)

            @block.vector
            def _(dve):
                dve.wait_ge(loaded, 32)
                dve.wait_ge(logits_done, TILES)
                nc.vector.tensor_copy(logits[:, :, :], logit_ps[:, :].rearrange("p (t e) -> p t e", e=n_e)).then_inc(step, 1)
                dve.wait_ge(step, 1)
                one_hot_of_max(nc, dve, st, "top", logits, n_e, pick, scratch, eq, top, rev, step, 1)
                dve.wait_ge(score_ready, 1)
                for k in range(TILES):
                    nc.vector.tensor_scalar(scaled[:, k, :], per.x_rows[:, k, :], score[:, k:k + 1], None,
                                            ALU.mult).then_inc(scaled_ready, 1)

            @block.gpsimd
            def _(pool):
                nc.gpsimd.tensor_copy(per.acc[:, :, :], per.x_rows[:, :, :]).then_inc(acc_set, 1)

            @block.scalar
            def _(act):
                act.wait_ge(step, 2)
                nc.scalar.activation(score[:, :], top[:, :], ACT.Sigmoid).then_inc(score_ready, 1)
                for c in range(CHUNKS):
                    act.wait_ge(transposed, 4 * c + 4)
                    nc.scalar.activation(scaled_cols[:, c * HALF:(c + 1) * HALF], tr[:, c, :],
                                         ACT.Copy).then_inc(copied, 1)
        shared = [t["L1_ffn_shared_" + n] for n in ("gate_w", "up_w", "down_w")]
        experts_stage(nc, per, "L1_shared", 1, per.x_cols, None,
                      lambda e: (shared[0], shared[1]), lambda e: shared[2], flip=False)
        routed = [t["L1_ffn_routed_" + n].rearrange("e a b -> (e a) b") for n in ("gate_w", "up_w", "down_w")]
        experts_stage(nc, per, "L1_experts", n_e, scaled_cols, pick,
                      lambda e: (routed[0][span(e * C, C), :], routed[1][span(e * C, C), :]),
                      lambda e: routed[2][span(e * 2 * C, 2 * C), :], flip=False)
    norm_stage(nc, per, "L1_norm1", per.acc, per.x_rows)


def layer2_ffn(nc, per, t):
    n_e = 8
    with ExitStack() as ctx:
        held = Held(nc, ctx, "L2_routed")
        share = held.sb("share", [P, TILES, n_e])
        with Stage(nc, "L2_router") as st:
            w = st.sb("w", [n_e, C])
            w_t = st.sb("w_t", [C, n_e])
            rev = st.sb("rev", [P, 32])
            logits = st.sb("logits", [P, TILES, n_e])
            rest = st.sb("rest", [P, TILES, n_e])
            eq = st.sb("eq", [P, TILES, n_e])
            pick1 = st.sb("pick1", [P, TILES, n_e])
            pick2 = st.sb("pick2", [P, TILES, n_e])
            top1 = st.sb("top1", [P, TILES])
            top2 = st.sb("top2", [P, TILES])
            scratch = st.sb("scratch", [P, TILES])
            gap = st.sb("gap", [P, TILES])
            e2 = st.sb("e2", [P, TILES])
            p1 = st.sb("p1", [P, TILES])
            p2 = st.sb("p2", [P, TILES])
            ps = st.ps("ps", [P, 2, HALF])
            loaded, flipped, w_ready = st.sem("loaded"), st.sem("flipped"), st.sem("w_ready")
            logits_done, step, exp_ready = st.sem("logits_done"), st.sem("step"), st.sem("exp_ready")
            gap_ready, acc_set = st.sem("gap_ready"), st.sem("acc_set")
            block = st.begin()

            @block.sync
            def _(sp):
                sp.dma_start(w[:, :], t["L2_ffn_gate_w"]).then_inc(loaded, 16)
                sp.dma_start(rev[:, :], t["reversed"]).then_inc(loaded, 16)

            @block.gpsimd
            def _(pool):
                nc.gpsimd.tensor_copy(per.acc[:, :, :], per.x_rows[:, :, :]).then_inc(acc_set, 1)

            @block.tensor
            def _(pe):
                pe.wait_ge(loaded, 32)
                nc.tensor.transpose(ps[:, 0, 0:n_e], w[:, :], per.ident[0:n_e, 0:n_e]).then_inc(flipped, 1)
                pe.wait_ge(w_ready, 1)
                for k in range(TILES):
                    nc.tensor.matmul(ps[:, 1, k * n_e:(k + 1) * n_e], per.x_cols[:, k * P:(k + 1) * P], w_t[:, :],
                                     start=True, stop=True).then_inc(logits_done, 1)

            @block.scalar
            def _(act):
                act.wait_ge(flipped, 1)
                nc.scalar.activation(w_t[:, :], ps[:, 0, 0:n_e], ACT.Copy).then_inc(w_ready, 1)
                act.wait_ge(gap_ready, 1)
                nc.scalar.activation(e2[:, :], gap[:, :], ACT.Exp).then_inc(exp_ready, 1)

            @block.vector
            def _(dve):
                def wide(a):
                    return a[:, :].unsqueeze(2).to_broadcast([P, TILES, n_e])
                dve.wait_ge(loaded, 32)
                dve.wait_ge(logits_done, TILES)
                nc.vector.tensor_copy(logits[:, :, :],
                                      ps[:, 1, 0:TILES * n_e].rearrange("p (t e) -> p t e", e=n_e)).then_inc(step, 1)
                dve.wait_ge(step, 1)
                n = one_hot_of_max(nc, dve, st, "top1", logits, n_e, pick1, scratch, eq, top1, rev, step, 1)
                nc.vector.scalar_tensor_tensor(rest[:, :, :], pick1[:, :, :], -3.0e38, logits[:, :, :],
                                               ALU.mult, ALU.add).then_inc(step, 1)
                dve.wait_ge(step, n + 1)
                n = one_hot_of_max(nc, dve, st, "top2", rest, n_e, pick2, scratch, eq, top2, rev, step, n + 1)
                nc.vector.tensor_tensor(gap[:, :], top2[:, :], top1[:, :], ALU.subtract).then_inc(gap_ready, 1)
                dve.wait_ge(exp_ready, 1)
                nc.vector.tensor_scalar(p1[:, :], e2[:, :], 1.0, None, ALU.add).then_inc(step, 1)
                dve.wait_ge(step, n + 1)
                nc.vector.reciprocal(p1[:, :], p1[:, :]).then_inc(step, 1)
                dve.wait_ge(step, n + 2)
                nc.vector.tensor_tensor(p2[:, :], e2[:, :], p1[:, :], ALU.mult).then_inc(step, 1)
                dve.wait_ge(step, n + 3)
                nc.vector.tensor_tensor(pick1[:, :, :], pick1[:, :, :], wide(p1), ALU.mult).then_inc(step, 1)
                nc.vector.tensor_tensor(pick2[:, :, :], pick2[:, :, :], wide(p2), ALU.mult).then_inc(step, 1)
                dve.wait_ge(step, n + 5)
                nc.vector.tensor_tensor(share[:, :, :], pick1[:, :, :], pick2[:, :, :], ALU.add).then_inc(step, 1)
        w12 = t["L2_ffn_w12"].rearrange("e h d -> (e h) d")
        w3 = t["L2_ffn_w3"].rearrange("e d h -> (e d) h")
        experts_stage(nc, per, "L2_experts", n_e, per.x_cols, share,
                      lambda e: (w12[span(e * 4 * C, 4 * C), :],), lambda e: w3[span(e * C, C), :], flip=True)
    norm_stage(nc, per, "L2_norm1", per.acc, per.x_rows)


def experts_stage(nc, per, name, n_e, cols_in, share, w_up, w_down, flip):
    IN = 2 * C
    with Stage(nc, name) as st:
        up = [st.sb(f"up{k}", [C, 2 * IN]) for k in range(2)]
        down = [st.sb(f"down{k}", [P, 2, C]) for k in range(2)]
        if flip:
            up_raw = st.sb("up_raw", [P, 4, C])
            down_raw = st.sb("down_raw", [C, IN])
        gated = st.sb("gated", [P, 2, HALF])
        hidden = [st.sb(f"hidden{k}", [P, 2, HALF]) for k in range(2)]
        mine = [st.sb(f"mine{k}", [P, TILES]) for k in range(2)]
        pair_ps = st.ps("pair_ps", [P, 2, 2, HALF])
        rows_ps = st.ps("rows_ps", [P, 2, HALF])
        flip_ps = st.ps("flip_ps", [P, 2, HALF])
        w_in = [st.sem(f"w_in{k}") for k in range(2)]
        w_ready, flipped = st.sem("w_ready"), st.sem("flipped")
        pair_done, silu_done, hidden_ready = st.sem("pair_done"), st.sem("silu_done"), st.sem("hidden_ready")
        rows_done, rows_added, mine_ready = st.sem("rows_done"), st.sem("rows_added"), st.sem("mine_ready")
        n_w = 2 if flip else 3
        block = st.begin()

        def experts(eng, body):
            body(0)
            if n_e > 4:
                with eng.Fori(1, n_e // 2 - 1) as i:
                    body(i)
            if n_e > 2:
                body(n_e // 2 - 1)

        pair = range(min(n_e, 2))

        def at(i, k, each, plus=0):
            return i * (2 * each) + (each * k + plus)

        def at_least(eng, sem, value):
            if not isinstance(value, int) or value > 0:
                eng.wait_ge(sem, value)

        @block.gpsimd
        def _(pool):
            def load(i, k):
                if flip:
                    at_least(pool, flipped, at(i, k, 1))
                else:
                    at_least(pool, rows_done, at(i, k, 4, -4))
                e = i * 2 + k
                if flip:
                    pool.dma_start(up_raw[:, :, :], w_up(e)[0].rearrange("(a p) d -> p a d", p=P)).then_inc(w_in[k], 16)
                    pool.dma_start(down_raw[:, :], w_down(e)).then_inc(w_in[k], 16)
                else:
                    for g in range(2):
                        pool.dma_start(up[k][:, g * IN:(g + 1) * IN], w_up(e)[g]).then_inc(w_in[k], 16)
                    pool.dma_start(down[k][:, :, :], w_down(e).rearrange("(a p) c -> p a c", p=P)).then_inc(w_in[k], 16)

            experts(pool, lambda i: [load(i, k) for k in pair])

        @block.tensor
        def _(pe):
            def rows_of(i, k, c):
                s = 4 * k + c
                pe.wait_ge(hidden_ready, at(i, k, 8, 2 * c + 2))
                at_least(pe, rows_added, at(i, k, 4, c - 1))
                for j in range(4):
                    for h in range(2):
                        last = nc.tensor.matmul(rows_ps[:, s % 2, j * C:(j + 1) * C],
                                                hidden[s % 2][:, h, j * P:(j + 1) * P], down[k][:, h, :],
                                                start=h == 0, stop=h == 1)
                last.then_inc(rows_done, 1)

            def step(i, k):
                if flip:
                    pe.wait_ge(w_in[k], i * (16 * n_w) + 16 * n_w)
                    at_least(pe, w_ready, at(i, k, 2))
                    for a in range(4):
                        nc.tensor.transpose(flip_ps[:, 0, a * P:(a + 1) * P], up_raw[:, a, :], per.ident[:, :])
                    for a in range(2):
                        last = nc.tensor.transpose(flip_ps[:, 1, a * P:(a + 1) * P], down_raw[:, a * P:(a + 1) * P],
                                                   per.ident[:, :])
                    last.then_inc(flipped, 1)
                    pe.wait_ge(w_ready, at(i, k, 2, 2))
                else:
                    pe.wait_ge(w_in[k], i * (16 * n_w) + 16 * n_w)
                for c in range(CHUNKS):
                    for h in range(2):
                        n = 8 * k + 2 * c + h
                        at_least(pe, hidden_ready, at(i, k, 8, 2 * c + h - 1))
                        for g in range(2):
                            last = nc.tensor.matmul(pair_ps[:, n % 2, g, :], up[k][:, g * IN + h * P:g * IN + (h + 1) * P],
                                                    cols_in[:, c * HALF:(c + 1) * HALF], start=True, stop=True)
                        last.then_inc(pair_done, 1)
                    if c:
                        rows_of(i, k, c - 1)
                    elif k:
                        rows_of(i, 0, CHUNKS - 1)
                    elif not (isinstance(i, int) and i == 0):
                        rows_of(i - 1, 1, CHUNKS - 1)

            experts(pe, lambda i: [step(i, k) for k in pair])
            rows_of((n_e - 1) // 2, (n_e - 1) % 2, CHUNKS - 1)

        @block.scalar
        def _(act):
            def copies(i, k):
                act.wait_ge(flipped, at(i, k, 1, 1))
                at_least(act, rows_done, at(i, k, 4, -4))
                nc.scalar.activation(up[k][:, :], flip_ps[:, 0, :], ACT.Copy).then_inc(w_ready, 1)
                nc.scalar.activation(down[k][:, :, :], flip_ps[:, 1, 0:IN].rearrange("p (a c) -> p a c", c=C),
                                     ACT.Copy).then_inc(w_ready, 1)

            def step(i, k):
                if flip:
                    copies(i, k)
                for n in range(8):
                    act.wait_ge(pair_done, at(i, k, 8, n + 1))
                    at_least(act, hidden_ready, at(i, k, 8, n - 1))
                    nc.scalar.activation(gated[:, n % 2, :], pair_ps[:, n % 2, 0, :], ACT.Silu).then_inc(silu_done, 1)

            experts(act, lambda i: [step(i, k) for k in pair])

        @block.vector
        def _(dve):
            def my_share(i, k):
                if share is not None:
                    src = share[:, :, span(i * 2 + k, 1)].rearrange("p t a -> p (t a)")
                    nc.vector.tensor_scalar(mine[k][:, :], src, 1.0, None, ALU.mult).then_inc(mine_ready, 1)

            def add_rows(i, k, c):
                s = 4 * k + c
                dve.wait_ge(rows_done, at(i, k, 4, c + 1))
                if share is not None:
                    dve.wait_ge(mine_ready, at(i, k, 1, 1))
                at_least(dve, rows_added, at(i, k, 4, c))
                for j in range(4):
                    tile = 4 * c + j
                    psum = rows_ps[:, s % 2, j * C:(j + 1) * C]
                    if share is not None:
                        last = nc.vector.scalar_tensor_tensor(per.acc[:, tile, :], psum, mine[k][:, tile:tile + 1],
                                                              per.acc[:, tile, :], ALU.mult, ALU.add)
                    else:
                        last = nc.vector.tensor_tensor(per.acc[:, tile, :], psum, per.acc[:, tile, :], ALU.add)
                last.then_inc(rows_added, 1)

            def step(i, k):
                for c in range(CHUNKS):
                    for h in range(2):
                        n = 2 * c + h
                        dve.wait_ge(silu_done, at(i, k, 8, n + 1))
                        at_least(dve, rows_done, at(i, k, 4, c - 1))
                        nc.vector.tensor_tensor(hidden[c % 2][:, h, :], pair_ps[:, n % 2, 1, :], gated[:, n % 2, :],
                                                ALU.mult).then_inc(hidden_ready, 1)
                    if c:
                        add_rows(i, k, c - 1)
                    elif k:
                        add_rows(i, 0, CHUNKS - 1)
                    elif not (isinstance(i, int) and i == 0):
                        add_rows(i - 1, 1, CHUNKS - 1)
                    if c == 0:
                        my_share(i, k)

            experts(dve, lambda i: [step(i, k) for k in pair])
            add_rows((n_e - 1) // 2, (n_e - 1) % 2, CHUNKS - 1)


def layer3_ffn(nc, per, t):
    HID = 4 * C
    HB = HID // P
    with ExitStack() as ctx:
        held = Held(nc, ctx, "L3_held")
        w_t = {n: held.sb(n, [P, k, m]) for n, k, m in
               (("w1", 1, HID), ("w2", 1, HID), ("h1", HB, HID), ("h2", HB, HID), ("w3", HB, C))}
        s_cols = held.sb("s_cols", [P, 4, HB])
        s3_bc = held.sb("s3_bc", [P, C])
        with Stage(nc, "L3_weights") as st:
            raw = {n: st.sb(n + "_raw", [P, k, m]) for n, k, m in
                   (("w1", HB, C), ("w2", HB, C), ("h1", HB, HID), ("h2", HB, HID), ("w3", 1, HID))}
            tr = st.ps("tr", [P, 4, HALF])
            loaded = {n: st.sem("loaded_" + n) for n in raw}
            scales_in, flipped, copied = st.sem("scales_in"), st.sem("flipped"), st.sem("copied")
            groups = []
            for n in ("w1", "w2"):
                groups.append((n, [(o, 0) for o in range(HB)], w_t[n][:, 0, :]))
            for n in ("h1", "h2"):
                groups += [(n, [(o, i) for o in range(HB)], w_t[n][:, i, :]) for i in range(HB)]
            groups.append(("w3", [(0, i) for i in range(HB)], w_t["w3"][:, :, :].rearrange("p k m -> p (k m)")))
            block = st.begin()

            @block.sync
            def _(sp):
                for n, r in raw.items():
                    sp.dma_start(r[:, :, :], t[f"L3_ffn_{n}_w"].rearrange("(a p) i -> p a i", p=P)).then_inc(loaded[n], 16)

            @block.gpsimd
            def _(pool):
                for k, n in enumerate(("w1", "w2", "h1", "h2")):
                    pool.dma_start(s_cols[:, k, :], t[f"L3_ffn_{n}_s"].rearrange("(a p) -> p a", p=P),
                                   allow_slow_non_contiguous=True).then_inc(scales_in, 16)
                pool.dma_start(s3_bc[:, :], t["L3_ffn_w3_s"].rearrange("(a c) -> a c", a=1).partition_broadcast(P)
                               .rearrange("p a c -> p (a c)")).then_inc(scales_in, 16)
                pool.wait_ge(scales_in, 80)

            @block.tensor
            def _(pe):
                for g, (n, blocks, _) in enumerate(groups):
                    pe.wait_ge(loaded[n], 16)
                    if g >= 4:
                        pe.wait_ge(copied, g - 3)
                    for j, (o, i) in enumerate(blocks):
                        last = nc.tensor.transpose(tr[:, g % 4, j * P:(j + 1) * P], raw[n][:, o, i * P:(i + 1) * P],
                                                   per.ident[:, :])
                    last.then_inc(flipped, 1)

            @block.scalar
            def _(act):
                for g, (_, _, place) in enumerate(groups):
                    act.wait_ge(flipped, g + 1)
                    nc.scalar.activation(place, tr[:, g % 4, :], ACT.Copy).then_inc(copied, 1)

        with Stage(nc, "L3_ffn") as st:
            h_a = st.sb("h_a", [P, HB, TOKENS])
            h_b = st.sb("h_b", [P, HB, TOKENS])
            gated = st.sb("gated", [P, 2, HALF])
            scaled = st.sb("scaled", [P, 2, HALF])
            bank = st.ps("bank", [P, 8, HALF])
            filled, gate_done, made = st.sem("filled"), st.sem("gate_done"), st.sem("made")
            gelu_done, scaled_ready, added = st.sem("gelu_done"), st.sem("scaled_ready"), st.sem("added")
            N1 = CHUNKS * HB
            block = st.begin()

            @block.tensor
            def _(pe):
                def cols(c):
                    return slice(c * HALF, (c + 1) * HALF)
                for n in range(N1):
                    c, o = divmod(n, HB)
                    if n >= 4:
                        pe.wait_ge(made, n - 3)
                    for g, w in enumerate(("w1", "w2")):
                        last = nc.tensor.matmul(bank[:, 2 * (n % 4) + g, :], w_t[w][:, 0, o * P:(o + 1) * P],
                                                per.x_cols[:, cols(c)], start=True, stop=True)
                    last.then_inc(filled, 1)
                for layer, (w, src) in enumerate((("h1", h_a), ("h2", h_b))):
                    for n in range(N1):
                        c, o = divmod(n, HB)
                        m = layer * N1 + n
                        if layer == 0:
                            pe.wait_ge(made, HB * (c + 1) if m >= 8 else N1)
                        else:
                            pe.wait_ge(gelu_done, HB * (c + 1))
                        if m >= 8:
                            pe.wait_ge(gelu_done, m - 7)
                        for i in range(HB):
                            last = nc.tensor.matmul(bank[:, m % 8, :], w_t[w][:, i, o * P:(o + 1) * P],
                                                    src[:, i, cols(c)], start=i == 0, stop=i == HB - 1)
                        last.then_inc(filled, 1)
                for c in range(CHUNKS):
                    pe.wait_ge(gelu_done, N1 + HB * (c + 1))
                    if c == 0:
                        pe.wait_ge(gelu_done, 2 * N1)
                    for j in range(4):
                        for i in range(HB):
                            last = nc.tensor.matmul(bank[:, c, j * C:(j + 1) * C],
                                                    h_a[:, i, c * HALF + j * P:c * HALF + (j + 1) * P],
                                                    w_t["w3"][:, i, :], start=i == 0, stop=i == HB - 1)
                    last.then_inc(filled, 1)

            @block.scalar
            def _(act):
                for n in range(N1):
                    c, o = divmod(n, HB)
                    act.wait_ge(filled, n + 1)
                    if n >= 2:
                        act.wait_ge(made, n - 1)
                    nc.scalar.activation(gated[:, n % 2, :], bank[:, 2 * (n % 4), :], ACT.Silu,
                                         scale=s_cols[:, 0, o:o + 1]).then_inc(gate_done, 1)
                for layer, dst in enumerate((h_b, h_a)):
                    for n in range(N1):
                        c, o = divmod(n, HB)
                        m = layer * N1 + n
                        act.wait_ge(filled, N1 + m + 1)
                        nc.scalar.activation(dst[:, o, c * HALF:(c + 1) * HALF], bank[:, m % 8, :], ACT.Gelu,
                                             scale=s_cols[:, 2 + layer, o:o + 1]).then_inc(gelu_done, 1)

            @block.vector
            def _(dve):
                for n in range(N1):
                    c, o = divmod(n, HB)
                    dve.wait_ge(gate_done, n + 1)
                    nc.vector.scalar_tensor_tensor(h_a[:, o, c * HALF:(c + 1) * HALF], bank[:, 2 * (n % 4) + 1, :],
                                                   s_cols[:, 1, o:o + 1], gated[:, n % 2, :],
                                                   ALU.mult, ALU.mult).then_inc(made, 1)
                for c in range(CHUNKS):
                    dve.wait_ge(filled, 3 * N1 + c + 1)
                    if c >= 2:
                        dve.wait_ge(added, c - 1)
                    tiles = slice(4 * c, 4 * c + 4)
                    nc.vector.tensor_tensor(scaled[:, c % 2, :].rearrange("p (t c) -> p t c", c=C),
                                            bank[:, c, :].rearrange("p (t c) -> p t c", c=C),
                                            s3_bc[:, :].unsqueeze(1).to_broadcast([P, 4, C]), ALU.mult).then_inc(scaled_ready, 1)
                    dve.wait_ge(scaled_ready, c + 1)
                    nc.vector.tensor_tensor(per.acc[:, tiles, :], scaled[:, c % 2, :].rearrange("p (t c) -> p t c", c=C),
                                            per.x_rows[:, tiles, :], ALU.add).then_inc(added, 1)
    norm_stage(nc, per, "L3_norm1", per.acc, per.x_rows, to_cols=False)



def build_network(nc, t, out, upto=8, start=0):
    with ExitStack() as ctx:
        per = Persistent(nc, ctx)
        load_stage(nc, per, t["L0_attn_x"], t["ident"])
        parts = [
            lambda: layer0_attention(nc, per, t),
            lambda: layer0_ffn(nc, per, t),
            lambda: layer1_attention(nc, per, t),
            lambda: layer1_ffn(nc, per, t),
            lambda: layer2_attention(nc, per, t),
            lambda: layer2_ffn(nc, per, t),
            lambda: layer3_attention(nc, per, t),
            lambda: layer3_ffn(nc, per, t),
        ]
        for part in parts[start:upto]:
            part()
        store_stage(nc, per, out)


def layer0_attention(nc, per, t):
    with ExitStack() as ctx:
        heads = SmallHeads(nc, Held(nc, ctx, "L0"))
        small_qkv_stage(nc, per, "L0_qkv", heads, t["L0_attn_W_qkv"], None, t["L0_attn_b_qkv"],
                        (t["rotation"], t["cos"], t["sin"]))
        attention_stage(nc, per, "L0_attn", "small", H8, D8, D8 ** -0.5,
                        t["L0_attn_W_out"].rearrange("(h d) o -> d h o", d=D8), heads=heads)
    norm_stage(nc, per, "L0_norm0", per.acc, per.x_rows, bias=t["L0_attn_b_out"])


def layer1_attention(nc, per, t):
    with ExitStack() as ctx:
        heads = SmallHeads(nc, Held(nc, ctx, "L1"))
        small_qkv_stage(nc, per, "L1_qkv", heads, t["L1_attn_w_qkv"], t["L1_attn_w_out"], None, None)
        attention_stage(nc, per, "L1_attn", "small", H8, D8, D8 ** -0.5, heads.w_out, heads=heads,
                        masks=(t["mask_t"], t["mask_q"]), windowed=True)
    norm_stage(nc, per, "L1_norm0", per.acc, per.x_rows)


def layer2_attention(nc, per, t):
    w_q, w_kv = t["L2_attn_Wq"], t["L2_attn_Wkv"]
    norm_stage(nc, per, "L2_norm_in", per.x_rows, per.acc, affine=(t["L2_attn_norm_w"], t["L2_attn_norm_b"]))
    attention_stage(nc, per, "L2_attn", "mqa", 8, 64, 64 ** -0.5,
                    t["L2_attn_Wo"].rearrange("(h d) o -> d h o", d=64),
                    weights=(lambda i: w_q[:, span(i * 64, 64)], lambda i: w_kv[:, 0:64],
                             lambda i: w_kv[:, 64:128]), x_init=False)
    norm_stage(nc, per, "L2_norm_out", per.acc, per.acc, affine=(t["L2_attn_out_norm_w"], t["L2_attn_out_norm_b"]),
               plus=per.x_rows, to_cols=False)
    norm_stage(nc, per, "L2_norm0", per.acc, per.x_rows)


def layer3_attention(nc, per, t):
    w = [t[f"L3_attn_W{n}"].rearrange("h d e -> (h d) e") for n in "qkv"]
    attention_stage(nc, per, "L3_attn", "full", 16, 64, 64 ** -0.5,
                    t["L3_attn_Wp"].rearrange("(e h) o -> e h o", h=16),
                    weights=[lambda i, m=m: m[span(i * C, C), :] for m in w])
    norm_stage(nc, per, "L3_norm0", per.acc, per.x_rows, bias=t["L3_attn_bp"])


class Held:

    def __init__(self, nc, ctx, name):
        self.nc, self.ctx, self.name = nc, ctx, name

    def sb(self, name, shape, dt=F32):
        return self.ctx.enter_context(self.nc.sbuf_tensor(f"{self.name}_{name}", shape, dt))


def constants():
    d = np.arange(P)
    rotation = np.zeros((P, P), np.float32)
    for o in range(P):
        h, r = divmod(o, D8)
        if r < D8 // 2:
            rotation[h * D8 + r + D8 // 2, o] = -1.0
        else:
            rotation[h * D8 + r - D8 // 2, o] = 1.0
    inv = (np.float32(1.0) / np.power(np.float32(10000.0), np.arange(0, D8, 2, dtype=np.float32) / np.float32(D8))
           ).astype(np.float32)
    angle = (np.arange(SEQ, dtype=np.float32)[None, :] * inv[d % (D8 // 2)][:, None]).astype(np.float32)
    p, q = np.arange(P)[:, None], np.arange(P)[None, :]
    own = (p <= q) & (q - p < WINDOW)
    before = q + P - p < WINDOW
    ok = np.zeros((P, 3, SEQ), bool)
    for j in range(QB):
        cols = slice(j * P, (j + 1) * P)
        ok[:, 0, cols] = (p <= q) if j == 0 else True
        ok[:, 1, cols] = own & ((p >= PREFIX) | (j > 0))
        ok[:, 2, cols] = before
    mask_t = np.where(ok, 0.0, MASKED).astype(np.float32)
    ok_q = np.zeros((P, 2, 2 * P + PREFIX), bool)
    for j in range(2):
        ok_q[:, j, 0:P] = before.T
        ok_q[:, j, P:2 * P] = ok[:, 1, j * P:(j + 1) * P].T
        ok_q[:, j, 2 * P:] = ok[0:PREFIX, 0, j * P:(j + 1) * P].T
    mask_q = np.where(ok_q, 0.0, MASKED).astype(np.float32)
    return {"ident": np.eye(P, dtype=np.float32), "rotation": rotation,
            "cos": np.cos(angle).astype(np.float32), "sin": np.sin(angle).astype(np.float32),
            "mask_t": mask_t, "mask_q": mask_q,
            "reversed": np.tile(np.arange(32, 0, -1, dtype=np.float32), (P, 1))}


def kernel(**inputs):
    import concourse.bacc as bacc
    from concourse.bass_utils import run_bass_kernel_spmd

    nc = bacc.Bacc("TRN2", target_bir_lowering=False, num_devices=1)
    arrays, t = {}, {}
    for name, a in {**inputs, **constants()}.items():
        arrays[name] = np.ascontiguousarray(a)
        t[name] = nc.dram_tensor(name, arrays[name].shape, mybir.dt.from_np(arrays[name].dtype),
                                 kind="ExternalInput").ap()
    out = nc.dram_tensor("out", (BATCH, SEQ, C), F32, kind="ExternalOutput").ap()
    build_network(nc, t, out)
    return run_bass_kernel_spmd(nc, [arrays], core_ids=[0]).results[0]["out"]
```

```python
import numpy as np
from contextlib import ExitStack

import concourse.bass as bass
from concourse import mybir

F32 = mybir.dt.float32
F32R = mybir.dt.float32r
BF16 = mybir.dt.bfloat16
ALU = mybir.AluOpType
ACT = mybir.ActivationFunctionType
AX = mybir.AxisListType

P = 128
BATCH = 2
SEQ = 1024
C = 128
TOKENS = BATCH * SEQ
TILES = TOKENS // P
QB = SEQ // P
HALF = 512
CHUNKS = TOKENS // HALF
EPS = 1e-5
MASKED = -1e9
WINDOW = 64
PREFIX = 16


class Stage:

    def __init__(self, nc, name):
        self.nc, self.name = nc, name
        self.ctx, self.sems = ExitStack(), []

    def __enter__(self):
        return self

    def sb(self, name, shape, dt=F32):
        return self.ctx.enter_context(self.nc.sbuf_tensor(f"{self.name}_{name}", shape, dt))

    def ps(self, name, shape):
        return self.ctx.enter_context(self.nc.psum_tensor(f"{self.name}_{name}", shape, F32))

    def sem(self, name):
        self.sems.append(self.nc.alloc_semaphore(f"{self.name}_{name}"))
        return self.sems[-1]

    def begin(self):
        self.guard = self.nc.Block()
        return self.guard.__enter__()

    def __exit__(self, *e):
        if e[0] is not None:
            return False
        self.guard.__exit__(None, None, None)
        self.nc.clear_and_free_semaphores(self.sems)
        self.nc.all_engine_barrier()
        self.ctx.close()
        return False


class Persistent:

    def __init__(self, nc, ctx):
        def sb(name, shape, dt=F32):
            return ctx.enter_context(nc.sbuf_tensor(name, shape, dt))
        self.x_rows = sb("x_rows", [P, TILES, C])
        self.x_cols = sb("x_cols", [C, TOKENS])
        self.acc = sb("acc", [P, TILES, C])
        self.ident = sb("identity", [P, P])
        self.ones_row = sb("ones_row", [1, P])


def span(start, n):
    return slice(start, start + n) if isinstance(start, int) else bass.ds(start, n)


def tile_bcast(row_bc):
    return row_bc[:, :].unsqueeze(1).to_broadcast([P, TILES, C])



def load_stage(nc, per, x, ident):
    with Stage(nc, "load") as st:
        tr = st.ps("tr", [P, CHUNKS, HALF])
        x_in, id_in = st.sem("x_in"), st.sem("id_in")
        transposed, ones_set, copied = st.sem("transposed"), st.sem("ones_set"), st.sem("copied")
        block = st.begin()

        @block.sync
        def _(sp):
            sp.dma_start(per.ident[:, :], ident).then_inc(id_in, 16)
            xv = x.rearrange("b (q p) c -> p (b q) c", p=P)
            sp.dma_start(per.x_rows[:, :, :], xv).then_inc(x_in, 16)

        @block.vector
        def _(dve):
            nc.vector.memset(per.ones_row[:, :], 1.0).then_inc(ones_set, 1)

        @block.tensor
        def _(pe):
            pe.wait_ge(id_in, 16)
            pe.wait_ge(x_in, 16)
            for t in range(TILES):
                nc.tensor.transpose(tr[:, t // 4, (t % 4) * P:(t % 4 + 1) * P], per.x_rows[:, t, :],
                                    per.ident[:, :]).then_inc(transposed, 1)

        @block.scalar
        def _(act):
            for c in range(CHUNKS):
                act.wait_ge(transposed, 4 * c + 4)
                nc.scalar.activation(per.x_cols[:, c * HALF:(c + 1) * HALF], tr[:, c, :],
                                     ACT.Copy).then_inc(copied, 1)


def norm_stage(nc, per, name, src, dst, bias=None, affine=None, plus=None, to_cols=True):
    with Stage(nc, name) as st:
        stats = st.sb("stats", [P, TILES, 6])
        moments = st.sb("moments", [P, TILES, 2])
        var = st.sb("var", [P, TILES])
        power = st.sb("power", [P, TILES])
        rstd = st.sb("rstd", [P, TILES])
        rows_bc = st.sb("rows_bc", [P, 3, C])
        tr = st.ps("tr", [P, CHUNKS, HALF])
        rows_in = st.sem("rows_in")
        biased, stats_done = st.sem("biased"), st.sem("stats_done")
        moments_ready, rstd_ready = st.sem("moments_ready"), st.sem("rstd_ready")
        var_ready, power_set = st.sem("var_ready"), st.sem("power_set")
        normed, scaled = st.sem("normed"), st.sem("scaled")
        transposed, copied = st.sem("transposed"), st.sem("copied")
        block = st.begin()
        rows = [r for r in ([bias] if bias is not None else []) + list(affine or [])]

        @block.sync
        def _(sp):
            for k, r in enumerate(rows):
                sp.dma_start(rows_bc[:, k, :],
                             r.rearrange("(a c) -> a c", a=1).partition_broadcast(P)
                             .rearrange("p a c -> p (a c)")).then_inc(rows_in, 16)

        @block.vector
        def _(dve):
            if rows:
                dve.wait_ge(rows_in, 16 * len(rows))
            if bias is not None:
                nc.vector.tensor_tensor(src[:, :, :], src[:, :, :], tile_bcast(rows_bc[:, 0, :]),
                                        ALU.add).then_inc(biased, 1)
                dve.wait_ge(biased, 1)
            for t in range(TILES):
                nc.vector.bn_stats(stats[:, t, :], src[:, t, :]).then_inc(stats_done, 1)
            for t in range(TILES):
                dve.wait_ge(stats_done, t + 1)
                nc.vector.bn_aggr(moments[:, t, :], stats[:, t, :]).then_inc(moments_ready, 1)
            dve.wait_ge(moments_ready, TILES)
            nc.vector.tensor_scalar(var[:, :], moments[:, :, 1], EPS, None, ALU.add).then_inc(var_ready, 1)
            dve.wait_ge(rstd_ready, 1)
            for t in range(TILES):
                nc.vector.tensor_scalar(dst[:, t, :], src[:, t, :], moments[:, t, 0:1],
                                        rstd[:, t:t + 1], ALU.subtract, ALU.mult).then_inc(normed, 1)
            if affine is not None:
                k = len(rows) - 2
                dve.wait_ge(normed, TILES)
                nc.vector.tensor_tensor(dst[:, :, :], dst[:, :, :], tile_bcast(rows_bc[:, k, :]),
                                        ALU.mult).then_inc(scaled, 1)
                dve.wait_ge(scaled, 1)
                nc.vector.tensor_tensor(dst[:, :, :], dst[:, :, :], tile_bcast(rows_bc[:, k + 1, :]),
                                        ALU.add).then_inc(scaled, 1)
                if plus is not None:
                    dve.wait_ge(scaled, 2)
                    nc.vector.tensor_tensor(dst[:, :, :], dst[:, :, :], plus[:, :, :],
                                            ALU.add).then_inc(scaled, 1)

        @block.gpsimd
        def _(pool):
            nc.gpsimd.memset(power[:, :], -0.5).then_inc(power_set, 1)
            pool.wait_ge(power_set, 1)
            pool.wait_ge(var_ready, 1)
            nc.gpsimd.tensor_tensor(rstd[:, :], var[:, :], power[:, :], ALU.pow).then_inc(rstd_ready, 1)

        if to_cols:
            @block.tensor
            def _(pe):
                if affine is not None:
                    pe.wait_ge(scaled, 2)
                for t in range(TILES):
                    pe.wait_ge(normed, t + 1)
                    nc.tensor.transpose(tr[:, t // 4, (t % 4) * P:(t % 4 + 1) * P], dst[:, t, :],
                                        per.ident[:, :]).then_inc(transposed, 1)

            @block.scalar
            def _(act):
                for c in range(CHUNKS):
                    act.wait_ge(transposed, 4 * c + 4)
                    nc.scalar.activation(per.x_cols[:, c * HALF:(c + 1) * HALF], tr[:, c, :],
                                         ACT.Copy).then_inc(copied, 1)


def store_stage(nc, per, out):
    with Stage(nc, "store") as st:
        stored = st.sem("stored")
        block = st.begin()

        @block.sync
        def _(sp):
            sp.dma_start(out.rearrange("b (q p) c -> p (b q) c", p=P),
                         per.x_rows[:, :, :]).then_inc(stored, 16)
            sp.wait_ge(stored, 16)



D8 = 8
H8 = 16


class SmallHeads:

    def __init__(self, nc, st):
        self.stacks = {x: nc.dram_tensor(f"{st.name}_stack_{x}", (H8 * 4 * D8, TOKENS), F32).ap() for x in "qk"}
        self.v_rows = st.sb("v_rows", [P, TILES, H8 * (D8 + 1)])
        self.w_out = st.sb("w_out_flipped", [C, C])


def small_qkv_stage(nc, per, name, heads, w_in, w_out, bias, rope):
    w_transposed = w_out is not None
    with Stage(nc, name) as st:
        w_raw = st.sb("w_raw", [P, 4, P])
        w = st.sb("w", [P, 3, P])
        acc_ps = st.ps("acc_ps", [P, 4, HALF])
        rot_ps = st.ps("rot_ps", [P, 4, HALF])
        parts = {n: st.sb(n, [P, TOKENS], F32R) for n in ("qh", "ql", "kh", "kl")}
        flat = st.sb("flat", [P, 2, HALF])
        t_cos = st.sb("t_cos", [P, 2, HALF])
        t_sin = st.sb("t_sin", [P, 2, HALF])
        roped = st.sb("roped", [P, 2, HALF])
        b_cols = st.sb("b_cols", [P, 2])
        b_row = st.sb("b_row", [1, C])
        rot = st.sb("rot", [P, P])
        cos = st.sb("cos", [P, SEQ])
        sin = st.sb("sin", [P, SEQ])
        loaded, w_flipped, w_ready = st.sem("loaded"), st.sem("w_flipped"), st.sem("w_ready")
        proj_done, flat_ready, rot_done = st.sem("proj_done"), st.sem("flat_ready"), st.sem("rot_done")
        cos_done, sin_done, roped_ready = st.sem("cos_done"), st.sem("sin_done"), st.sem("roped_ready")
        high_ready, low_ready, stacked = st.sem("high_ready"), st.sem("low_ready"), st.sem("stacked")
        v_done, v_copied, ones_set = st.sem("v_done"), st.sem("v_copied"), st.sem("ones_set")
        n_loads = 1 + w_transposed + (3 if bias is not None else 0) + (3 if rope is not None else 0)
        steps = [(x, c) for x in range(2) for c in range(CHUNKS)]
        block = st.begin()

        @block.sync
        def _(sp):
            if w_transposed:
                sp.dma_start(w_raw[:, 0:3, :], w_in.rearrange("(a o) i -> o a i", a=3)).then_inc(loaded, 16)
                sp.dma_start(w_raw[:, 3, :], w_out).then_inc(loaded, 16)
            else:
                sp.dma_start(w[:, :, :], w_in.rearrange("i (a o) -> i a o", a=3)).then_inc(loaded, 16)
            if bias is not None:
                for x in range(2):
                    sp.dma_start(b_cols[:, x:x + 1],
                                 bias[x * C:(x + 1) * C].rearrange("(p a) -> p a", a=1)).then_inc(loaded, 16)
                sp.dma_start(b_row[:, :], bias[2 * C:3 * C].rearrange("(a c) -> a c", a=1)).then_inc(loaded, 16)
            if rope is not None:
                for dst, src in zip((rot, cos, sin), rope):
                    sp.dma_start(dst[:, :], src).then_inc(loaded, 16)
            for n, (x, c) in enumerate(steps):
                cols = slice(c * HALF, (c + 1) * HALF)
                stack = heads.stacks["qk"[x]].rearrange("(h r d) t -> h r d t", r=4, d=D8)
                sp.wait_ge(low_ready, n + 1)
                for r, part in enumerate(("hhll", "hlhl")[x]):
                    sp.dma_start(stack[:, r, :, cols],
                                 parts["qk"[x] + part][:, cols].bitcast(F32)).then_inc(stacked, 16)
            sp.wait_ge(stacked, 16 * 4 * len(steps))

        @block.tensor
        def _(pe):
            pe.wait_ge(loaded, 16 * n_loads)
            if w_transposed:
                for a in range(4):
                    nc.tensor.transpose(acc_ps[:, 0, a * P:(a + 1) * P], w_raw[:, a, :],
                                        per.ident[:, :]).then_inc(w_flipped, 1)
                pe.wait_ge(w_ready, 2)

            def rotate(n):
                pe.wait_ge(flat_ready, n + 1)
                if n >= 4:
                    pe.wait_ge(sin_done, n - 3)
                nc.tensor.matmul(rot_ps[:, n % 4, :], rot[:, :], flat[:, n % 2, :],
                                 start=True, stop=True).then_inc(rot_done, 1)

            for n, (x, c) in enumerate(steps):
                if n >= 4:
                    pe.wait_ge(flat_ready if rope is not None else low_ready, n - 3)
                nc.tensor.matmul(acc_ps[:, n % 4, :], w[:, x, :], per.x_cols[:, c * HALF:(c + 1) * HALF],
                                 start=True, stop=True).then_inc(proj_done, 1)
                if rope is not None and n >= 1:
                    rotate(n - 1)
            if rope is not None:
                rotate(len(steps) - 1)
            pe.wait_ge(flat_ready if rope is not None else low_ready, len(steps))
            for t in range(TILES):
                if bias is not None:
                    nc.tensor.matmul(acc_ps[:, t // 4, (t % 4) * P:(t % 4 + 1) * P], per.ones_row[:, :],
                                     b_row[:, :], start=True, stop=False)
                nc.tensor.matmul(acc_ps[:, t // 4, (t % 4) * P:(t % 4 + 1) * P],
                                 per.x_cols[:, t * P:(t + 1) * P], w[:, 2, :],
                                 start=bias is None, stop=True).then_inc(v_done, 1)

        @block.scalar
        def _(act):
            if w_transposed:
                act.wait_ge(w_flipped, 4)
                nc.scalar.activation(heads.w_out[:, :], acc_ps[:, 0, 3 * P:4 * P], ACT.Copy).then_inc(w_ready, 1)
                nc.scalar.activation(w[:, :, :], acc_ps[:, 0, 0:3 * P].rearrange("p (a o) -> p a o", a=3),
                                     ACT.Copy).then_inc(w_ready, 1)
            if rope is not None:
                for n, (x, c) in enumerate(steps):
                    act.wait_ge(proj_done, n + 1)
                    if n >= 2:
                        act.wait_ge(rot_done, n - 1)
                        act.wait_ge(cos_done, n - 1)
                    nc.scalar.activation(flat[:, n % 2, :], acc_ps[:, n % 4, :], ACT.Identity,
                                         bias=b_cols[:, x:x + 1]).then_inc(flat_ready, 1)
            act.wait_ge(ones_set, 1)
            for c in range(CHUNKS):
                act.wait_ge(v_done, 4 * c + 4)
                nc.scalar.activation(
                    heads.v_rows[:, 4 * c:4 * c + 4, :].rearrange("p t (h d) -> p t h d", d=D8 + 1)[:, :, :, 0:D8],
                    acc_ps[:, c, :].rearrange("p (t h d) -> p t h d", t=4, d=D8), ACT.Copy).then_inc(v_copied, 1)

        @block.gpsimd
        def _(pool):
            nc.gpsimd.memset(heads.v_rows[:, :, :], 1.0).then_inc(ones_set, 1)
            if rope is not None:
                for n, (x, c) in enumerate(steps):
                    pool.wait_ge(flat_ready, n + 1)
                    if n >= 2:
                        pool.wait_ge(roped_ready, n - 1)
                    at = (c % 2) * HALF
                    nc.gpsimd.tensor_tensor(t_cos[:, n % 2, :], flat[:, n % 2, :], cos[:, at:at + HALF],
                                            ALU.mult).then_inc(cos_done, 1)

        @block.vector
        def _(dve):
            for n, (x, c) in enumerate(steps):
                high, low = [parts["qk"[x] + s][:, c * HALF:(c + 1) * HALF] for s in "hl"]
                if rope is not None:
                    at = (c % 2) * HALF
                    dve.wait_ge(rot_done, n + 1)
                    nc.vector.tensor_tensor(t_sin[:, n % 2, :], rot_ps[:, n % 4, :], sin[:, at:at + HALF],
                                            ALU.mult).then_inc(sin_done, 1)
                    dve.wait_ge(sin_done, n + 1)
                    dve.wait_ge(cos_done, n + 1)
                    nc.vector.tensor_tensor(roped[:, n % 2, :], t_cos[:, n % 2, :], t_sin[:, n % 2, :],
                                            ALU.add).then_inc(roped_ready, 1)
                    dve.wait_ge(roped_ready, n + 1)
                    value = roped[:, n % 2, :]
                else:
                    dve.wait_ge(proj_done, n + 1)
                    value = acc_ps[:, n % 4, :]
                nc.vector.tensor_copy(high, value).then_inc(high_ready, 1)
                dve.wait_ge(high_ready, n + 1)
                nc.vector.tensor_tensor(low, value, high.bitcast(F32), ALU.subtract).then_inc(low_ready, 1)



class Jobs:

    def __init__(self, next_uses, out_uses, prologue_uses):
        self.r = out_uses
        self.per = next_uses + out_uses
        self.u0 = prologue_uses + next_uses

    def first(self, i, b):
        return isinstance(i, int) and i == 0 and b == 0

    def use(self, i, b, k):
        fixed = self.u0 + self.per * b + k - (0 if self.first(i, b) else self.r)
        return i * (2 * self.per) + fixed, fixed % 2

    def job(self, i, b, each=1, plus=0):
        return i * (2 * each) + (each * b + plus)


def attention_stage(nc, per, name, kind, n_heads, dim, scale, w_o, *, heads=None, weights=None, x_init=True):
    small = kind == "small"
    full = kind == "full"
    rows = 2 * 2 * D8 if small else 2 * dim
    steps = QB
    v_width = 32 if small else dim
    group = P // v_width
    units = 2 * (steps // group)
    pre_uses = 6 if kind == "mqa" else 0
    half_maxima = [("max", k) for k in range(2 * QB)]
    plan = [("query", h) for h in range(0 if small else 2)] + [("key", h) for h in range(2 if full else 0)]
    n_split = len(plan)
    plan += half_maxima[:QB] + [("values", 0)] * full + half_maxima[QB:]
    places = 3 * steps
    rows_place = places - 5
    spread = rows_place - 1
    r_uses = 3
    J = Jobs(len(plan) + 1, r_uses, pre_uses)
    OUT = C + 1
    last_i = n_heads - 1
    max_at = 64 if small else dim
    k_rows = max_at + 1 if small else P
    v_used = dim + 1
    with Stage(nc, name) as st:
        keys = [st.sb(f"keys{b}", [k_rows, SEQ], F32R) for b in range(2)]
        queries = [st.sb(f"queries{b}", [k_rows, SEQ], F32R) for b in range(2)]
        if small:
            keys_m = [st.sb(f"keys_m{b}", [max_at, SEQ], F32R) for b in range(2)]
            queries_m = [st.sb(f"queries_m{b}", [max_at, SEQ], F32R) for b in range(2)]
        else:
            keys_m, queries_m = keys, queries
            keys_b = [st.sb(f"keys_b{b}", [dim + 1, SEQ], F32R) for b in range(2)]
            queries_b = [st.sb(f"queries_b{b}", [dim + 1, SEQ], F32R) for b in range(2)]
            w_qk = st.sb("w_qk", [P, 4, dim])
            w_v = st.sb("w_v", [P, dim])
            prob_sum = [st.sb(f"prob_sum{b}", [P, SEQ]) for b in range(2)]
            ones_col = st.sb("ones_col", [P, 1])
        values = [st.sb(f"values{b}", [P, QB, v_width]) for b in range(2)]
        probs = st.sb("probs", [P, steps, SEQ])
        out_cols = [st.sb(f"out_cols{b}", [P, SEQ]) for b in range(2)]
        w_out = st.sb("w_out_heads", [P, n_heads * OUT])
        part_max = st.sb("part_max", [P, QB, 2])
        neg_max = st.sb("neg_max", [P, QB], F32R)
        max_rows = st.sb("max_rows", [QB, P])
        w_head = [st.sb(f"w_head{b}", [P, OUT]) for b in range(2)]
        recip = st.sb("recip", [P, 2, QB])
        work = st.ps("work", [P, 2, HALF])
        scores = st.ps("scores", [P, 2, SEQ])
        outs = st.ps("outs", [P, SEQ])

        work_filled, work_drained = st.sem("work_filled"), st.sem("work_drained")
        scores_ready, exp_done = st.sem("scores_ready"), st.sem("exp_done")
        values_done, out_saved, acc_set = st.sem("values_done"), st.sem("out_saved"), st.sem("acc_set")
        split_done, recip_done = st.sem("split_done"), st.sem("recip_done")
        max_joined, max_loaded = st.sem("max_joined"), st.sem("max_loaded")
        operands_in = [st.sem(f"operands_in{b}") for b in range(2)]
        max_operands_in = [st.sem(f"max_operands_in{b}") for b in range(2)]
        weights_in, probs_added = st.sem("weights_in"), st.sem("probs_added")
        values_in, keys_b_ready = st.sem("values_in"), st.sem("keys_b_ready")
        consts_in, consts_set, w_out_in = st.sem("consts_in"), st.sem("consts_set"), st.sem("w_out_in")
        w_head_ready = st.sem("w_head_ready")
        block = st.begin()

        def iterations(eng, body):
            body(0)
            with eng.Fori(1, last_i) as i:
                body(i)
            body(last_i)

        def is_last(i, b):
            return isinstance(i, int) and i == last_i and b == 1

        def after(i, b):
            return (i, 1) if b == 0 else (i + 1, 0)

        def before(i, b):
            return (i, 0) if b else (i - 1, 1)

        def at_least(eng, sem, value):
            if not isinstance(value, int) or value > 0:
                eng.wait_ge(sem, value)

        def unit_at(t):
            v = t - 2 if group == 2 else {5: 0, 6: 1, 9: 2, 10: 3}.get(t, -1)
            return divmod(v, 2) if 0 <= v < units else None

        save_steps = (0, 1) if group == 2 else (2, 3)
        n_weights = {"small": 0, "mqa": 2, "full": 5}[kind]
        n_consts = (group if small else 1) + 2 + 2 * (6 if small else 1)

        @block.sync
        def _(sp):
            def stacked(i, b, to_keys, to_queries, signal):
                cols = slice(b * SEQ, (b + 1) * SEQ)
                for dst, x in ((to_keys, "k"), (to_queries, "q")):
                    sp.dma_start(dst[0:rows, :].bitcast(F32),
                                 heads.stacks[x][span(i * rows, rows), cols]).then_inc(signal, 16)

            def operands(i, b):
                stacked(i, b, keys[b], queries[b], operands_in[b])

            def max_operands(i, b):
                stacked(i, b, keys_m[b], queries_m[b], max_operands_in[b])

            def head_projections(i):
                for k in range(2):
                    sp.dma_start(w_qk[:, k, :], weights[0](i)).then_inc(weights_in, 16)
                if full:
                    for k in range(2):
                        sp.dma_start(w_qk[:, 2 + k, :], weights[1](i)).then_inc(weights_in, 16)
                    sp.dma_start(w_v[:, :], weights[2](i)).then_inc(weights_in, 16)

            def maxima(b, use):
                sp.wait_ge(work_drained, use + 1)
                row = (queries if small else queries_b)[b][max_at:max_at + 1, :]
                sp.dma_start(row.bitcast(F32), max_rows[:, :]).then_inc(max_loaded, 16)

            if small:
                max_operands(0, 0)
                operands(0, 0)
                max_operands(0, 1)
            else:
                if kind == "mqa":
                    for k in range(2):
                        sp.dma_start(w_qk[:, 2 + k, :], weights[1](0)).then_inc(consts_in, 16)
                    sp.dma_start(w_v[:, :], weights[2](0)).then_inc(consts_in, 16)
                head_projections(0)
            maxima(0, J.u0 - 1)

            def slot(i, b):
                if is_last(i, b):
                    return
                ni, nb = after(i, b)
                if small:
                    at_least(sp, scores_ready, J.job(i, b, steps))
                    operands(ni, nb)
                    if not (isinstance(i, int) and i == last_i):
                        sp.wait_ge(work_filled, J.use(i, b, 0)[0])
                        max_operands(i + 1, b)
                elif b == 0 and not (isinstance(i, int) and i == last_i):
                    last_use = plan.index(("values", 0)) if full else n_split - 1
                    sp.wait_ge(work_filled, J.use(i, b, last_use)[0] + 1)
                    head_projections(i + 1)
                maxima(nb, J.use(i, b, len(plan))[0])

            iterations(sp, lambda i: (slot(i, 0), slot(i, 1)))

        @block.gpsimd
        def _(pool):
            wv = w_out[:, :].rearrange("p (h c) -> p h c", c=OUT)
            done = 0

            def filled(op):
                nonlocal done
                op.then_inc(consts_set, 1)
                done += 1
                pool.wait_ge(consts_set, done)

            filled(nc.gpsimd.memset(w_out[:, :], 0.0))
            filled(nc.gpsimd.memset(wv[:, :, C:OUT], 1.0 if small else 0.0))
            if small:
                for j in range(group):
                    part = wv[j * v_width:(j + 1) * v_width, :, C:OUT]
                    filled(nc.gpsimd.affine_select(out=part, in_=part, compare_op=ALU.is_equal, fill=0.0,
                                                   base=-dim, pattern=[[0, n_heads], [0, 1]], channel_multiplier=1))
            else:
                filled(nc.gpsimd.memset(ones_col[:, :], 1.0))
            for b in range(2):
                filled(nc.gpsimd.memset((keys if small else keys_b)[b][max_at:max_at + 1, :].bitcast(F32), 1.0))
                if small:
                    for x in (keys[b], queries[b], keys_m[b], queries_m[b]):
                        filled(nc.gpsimd.memset(x[rows:max_at, :].bitcast(F32), 0.0))
                    filled(nc.gpsimd.memset(values[b][:, :, :], 0.0))
            assert done == n_consts
            for j in range(group):
                pool.dma_start(wv[j * v_width:j * v_width + dim, :, 0:C], w_o).then_inc(w_out_in, 16)
            if x_init:
                nc.gpsimd.tensor_copy(per.acc[:, :, :], per.x_rows[:, :, :]).then_inc(acc_set, 1)
            else:
                nc.gpsimd.memset(per.acc[:, :, :], 0.0).then_inc(acc_set, 1)

            def slot(i, b):
                pool.wait_ge(work_filled, J.use(i, b, 0)[0])
                for k in range(1, steps):
                    pool.wait_ge(exp_done, J.job(i, b, steps, k + 1))
                    at_least(pool, probs_added, J.job(i, b, steps - 1, k - 1))
                    nc.gpsimd.tensor_tensor(prob_sum[b][:, :], probs[:, 0, :] if k == 1 else prob_sum[b][:, :],
                                            probs[:, k, :], ALU.add).then_inc(probs_added, 1)

            if not small:
                iterations(pool, lambda i: (slot(i, 0), slot(i, 1)))

        @block.tensor
        def _(pe):
            def fill(use):
                at_least(pe, work_drained, use - 1)

            def project(b, h, w, bank):
                nc.tensor.matmul(work[:, bank, :], w_qk[:, w:w + 2, :].rearrange("p a d -> p (a d)"),
                                 per.x_cols[:, b * SEQ + h * HALF:b * SEQ + (h + 1) * HALF],
                                 start=True, stop=True).then_inc(work_filled, 1)

            def project_values(b, bank):
                for t in range(QB):
                    last = nc.tensor.matmul(work[:, bank, t * dim:(t + 1) * dim],
                                            per.x_cols[:, b * SEQ + t * P:b * SEQ + (t + 1) * P], w_v[:, :],
                                            start=True, stop=True)
                last.then_inc(work_filled, 1)

            def next_job_use(b, n, u, bank):
                what, k = plan[n]
                if what == "query":
                    fill(u)
                    project(b, k, 0, bank)
                elif what == "key":
                    fill(u)
                    project(b, k, 2, bank)
                elif what == "values":
                    fill(u)
                    project_values(b, bank)
                else:
                    at_least(pe, work_drained, u if k == 0 and n_split else u - 1)
                    q, h = divmod(k, 2)
                    nc.tensor.matmul(work[:, bank, :], queries_m[b][0:(max_at if small else P), q * P:(q + 1) * P],
                                     keys_m[b][0:(max_at if small else P), h * HALF:(h + 1) * HALF],
                                     start=True, stop=True).then_inc(work_filled, 1)

            def max_rows_use(u, bank, job_count):
                fill(u)
                pe.wait_ge(max_joined, job_count)
                nc.tensor.transpose(work[0:QB, bank, 0:P], neg_max[:, :].bitcast(F32),
                                    per.ident[:, :]).then_inc(work_filled, 1)

            def half_scores(i, b, k, h):
                bank = k % 2
                cols = slice(h * HALF, (h + 1) * HALF)
                if h == 0:
                    at_least(pe, exp_done, J.job(i, b, steps, k - 1))
                last = nc.tensor.matmul(scores[:, bank, cols], keys[b][:, k * P:(k + 1) * P],
                                        queries[b][:, cols], start=True, stop=small)
                if not small:
                    last = nc.tensor.matmul(scores[:, bank, cols], keys_b[b][:, k * P:(k + 1) * P],
                                            queries_b[b][:, cols], start=False, stop=True)
                if h:
                    last.then_inc(scores_ready, 1)

            def value_unit(i, b, g, h):
                pe.wait_ge(exp_done, J.job(i, b, steps, group * (g + 1)))
                if g == 0:
                    at_least(pe, out_saved, J.job(i, b, 2, h - 1))
                    if small and h == 0:
                        pe.wait_ge(values_in, J.job(i, b, 1, 1))
                cols = slice(h * HALF, (h + 1) * HALF)
                for j in range(group):
                    last = nc.tensor.matmul(outs[j * v_width:(j + 1) * v_width, cols], values[b][:, group * g + j, :],
                                            probs[:, group * g + j, cols], start=g == 0,
                                            stop=group * (g + 1) == steps, skip_group_check=True)
                last.then_inc(values_done, 1)

            def output_use(i, b, k, u, bank):
                if k == 0:
                    pe.wait_ge(out_saved, J.job(i, b, 2, 2))
                    pe.wait_ge(w_head_ready, J.job(i, b, 1, 1))
                    if not small:
                        pe.wait_ge(probs_added, J.job(i, b, steps - 1, steps - 1))
                fill(u)
                wide = OUT if small else C
                for n, j in enumerate(range(3 * k, min(3 * k + 3, QB))):
                    last = nc.tensor.matmul(work[:, bank, n * OUT:n * OUT + wide], out_cols[b][:, j * P:(j + 1) * P],
                                            w_head[b][:, 0:wide], start=True, stop=True)
                    if not small:
                        last = nc.tensor.matmul(work[:, bank, n * OUT + C:(n + 1) * OUT],
                                                prob_sum[b][:, j * P:(j + 1) * P], ones_col[:, :],
                                                start=True, stop=True)
                last.then_inc(work_filled, 1)

            pe.wait_ge(consts_set, n_consts)
            if small:
                pe.wait_ge(max_operands_in[0], 32)
            elif kind == "mqa":
                pe.wait_ge(consts_in, 16 * 3)
                for b in range(2):
                    for h in range(2):
                        fill(3 * b + h)
                        project(b, h, 2, (3 * b + h) % 2)
                    fill(3 * b + 2)
                    project_values(b, (3 * b + 2) % 2)
            if not small:
                pe.wait_ge(weights_in, 16 * n_weights)
            for n in range(len(plan)):
                next_job_use(0, n, pre_uses + n, (pre_uses + n) % 2)
            max_rows_use(J.u0 - 1, (J.u0 - 1) % 2, 1)

            def slot(i, b):
                last_slot, first_slot = is_last(i, b), J.first(i, b)
                ni, nb = after(i, b)
                r0 = 0 if last_slot else len(plan) + 1

                def between(place):
                    if not last_slot:
                        if place == 0 and small:
                            pe.wait_ge(max_operands_in[nb], ni * 32 + 32)
                        elif place == 0 and nb == 0:
                            pe.wait_ge(weights_in, ni * (16 * n_weights) + 16 * n_weights)
                        for n in range(place * len(plan) // spread, min(place + 1, spread) * len(plan) // spread):
                            next_job_use(nb, n, *J.use(i, b, n))
                        if place == rows_place:
                            max_rows_use(*J.use(i, b, len(plan)), J.job(i, b, 1, 2))
                    if place >= places - 3 and not first_slot:
                        k = place - (places - 3)
                        output_use(*before(i, b), k, *J.use(i, b, r0 + k))

                pe.wait_ge(max_loaded, J.job(i, b, 16, 16))
                if small:
                    pe.wait_ge(operands_in[b], i * 32 + 32)
                elif full:
                    pe.wait_ge(keys_b_ready, J.job(i, b, 1, 1))
                elif first_slot:
                    pe.wait_ge(keys_b_ready, 2)
                for k in range(steps):
                    half_scores(i, b, k, 0)
                    between(3 * k)
                    half_scores(i, b, k, 1)
                    between(3 * k + 1)
                    if unit_at(k + steps) and not first_slot:
                        value_unit(*before(i, b), *unit_at(k + steps))
                    if unit_at(k):
                        value_unit(i, b, *unit_at(k))
                    between(3 * k + 2)

            iterations(pe, lambda i: (slot(i, 0), slot(i, 1)))
            for k in range(steps):
                if unit_at(k + steps):
                    value_unit(last_i, 1, *unit_at(k + steps))
            for k in range(3):
                output_use(last_i, 1, k, *J.use(last_i, 1, r_uses + k))

        @block.scalar
        def _(act):
            def save(i, b, h):
                act.wait_ge(values_done, J.job(i, b, units, units - 1 + h))
                cols = slice(h * HALF, (h + 1) * HALF)
                nc.scalar.activation(out_cols[b][:, cols], outs[:, cols], ACT.Copy).then_inc(out_saved, 1)

            def high_keys(b, use):
                act.wait_ge(work_drained, use + 1)
                nc.scalar.activation(keys_b[b][0:dim, :], keys[b][0:dim, :].bitcast(F32),
                                     ACT.Copy).then_inc(keys_b_ready, 1)

            if kind == "mqa":
                for b in range(2):
                    high_keys(b, 3 * b + 1)
            if full:
                high_keys(0, 3)

            def slot(i, b):
                for k in range(steps):
                    act.wait_ge(scores_ready, J.job(i, b, steps, k + 1))
                    at_least(act, values_done, J.job(i, b, units, 2 * (k // group + 1) - units))
                    if not small:
                        at_least(act, probs_added, J.job(i, b, steps - 1, max(k, 1) - (steps - 1)))
                    nc.scalar.activation(probs[:, k, :], scores[:, k % 2, :], ACT.Exp, scale=scale).then_inc(exp_done, 1)
                    if k in save_steps and not J.first(i, b):
                        save(*before(i, b), save_steps.index(k))
                    if k == 3 and full and not is_last(i, b):
                        high_keys(1 - b, J.use(i, b, 3)[0])

            iterations(act, lambda i: (slot(i, 0), slot(i, 1)))
            for h in range(2):
                save(last_i, 1, h)

        @block.vector
        def _(dve):
            pre_splits = 4 if kind == "mqa" else 0

            def split(whole, low, part, b, h, u, bank, s):
                cols = slice(h * HALF, (h + 1) * HALF)
                dve.wait_ge(work_filled, u + 1)
                nc.vector.tensor_copy(whole[:, cols], work[:, bank, :]).then_inc(split_done, 1)
                dve.wait_ge(split_done, s + 1)
                nc.vector.tensor_tensor(low[part, cols], work[part, bank, :], whole[part, cols].bitcast(F32),
                                        ALU.subtract).then_inc(work_drained, 1)

            def split_key(b, h, u, bank, s):
                split(keys[b], keys[b], slice(dim, 2 * dim), b, h, u, bank, s)

            def copy_values(b, u, bank):
                dve.wait_ge(work_filled, u + 1)
                nc.vector.tensor_copy(values[b][:, :, :],
                                      work[:, bank, :].rearrange("p (t d) -> p t d", d=dim)).then_inc(work_drained, 1)

            def next_job_use(b, n, u, bank, s0):
                what, k = plan[n]
                if what == "query":
                    split(queries[b], queries_b[b], slice(0, dim), b, k, u, bank, s0 + k)
                elif what == "key":
                    split_key(b, k, u, bank, s0 + 2 + k)
                elif what == "values":
                    copy_values(b, u, bank)
                else:
                    dve.wait_ge(work_filled, u + 1)
                    nc.vector.tensor_reduce(part_max[:, k // 2, k % 2:k % 2 + 1], work[:, bank, :], AX.X,
                                            ALU.max).then_inc(work_drained, 1)

            def join_max(u, bank, dma_value):
                dve.wait_ge(work_drained, u)
                nc.vector.tensor_reduce(neg_max[:, :], part_max[:, :, :], AX.X, ALU.max,
                                        negate=True).then_inc(max_joined, 1)
                dve.wait_ge(work_filled, u + 1)
                at_least(dve, max_loaded, dma_value)
                nc.vector.tensor_copy(max_rows[:, :], work[0:QB, bank, 0:P]).then_inc(work_drained, 1)

            def output_use(b, k, u, bank, r0):
                n = min(3, QB - 3 * k)
                dve.wait_ge(work_filled, u + 1)
                at = work[:, bank, 0:n * OUT].rearrange("p (j c) -> p j c", c=OUT)
                nc.vector.reciprocal(recip[:, b, 3 * k:3 * k + n], at[:, :, C]).then_inc(recip_done, 1)
                dve.wait_ge(recip_done, r0 + k + 1)
                for j in range(n):
                    t = b * QB + 3 * k + j
                    last = nc.vector.scalar_tensor_tensor(per.acc[:, t, :], at[:, j, 0:C],
                                                          recip[:, b, 3 * k + j:3 * k + j + 1], per.acc[:, t, :],
                                                          ALU.mult, ALU.add)
                last.then_inc(work_drained, 1)

            def head_weights(i, b):
                nc.vector.tensor_scalar(w_head[b][:, :], w_out[:, span(i * OUT, OUT)], 1.0, None,
                                        ALU.mult).then_inc(w_head_ready, 1)

            def head_values(i, b):
                nc.vector.tensor_scalar(values[b][:, :, 0:v_used],
                                        heads.v_rows[:, b * QB:(b + 1) * QB, span(i * v_used, v_used)], 1.0, None,
                                        ALU.mult).then_inc(values_in, 1)

            dve.wait_ge(consts_set, n_consts)
            dve.wait_ge(w_out_in, 16 * group)
            if small:
                head_values(0, 0)
            if kind == "mqa":
                for b in range(2):
                    for h in range(2):
                        split_key(b, h, 3 * b + h, (3 * b + h) % 2, 2 * b + h)
                    copy_values(b, 3 * b + 2, (3 * b + 2) % 2)
            for n in range(len(plan)):
                next_job_use(0, n, pre_uses + n, (pre_uses + n) % 2, pre_splits)
            join_max(J.u0 - 1, (J.u0 - 1) % 2, 0)

            def slot(i, b):
                last_slot, first_slot = is_last(i, b), J.first(i, b)
                ni, nb = after(i, b)
                r0 = 0 if last_slot else len(plan) + 1
                dve.wait_ge(work_filled, J.use(i, b, 0)[0])
                head_weights(i, b)
                if not last_slot:
                    at_least(dve, scores_ready, J.job(i, b, steps))
                    for n in range(len(plan)):
                        if n == n_split + QB:
                            at_least(dve, values_done, J.job(i, b, units))
                            if small:
                                head_values(ni, nb)
                        next_job_use(nb, n, *J.use(i, b, n), J.job(i, b, n_split, n_split + pre_splits))
                    join_max(*J.use(i, b, len(plan)), J.job(i, b, 16, 16))
                if not first_slot:
                    for k in range(3):
                        output_use(1 - b, k, *J.use(i, b, r0 + k), J.job(i, b, 3, -3))

            dve.wait_ge(acc_set, 1)
            iterations(dve, lambda i: (slot(i, 0), slot(i, 1)))
            for k in range(3):
                output_use(1, k, *J.use(last_i, 1, r_uses + k), 3 * (2 * n_heads - 1))



class WindowJobs:

    def __init__(self, steps, q_uses, r_uses, m_uses, prologue_uses):
        self.steps, self.q, self.r, self.m = steps, q_uses, r_uses, m_uses
        self.per = q_uses + r_uses + m_uses
        self.pre = prologue_uses
        self.u0 = prologue_uses + q_uses + m_uses

    def first(self, i, b):
        return isinstance(i, int) and i == 0 and b == 0

    def use(self, i, b, k):
        fixed = self.u0 + self.per * b + k - (0 if self.first(i, b) else self.r)
        return i * (2 * self.per) + fixed, fixed % 2

    def job(self, i, b, each=1, plus=0):
        return i * (2 * each) + (each * b + plus)


def window_attention_stage(nc, per, name, kind, n_heads, dim, scale, w_o, *, heads=None, weights=None,
                    masks=None, x_init=True, windowed=False):
    small = kind == "small"
    rows = 2 * 2 * D8 if small else 2 * dim
    steps = 3 if windowed else QB
    q_uses = {"small": 0, "mqa": 2, "full": 5}[kind]
    m_uses = (QB if windowed else 2 * QB) + 1
    r_uses = 3
    pre_uses = 6 if kind == "mqa" else 0
    J = WindowJobs(steps, q_uses, r_uses, m_uses, pre_uses)
    OUT = C + 1
    last_i = n_heads - 1
    max_at = 64 if small else dim
    k_rows = max_at + 1 if small else P
    m_rows = max_at if small else P
    v_used = dim + 1
    v_width = 64 if small else dim + 1
    with Stage(nc, name) as st:
        keys = [st.sb(f"keys{b}", [k_rows, SEQ], F32R) for b in range(2)]
        queries = [st.sb(f"queries{b}", [k_rows, SEQ], F32R) for b in range(2)]
        if not small:
            keys_b = [st.sb(f"keys_b{b}", [dim + 1, SEQ], F32R) for b in range(2)]
            queries_b = [st.sb(f"queries_b{b}", [dim + 1, SEQ], F32R) for b in range(2)]
            w_qk = st.sb("w_qk", [P, 4, dim])
            w_v = st.sb("w_v", [P, dim])
        values = [st.sb(f"values{b}", [P, QB, v_width]) for b in range(2)]
        probs = [st.sb(f"probs{b}", [P, SEQ]) for b in range(2)]
        out_cols = [st.sb(f"out_cols{b}", [v_width, SEQ]) for b in range(2)]
        w_out = st.sb("w_out_heads", [v_width, n_heads * OUT])
        part_max = st.sb("part_max", [P, QB, 2])
        neg_max = st.sb("neg_max", [P, QB], F32R)
        max_rows = st.sb("max_rows", [QB, P])
        w_head = [st.sb(f"w_head{b}", [v_width, OUT]) for b in range(2)]
        recip = st.sb("recip", [P, 2, QB])
        work = st.ps("work", [P, 2, HALF])
        scores = st.ps("scores", [P, 2, SEQ])
        outs = st.ps("outs", [P, SEQ])
        if windowed:
            mask_in = st.sb("mask_in", [P, 3, SEQ])
            mask_t = st.sb("mask_t", [P, 3, SEQ], BF16)
            mask_q_in = st.sb("mask_q_in", [P, 2, 272])
            mask_q = st.sb("mask_q", [P, 2, 272], BF16)
            ident_b = st.sb("ident_b", [P, P], BF16)

        work_filled, work_drained = st.sem("work_filled"), st.sem("work_drained")
        scores_ready, exp_done = st.sem("scores_ready"), st.sem("exp_done")
        values_done, out_saved, acc_set = st.sem("values_done"), st.sem("out_saved"), st.sem("acc_set")
        split_done, recip_done = st.sem("split_done"), st.sem("recip_done")
        max_joined, max_loaded = st.sem("max_joined"), st.sem("max_loaded")
        operands_in, values_in, keys_b_ready = st.sem("operands_in"), st.sem("values_in"), st.sem("keys_b_ready")
        consts_in, consts_set, w_out_in = st.sem("consts_in"), st.sem("consts_set"), st.sem("w_out_in")
        masks_ready, w_head_ready = st.sem("masks_ready"), st.sem("w_head_ready")
        block = st.begin()

        def iterations(eng, body):
            body(0)
            if last_i > 1:
                with eng.Fori(1, last_i) as i:
                    body(i)
            body(last_i)

        def is_last(i, b):
            return isinstance(i, int) and i == last_i and b == 1

        def after(i, b):
            return (i, 1) if b == 0 else (i + 1, 0)

        def at_least(eng, sem, value):
            if not isinstance(value, int) or value > 0:
                eng.wait_ge(sem, value)

        N_OPERANDS = 2
        n_consts = 3 + 2 * (4 if small else 2)

        @block.sync
        def _(sp):
            if windowed:
                sp.dma_start(mask_in[:, :, :], masks[0]).then_inc(consts_in, 16)
                sp.dma_start(mask_q_in[:, :, :], masks[1]).then_inc(consts_in, 16)

            def operands(i, b):
                if small:
                    cols = slice(b * SEQ, (b + 1) * SEQ)
                    for dst, x in ((keys[b], "k"), (queries[b], "q")):
                        sp.dma_start(dst[0:rows, :].bitcast(F32),
                                     heads.stacks[x][span(i * rows, rows), cols]).then_inc(operands_in, 16)

            def maxima(i, b, use):
                sp.wait_ge(work_drained, use + 1)
                row = (queries if small else queries_b)[b][max_at:max_at + 1, :]
                sp.dma_start(row.bitcast(F32), max_rows[:, :]).then_inc(max_loaded, 16)

            operands(0, 0)
            maxima(0, 0, J.pre + J.q + J.m - 1)

            def slot(i, b):
                if is_last(i, b):
                    return
                ni, nb = after(i, b)
                if small:
                    at_least(sp, scores_ready, J.job(i, b, steps))
                    operands(ni, nb)
                m0 = J.q + (0 if J.first(i, b) else J.r)
                maxima(ni, nb, J.use(i, b, m0 + J.m - 1)[0])

            iterations(sp, lambda i: (slot(i, 0), slot(i, 1)))

        @block.gpsimd
        def _(pool):
            def head_projections(i):
                for k in range(2):
                    pool.dma_start(w_qk[:, k, :], weights[0](i)).then_inc(operands_in, 16)
                if kind == "full":
                    for k in range(2):
                        pool.dma_start(w_qk[:, 2 + k, :], weights[1](i)).then_inc(operands_in, 16)
                    pool.dma_start(w_v[:, :], weights[2](i)).then_inc(operands_in, 16)

            if kind == "mqa":
                for k in range(2):
                    pool.dma_start(w_qk[:, 2 + k, :], weights[1](0)).then_inc(consts_in, 16)
                pool.dma_start(w_v[:, :], weights[2](0)).then_inc(consts_in, 16)
            if not small:
                head_projections(0)
            wv = w_out[:, :].rearrange("p (h c) -> p h c", c=OUT)
            nc.gpsimd.memset(w_out[:, :], 0.0).then_inc(consts_set, 1)
            pool.wait_ge(consts_set, 1)
            nc.gpsimd.memset(wv[:, :, C:OUT], 1.0).then_inc(consts_set, 1)
            pool.wait_ge(consts_set, 2)
            nc.gpsimd.affine_select(out=wv[:, :, C:OUT], in_=wv[:, :, C:OUT], compare_op=ALU.is_equal, fill=0.0,
                                    base=-dim, pattern=[[0, n_heads], [0, 1]],
                                    channel_multiplier=1).then_inc(consts_set, 1)
            done = 3
            for b in range(2):
                fills = [((keys if small else keys_b)[b][max_at:max_at + 1, :].bitcast(F32), 1.0)]
                if small:
                    fills += [(x[rows:max_at, :].bitcast(F32), 0.0) for x in (keys[b], queries[b])]
                    fills += [(values[b][:, :, :], 0.0)]
                else:
                    fills += [(values[b][:, :, dim:dim + 1], 1.0)]
                for where, value in fills:
                    pool.wait_ge(consts_set, done)
                    nc.gpsimd.memset(where, value).then_inc(consts_set, 1)
                    done += 1
            assert done == n_consts
            pool.wait_ge(consts_set, n_consts)
            if small and windowed:
                for h in range(n_heads):
                    pool.dma_start(wv[0:dim, h, 0:C], w_o[h * dim:(h + 1) * dim, :]).then_inc(w_out_in, 16)
            else:
                pool.dma_start(wv[0:dim, :, 0:C], w_o).then_inc(w_out_in, 16)
            if x_init:
                nc.gpsimd.tensor_copy(per.acc[:, :, :], per.x_rows[:, :, :]).then_inc(acc_set, 1)
            else:
                nc.gpsimd.memset(per.acc[:, :, :], 0.0).then_inc(acc_set, 1)

            def following_projections(i):
                if isinstance(i, int) and i == last_i:
                    return
                pool.wait_ge(work_filled, J.use(i, 0, J.q - 1)[0] + 1)
                head_projections(i + 1)

            if not small:
                iterations(pool, following_projections)

        @block.tensor
        def _(pe):
            def fill(use):
                at_least(pe, work_drained, use - 1)

            def key_value_uses(b, u, k_only_from=0):
                for h in range(2):
                    fill(u + h)
                    nc.tensor.matmul(work[:, (u + h) % 2, :], w_qk[:, 2:4, :].rearrange("p a d -> p (a d)"),
                                     per.x_cols[:, b * SEQ + h * HALF:b * SEQ + (h + 1) * HALF],
                                     start=True, stop=True).then_inc(work_filled, 1)
                value_use(b, u + 2, (u + 2) % 2)

            def value_use(b, u, bank):
                fill(u)
                for t in range(QB):
                    last = nc.tensor.matmul(work[:, bank, t * dim:(t + 1) * dim],
                                            per.x_cols[:, b * SEQ + t * P:b * SEQ + (t + 1) * P], w_v[:, :],
                                            start=True, stop=True)
                last.then_inc(work_filled, 1)

            def project(b, use_of):
                if kind == "small":
                    return
                for k in range(2):
                    u, bank = use_of(k)
                    fill(u)
                    nc.tensor.matmul(work[:, bank, :], w_qk[:, 0:2, :].rearrange("p a d -> p (a d)"),
                                     per.x_cols[:, b * SEQ + k * HALF:b * SEQ + (k + 1) * HALF],
                                     start=True, stop=True).then_inc(work_filled, 1)
                if kind == "full":
                    for k in range(2):
                        u, bank = use_of(2 + k)
                        fill(u)
                        nc.tensor.matmul(work[:, bank, :], w_qk[:, 2:4, :].rearrange("p a d -> p (a d)"),
                                         per.x_cols[:, b * SEQ + k * HALF:b * SEQ + (k + 1) * HALF],
                                         start=True, stop=True).then_inc(work_filled, 1)
                    u, bank = use_of(4)
                    value_use(b, u, bank)

            def max_use(b, k, u, bank):
                fill(u)
                if windowed:
                    lo = 0 if k else P
                    nc.tensor.matmul(work[:, bank, lo:272], ident_b[:, :], mask_q[:, min(k, 1), lo:272],
                                     start=True, stop=False, skip_group_check=True)
                    q = queries[b][0:m_rows, k * P:(k + 1) * P]
                    nc.tensor.matmul(work[:, bank, lo:2 * P], q, keys[b][0:m_rows, max(k - 1, 0) * P:(k + 1) * P],
                                     start=False, stop=False, skip_group_check=True)
                    nc.tensor.matmul(work[:, bank, 2 * P:272], q, keys[b][0:m_rows, 0:PREFIX],
                                     start=False, stop=True, skip_group_check=True).then_inc(work_filled, 1)
                else:
                    q, h = k // 2, k % 2
                    nc.tensor.matmul(work[:, bank, :], queries[b][0:m_rows, q * P:(q + 1) * P],
                                     keys[b][0:m_rows, h * HALF:(h + 1) * HALF],
                                     start=True, stop=True).then_inc(work_filled, 1)

            def max_rows_use(u, bank, job_count):
                fill(u)
                pe.wait_ge(max_joined, job_count)
                nc.tensor.transpose(work[0:QB, bank, 0:P], neg_max[:, :].bitcast(F32),
                                    per.ident[:, :]).then_inc(work_filled, 1)

            def score_step(i, b, k):
                g = steps * b + k
                bank = g % 2
                at_least(pe, exp_done, J.job(i, b, steps, k - 1))
                if windowed:
                    last = window_scores(b, k, bank)
                else:
                    for h in range(2):
                        cols = slice(h * HALF, (h + 1) * HALF)
                        last = nc.tensor.matmul(scores[:, bank, cols], keys[b][:, k * P:(k + 1) * P],
                                                queries[b][:, cols], start=True, stop=small)
                        if not small:
                            last = nc.tensor.matmul(scores[:, bank, cols], keys_b[b][:, k * P:(k + 1) * P],
                                                    queries_b[b][:, cols], start=False, stop=True)
                last.then_inc(scores_ready, 1)

            def window_scores(b, k, bank):
                if k == 0:
                    for h in range(2):
                        cols = slice(h * HALF, (h + 1) * HALF)
                        nc.tensor.matmul(scores[0:PREFIX, bank, cols], ident_b[:, 0:PREFIX], mask_t[:, 0, cols],
                                         start=True, stop=False, skip_group_check=True)
                        last = nc.tensor.matmul(scores[0:PREFIX, bank, cols], keys[b][:, 0:PREFIX],
                                                queries[b][:, cols], start=False, stop=True, skip_group_check=True)
                    return last
                for h in range(2):
                    first = k - 1 if h == 0 else 0
                    cols = slice(h * HALF + first * P, (h + 1) * HALF)
                    nc.tensor.matmul(scores[:, bank, cols], ident_b[:, :], mask_t[:, k, cols],
                                     start=True, stop=False, skip_group_check=True)
                    for q in range(4 * h + first, 4 * h + 4):
                        kb = q - (k - 1)
                        last = nc.tensor.matmul(scores[:, bank, q * P:(q + 1) * P], keys[b][:, kb * P:(kb + 1) * P],
                                                queries[b][:, q * P:(q + 1) * P], start=False,
                                                stop=q == 4 * h + 3, skip_group_check=True)
                return last

            def value_step(i, b, k):
                pbuf = (steps * b + k) % 2
                pe.wait_ge(exp_done, J.job(i, b, steps, k + 1))
                if k == 0:
                    at_least(pe, out_saved, J.job(i, b))
                v = values[b]
                if windowed:
                    for h in range(2):
                        cols = slice(h * HALF, (h + 1) * HALF)
                        if k == 0:
                            last = nc.tensor.matmul(outs[0:v_width, cols], v[0:PREFIX, 0, :], probs[pbuf][0:PREFIX, cols],
                                                    start=True, stop=False, skip_group_check=True)
                            continue
                        for q in range(4 * h + (k - 1 if h == 0 else 0), 4 * h + 4):
                            last = nc.tensor.matmul(outs[0:v_width, q * P:(q + 1) * P], v[:, q - (k - 1), :],
                                                    probs[pbuf][:, q * P:(q + 1) * P], start=False,
                                                    stop=k == 2 and q == 4 * h + 3, skip_group_check=True)
                else:
                    for h in range(2):
                        cols = slice(h * HALF, (h + 1) * HALF)
                        last = nc.tensor.matmul(outs[0:v_width, cols], v[:, k, :], probs[pbuf][:, cols],
                                                start=k == 0, stop=k == steps - 1)
                last.then_inc(values_done, 1)

            def output_product(i, b, use_of):
                pe.wait_ge(out_saved, J.job(i, b, 1, 1))
                pe.wait_ge(w_head_ready, J.job(i, b, 1, 1))
                for k in range(3):
                    u, bank = use_of(k)
                    fill(u)
                    for j in range(3 * k, min(3 * k + 3, QB)):
                        last = nc.tensor.matmul(work[:, bank, (j - 3 * k) * OUT:(j - 3 * k + 1) * OUT],
                                                out_cols[b][:, j * P:(j + 1) * P], w_head[b][:, :], start=True, stop=True)
                    last.then_inc(work_filled, 1)

            pe.wait_ge(consts_set, n_consts)
            if small:
                pe.wait_ge(operands_in, 16 * N_OPERANDS)
            elif kind == "mqa":
                pe.wait_ge(consts_in, 16 * 3)
                for b in range(2):
                    key_value_uses(b, 3 * b)
                pe.wait_ge(operands_in, 16 * 2)
            else:
                pe.wait_ge(operands_in, 16 * 5)
            if windowed:
                pe.wait_ge(masks_ready, 3)
            project(0, lambda k: (J.pre + k, (J.pre + k) % 2))
            m_start = J.pre + J.q
            at_least(pe, work_drained, m_start)
            for k in range(J.m - 1):
                max_use(0, k, m_start + k, (m_start + k) % 2)
            max_rows_use(m_start + J.m - 1, (m_start + J.m - 1) % 2, 1)

            def slot(i, b):
                last_slot = is_last(i, b)
                first_slot = J.first(i, b)
                nq = 0 if last_slot else J.q
                ni, nb = after(i, b)
                pi, pb = (i, 0) if b else (i - 1, 1)
                m0 = J.q + (0 if first_slot else J.r)
                pe.wait_ge(max_loaded, J.job(i, b, 16, 16))
                if small:
                    pe.wait_ge(values_in, J.job(i, b, 1, 1))
                elif kind == "full":
                    pe.wait_ge(keys_b_ready, J.job(i, b, 1, 1))
                elif first_slot:
                    pe.wait_ge(keys_b_ready, 2)
                todo = list(range(J.m - 1))
                middle = max(steps - 3, 1)
                share = -(-len(todo) // middle)
                for k in range(steps):
                    score_step(i, b, k)
                    if k:
                        value_step(i, b, k - 1)
                    if k == 0 and not last_slot:
                        if small:
                            pe.wait_ge(operands_in, J.job(i, b, 16 * N_OPERANDS, 2 * 16 * N_OPERANDS))
                        elif nb == 0:
                            n_w = 2 if kind == "mqa" else 5
                            pe.wait_ge(operands_in, i * (16 * n_w) + 2 * 16 * n_w)
                        project(nb, lambda k: J.use(i, b, k))
                    if k == (0 if windowed else 1) and not first_slot:
                        output_product(pi, pb, lambda k: J.use(i, b, nq + k))
                    if not last_slot and ((windowed and k == 1) or (not windowed and 2 <= k < steps - 1)):
                        if todo and todo[0] == 0:
                            pe.wait_ge(work_drained, J.use(i, b, m0)[0])
                        for j in todo[:share]:
                            max_use(nb, j, *J.use(i, b, m0 + j))
                        todo = todo[share:]
                    if not last_slot and k == steps - 1:
                        max_rows_use(*J.use(i, b, m0 + J.m - 1), J.job(i, b, 1, 2))
                value_step(i, b, steps - 1)

            iterations(pe, lambda i: (slot(i, 0), slot(i, 1)))
            output_product(last_i, 1, lambda k: J.use(last_i, 1, J.r + k))

        @block.scalar
        def _(act):
            def save(i, b):
                act.wait_ge(values_done, J.job(i, b, steps, steps))
                nc.scalar.activation(out_cols[b][:, :], outs[0:v_width, :], ACT.Copy).then_inc(out_saved, 1)

            def high_keys(b, use):
                act.wait_ge(work_drained, use + 1)
                nc.scalar.activation(keys_b[b][0:dim, :], keys[b][0:dim, :].bitcast(F32),
                                     ACT.Copy).then_inc(keys_b_ready, 1)

            if kind == "mqa":
                for b in range(2):
                    high_keys(b, 3 * b + 1)
            if kind == "full":
                high_keys(0, J.pre + 3)

            def slot(i, b):
                for k in range(steps):
                    buf = (steps * b + k) % 2
                    act.wait_ge(scores_ready, J.job(i, b, steps, k + 1))
                    at_least(act, values_done, J.job(i, b, steps, k - 1))
                    if windowed and k == 0:
                        where = (slice(0, PREFIX), slice(0, SEQ))
                    elif windowed and k == 2:
                        where = (slice(0, P), slice(P, SEQ))
                    else:
                        where = (slice(0, P), slice(0, SEQ))
                    nc.scalar.activation(probs[buf][where[0], where[1]], scores[where[0], buf, where[1]],
                                         ACT.Exp, scale=scale).then_inc(exp_done, 1)
                    if k == 0 and not J.first(i, b):
                        save(*((i, 0) if b else (i - 1, 1)))
                    if k == 3 and kind == "full" and not is_last(i, b):
                        high_keys(1 - b, J.use(i, b, 3)[0])

            iterations(act, lambda i: (slot(i, 0), slot(i, 1)))
            save(last_i, 1)

        @block.vector
        def _(dve):
            if windowed:
                dve.wait_ge(consts_in, 32)
                nc.vector.tensor_copy(mask_t[:, :, :], mask_in[:, :, :]).then_inc(masks_ready, 1)
                nc.vector.tensor_copy(mask_q[:, :, :], mask_q_in[:, :, :]).then_inc(masks_ready, 1)
                nc.vector.tensor_copy(ident_b[:, :], per.ident[:, :]).then_inc(masks_ready, 1)

            splits = {"small": 0, "mqa": 2, "full": 4}[kind]
            pre_splits = 4 if kind == "mqa" else 0

            def split_query(b, h, u, bank, s):
                cols = slice(h * HALF, (h + 1) * HALF)
                dve.wait_ge(work_filled, u + 1)
                nc.vector.tensor_copy(queries[b][:, cols], work[:, bank, :]).then_inc(split_done, 1)
                dve.wait_ge(split_done, s + 1)
                nc.vector.tensor_tensor(queries_b[b][0:dim, cols], work[0:dim, bank, :],
                                        queries[b][0:dim, cols].bitcast(F32), ALU.subtract).then_inc(work_drained, 1)

            def split_key(b, h, u, bank, s):
                cols = slice(h * HALF, (h + 1) * HALF)
                dve.wait_ge(work_filled, u + 1)
                nc.vector.tensor_copy(keys[b][:, cols], work[:, bank, :]).then_inc(split_done, 1)
                dve.wait_ge(split_done, s + 1)
                nc.vector.tensor_tensor(keys[b][dim:2 * dim, cols], work[dim:2 * dim, bank, :],
                                        keys[b][dim:2 * dim, cols].bitcast(F32), ALU.subtract).then_inc(work_drained, 1)

            def copy_values(b, u, bank):
                dve.wait_ge(work_filled, u + 1)
                nc.vector.tensor_copy(values[b][:, :, 0:dim],
                                      work[:, bank, :].rearrange("p (t d) -> p t d", d=dim)).then_inc(work_drained, 1)

            def project(b, use_of, s0):
                if small:
                    return
                for k in range(2):
                    split_query(b, k, *use_of(k), s0 + k)
                if kind == "full":
                    for k in range(2):
                        split_key(b, k, *use_of(2 + k), s0 + 2 + k)
                    copy_values(b, *use_of(4))

            def max_use(k, u, bank):
                dve.wait_ge(work_filled, u + 1)
                if windowed:
                    nc.vector.tensor_reduce(part_max[:, k, 0:1], work[:, bank, (0 if k else P):272], AX.X,
                                            ALU.max).then_inc(work_drained, 1)
                else:
                    nc.vector.tensor_reduce(part_max[:, k // 2, k % 2:k % 2 + 1], work[:, bank, :], AX.X,
                                            ALU.max).then_inc(work_drained, 1)

            def join_max(u, bank, dma_value):
                dve.wait_ge(work_drained, u)
                if windowed:
                    nc.vector.tensor_scalar(neg_max[:, :], part_max[:, :, 0], -1.0, None,
                                            ALU.mult).then_inc(max_joined, 1)
                else:
                    nc.vector.tensor_reduce(neg_max[:, :], part_max[:, :, :], AX.X, ALU.max,
                                            negate=True).then_inc(max_joined, 1)
                dve.wait_ge(work_filled, u + 1)
                at_least(dve, max_loaded, dma_value)
                nc.vector.tensor_copy(max_rows[:, :], work[0:QB, bank, 0:P]).then_inc(work_drained, 1)

            def output_product(b, use_of, r0):
                for k in range(3):
                    u, bank = use_of(k)
                    n = min(3, QB - 3 * k)
                    dve.wait_ge(work_filled, u + 1)
                    at = work[:, bank, 0:n * OUT].rearrange("p (j c) -> p j c", c=OUT)
                    nc.vector.reciprocal(recip[:, b, 3 * k:3 * k + n], at[:, :, C]).then_inc(recip_done, 1)
                    dve.wait_ge(recip_done, r0 + k + 1)
                    for j in range(n):
                        t = b * QB + 3 * k + j
                        last = nc.vector.scalar_tensor_tensor(per.acc[:, t, :], at[:, j, 0:C],
                                                              recip[:, b, 3 * k + j:3 * k + j + 1], per.acc[:, t, :],
                                                              ALU.mult, ALU.add)
                    last.then_inc(work_drained, 1)

            def head_weights(i, b):
                nc.vector.tensor_scalar(w_head[b][:, :], w_out[:, span(i * OUT, OUT)], 1.0, None,
                                        ALU.mult).then_inc(w_head_ready, 1)

            def head_values(i, b):
                nc.vector.tensor_scalar(values[b][:, :, 0:v_used],
                                        heads.v_rows[:, b * QB:(b + 1) * QB, span(i * v_used, v_used)], 1.0, None,
                                        ALU.mult).then_inc(values_in, 1)

            dve.wait_ge(consts_set, n_consts)
            dve.wait_ge(w_out_in, 16 * n_heads if windowed else 16)
            if small:
                head_values(0, 0)
            if kind == "mqa":
                for b in range(2):
                    for h in range(2):
                        split_key(b, h, 3 * b + h, (3 * b + h) % 2, 2 * b + h)
                    copy_values(b, 3 * b + 2, (3 * b + 2) % 2)
            project(0, lambda k: (J.pre + k, (J.pre + k) % 2), pre_splits)
            m_start = J.pre + J.q
            for k in range(J.m - 1):
                max_use(k, m_start + k, (m_start + k) % 2)
            join_max(m_start + J.m - 1, (m_start + J.m - 1) % 2, 0)

            def slot(i, b):
                last_slot, first_slot = is_last(i, b), J.first(i, b)
                nq = 0 if last_slot else J.q
                ni, nb = after(i, b)
                m0 = J.q + (0 if first_slot else J.r)
                at_least(dve, values_done, J.job(i, b, steps))
                head_weights(i, b)
                if not last_slot:
                    if small:
                        head_values(ni, nb)
                    project(nb, lambda k: J.use(i, b, k), J.job(i, b, splits, splits + pre_splits))
                if not first_slot:
                    output_product(1 - b, lambda k: J.use(i, b, nq + k), J.job(i, b, 3, -3))
                if not last_slot:
                    for k in range(J.m - 1):
                        max_use(k, *J.use(i, b, m0 + k))
                    join_max(*J.use(i, b, m0 + J.m - 1), J.job(i, b, 16, 16))

            dve.wait_ge(acc_set, 1)
            iterations(dve, lambda i: (slot(i, 0), slot(i, 1)))
            output_product(1, lambda k: J.use(last_i, 1, J.r + k), 3 * (2 * n_heads - 1))



def layer0_ffn(nc, per, t):
    with Stage(nc, "L0_ffn") as st:
        w = st.sb("w", [C, C])
        a1 = st.sb("a1", [C, C])
        a2 = st.sb("a2", [C, C])
        b_row = st.sb("b_row", [1, C])
        w_t = st.sb("w_t", [C, C])
        a1_t = st.sb("a1_t", [C, C])
        a12 = st.sb("a12", [C, C])
        wa = st.sb("wa", [C, C])
        act_out = st.sb("act_out", [P, TILES, C])
        small_ps = st.ps("small_ps", [P, 4, HALF])
        out_ps = st.ps("out_ps", [P, CHUNKS, HALF])
        loaded = st.sem("loaded")
        product, copied = st.sem("product"), st.sem("copied")
        rows_done, tanh_done, added = st.sem("rows_done"), st.sem("tanh_done"), st.sem("added")
        block = st.begin()

        @block.sync
        def _(sp):
            for dst, name in ((w, "weight"), (a1, "aux_weight1"), (a2, "aux_weight2")):
                sp.dma_start(dst[:, :], t["L0_ffn_" + name]).then_inc(loaded, 16)
            sp.dma_start(b_row[:, :], t["L0_ffn_bias"].rearrange("(a c) -> a c", a=1)).then_inc(loaded, 16)

        @block.tensor
        def _(pe):
            pe.wait_ge(loaded, 64)
            nc.tensor.transpose(small_ps[:, 0, 0:C], w[:, :], per.ident[:, :]).then_inc(product, 1)
            nc.tensor.transpose(small_ps[:, 1, 0:C], a1[:, :], per.ident[:, :]).then_inc(product, 1)
            pe.wait_ge(copied, 2)
            nc.tensor.matmul(small_ps[:, 2, 0:C], a1_t[:, :], a2[:, :], start=True, stop=True).then_inc(product, 1)
            pe.wait_ge(copied, 3)
            nc.tensor.matmul(small_ps[:, 3, 0:C], w_t[:, :], a12[:, :], start=True, stop=True).then_inc(product, 1)
            pe.wait_ge(copied, 4)
            for k in range(TILES):
                cols = slice((k % 4) * C, (k % 4 + 1) * C)
                nc.tensor.matmul(out_ps[:, k // 4, cols], per.ones_row[:, :], b_row[:, :], start=True, stop=False)
                nc.tensor.matmul(out_ps[:, k // 4, cols], per.x_cols[:, k * P:(k + 1) * P], wa[:, :],
                                 start=False, stop=True).then_inc(rows_done, 1)

        @block.scalar
        def _(act):
            for k, dst in enumerate((w_t, a1_t, a12, wa)):
                act.wait_ge(product, k + 1)
                nc.scalar.activation(dst[:, :], small_ps[:, k, 0:C], ACT.Copy).then_inc(copied, 1)
            for c in range(CHUNKS):
                act.wait_ge(rows_done, 4 * c + 4)
                nc.scalar.activation(act_out[:, 4 * c:4 * c + 4, :],
                                     out_ps[:, c, :].rearrange("p (t c) -> p t c", c=C), ACT.Tanh).then_inc(tanh_done, 1)

        @block.vector
        def _(dve):
            for c in range(CHUNKS):
                dve.wait_ge(tanh_done, c + 1)
                part = slice(4 * c, 4 * c + 4)
                nc.vector.tensor_tensor(per.acc[:, part, :], per.x_rows[:, part, :], act_out[:, part, :],
                                        ALU.add).then_inc(added, 1)
    norm_stage(nc, per, "L0_norm1", per.acc, per.x_rows)


def one_hot_of_max(nc, dve, st, name, scores, n, one_hot, scratch, eq, top, rev, step, at):
    def wide(a):
        return a[:, :].unsqueeze(2).to_broadcast([P, TILES, n])
    nc.vector.tensor_reduce(top[:, :], scores[:, :, :], AX.X, ALU.max).then_inc(step, 1)
    dve.wait_ge(step, at + 1)
    nc.vector.tensor_tensor(eq[:, :, :], scores[:, :, :], wide(top), ALU.is_equal).then_inc(step, 1)
    dve.wait_ge(step, at + 2)
    nc.vector.tensor_tensor(eq[:, :, :], eq[:, :, :], rev[:, 0:n].unsqueeze(1).to_broadcast([P, TILES, n]),
                            ALU.mult).then_inc(step, 1)
    dve.wait_ge(step, at + 3)
    nc.vector.tensor_reduce(scratch[:, :], eq[:, :, :], AX.X, ALU.max).then_inc(step, 1)
    dve.wait_ge(step, at + 4)
    nc.vector.tensor_tensor(one_hot[:, :, :], eq[:, :, :], wide(scratch), ALU.is_equal).then_inc(step, 1)
    dve.wait_ge(step, at + 5)
    return at + 5


def layer1_ffn(nc, per, t):
    n_e = 32
    with ExitStack() as ctx:
        held = Held(nc, ctx, "L1_routed")
        pick = held.sb("pick", [P, TILES, n_e])
        scaled_cols = held.sb("scaled_cols", [C, TOKENS])
        with Stage(nc, "L1_router") as st:
            w = st.sb("w", [C, n_e])
            rev = st.sb("rev", [P, n_e])
            logits = st.sb("logits", [P, TILES, n_e])
            eq = st.sb("eq", [P, TILES, n_e])
            top = st.sb("top", [P, TILES])
            scratch = st.sb("scratch", [P, TILES])
            score = st.sb("score", [P, TILES])
            scaled = st.sb("scaled", [P, TILES, C])
            logit_ps = st.ps("logit_ps", [P, HALF])
            tr = st.ps("tr", [P, CHUNKS, HALF])
            loaded, logits_done, logits_ready = st.sem("loaded"), st.sem("logits_done"), st.sem("logits_ready")
            step, score_ready = st.sem("step"), st.sem("score_ready")
            scaled_ready, transposed, copied = st.sem("scaled_ready"), st.sem("transposed"), st.sem("copied")
            acc_set = st.sem("acc_set")
            block = st.begin()

            @block.sync
            def _(sp):
                sp.dma_start(w[:, :], t["L1_ffn_gate_w"]).then_inc(loaded, 16)
                sp.dma_start(rev[:, :], t["reversed"]).then_inc(loaded, 16)

            @block.tensor
            def _(pe):
                pe.wait_ge(loaded, 32)
                for k in range(TILES):
                    nc.tensor.matmul(logit_ps[:, k * n_e:(k + 1) * n_e], per.x_cols[:, k * P:(k + 1) * P], w[:, :],
                                     start=True, stop=True).then_inc(logits_done, 1)
                for k in range(TILES):
                    pe.wait_ge(scaled_ready, k + 1)
                    nc.tensor.transpose(tr[:, k // 4, (k % 4) * P:(k % 4 + 1) * P], scaled[:, k, :],
                                        per.ident[:, :]).then_inc(transposed, 1)

            @block.vector
            def _(dve):
                dve.wait_ge(loaded, 32)
                dve.wait_ge(logits_done, TILES)
                nc.vector.tensor_copy(logits[:, :, :], logit_ps[:, :].rearrange("p (t e) -> p t e", e=n_e)).then_inc(step, 1)
                dve.wait_ge(step, 1)
                one_hot_of_max(nc, dve, st, "top", logits, n_e, pick, scratch, eq, top, rev, step, 1)
                dve.wait_ge(score_ready, 1)
                for k in range(TILES):
                    nc.vector.tensor_scalar(scaled[:, k, :], per.x_rows[:, k, :], score[:, k:k + 1], None,
                                            ALU.mult).then_inc(scaled_ready, 1)

            @block.gpsimd
            def _(pool):
                nc.gpsimd.tensor_copy(per.acc[:, :, :], per.x_rows[:, :, :]).then_inc(acc_set, 1)

            @block.scalar
            def _(act):
                act.wait_ge(step, 2)
                nc.scalar.activation(score[:, :], top[:, :], ACT.Sigmoid).then_inc(score_ready, 1)
                for c in range(CHUNKS):
                    act.wait_ge(transposed, 4 * c + 4)
                    nc.scalar.activation(scaled_cols[:, c * HALF:(c + 1) * HALF], tr[:, c, :],
                                         ACT.Copy).then_inc(copied, 1)
        shared = [t["L1_ffn_shared_" + n] for n in ("gate_w", "up_w", "down_w")]
        experts_stage(nc, per, "L1_shared", 1, per.x_cols, None,
                      lambda e: (shared[0], shared[1]), lambda e: shared[2], flip=False)
        routed = [t["L1_ffn_routed_" + n].rearrange("e a b -> (e a) b") for n in ("gate_w", "up_w", "down_w")]
        experts_stage(nc, per, "L1_experts", n_e, scaled_cols, pick,
                      lambda e: (routed[0][span(e * C, C), :], routed[1][span(e * C, C), :]),
                      lambda e: routed[2][span(e * 2 * C, 2 * C), :], flip=False)
    norm_stage(nc, per, "L1_norm1", per.acc, per.x_rows)


def layer2_ffn(nc, per, t):
    n_e = 8
    with ExitStack() as ctx:
        held = Held(nc, ctx, "L2_routed")
        share = held.sb("share", [P, TILES, n_e])
        with Stage(nc, "L2_router") as st:
            w = st.sb("w", [n_e, C])
            w_t = st.sb("w_t", [C, n_e])
            rev = st.sb("rev", [P, 32])
            logits = st.sb("logits", [P, TILES, n_e])
            rest = st.sb("rest", [P, TILES, n_e])
            eq = st.sb("eq", [P, TILES, n_e])
            pick1 = st.sb("pick1", [P, TILES, n_e])
            pick2 = st.sb("pick2", [P, TILES, n_e])
            top1 = st.sb("top1", [P, TILES])
            top2 = st.sb("top2", [P, TILES])
            scratch = st.sb("scratch", [P, TILES])
            gap = st.sb("gap", [P, TILES])
            e2 = st.sb("e2", [P, TILES])
            p1 = st.sb("p1", [P, TILES])
            p2 = st.sb("p2", [P, TILES])
            ps = st.ps("ps", [P, 2, HALF])
            loaded, flipped, w_ready = st.sem("loaded"), st.sem("flipped"), st.sem("w_ready")
            logits_done, step, exp_ready = st.sem("logits_done"), st.sem("step"), st.sem("exp_ready")
            gap_ready, acc_set = st.sem("gap_ready"), st.sem("acc_set")
            block = st.begin()

            @block.sync
            def _(sp):
                sp.dma_start(w[:, :], t["L2_ffn_gate_w"]).then_inc(loaded, 16)
                sp.dma_start(rev[:, :], t["reversed"]).then_inc(loaded, 16)

            @block.gpsimd
            def _(pool):
                nc.gpsimd.tensor_copy(per.acc[:, :, :], per.x_rows[:, :, :]).then_inc(acc_set, 1)

            @block.tensor
            def _(pe):
                pe.wait_ge(loaded, 32)
                nc.tensor.transpose(ps[:, 0, 0:n_e], w[:, :], per.ident[0:n_e, 0:n_e]).then_inc(flipped, 1)
                pe.wait_ge(w_ready, 1)
                for k in range(TILES):
                    nc.tensor.matmul(ps[:, 1, k * n_e:(k + 1) * n_e], per.x_cols[:, k * P:(k + 1) * P], w_t[:, :],
                                     start=True, stop=True).then_inc(logits_done, 1)

            @block.scalar
            def _(act):
                act.wait_ge(flipped, 1)
                nc.scalar.activation(w_t[:, :], ps[:, 0, 0:n_e], ACT.Copy).then_inc(w_ready, 1)
                act.wait_ge(gap_ready, 1)
                nc.scalar.activation(e2[:, :], gap[:, :], ACT.Exp).then_inc(exp_ready, 1)

            @block.vector
            def _(dve):
                def wide(a):
                    return a[:, :].unsqueeze(2).to_broadcast([P, TILES, n_e])
                dve.wait_ge(loaded, 32)
                dve.wait_ge(logits_done, TILES)
                nc.vector.tensor_copy(logits[:, :, :],
                                      ps[:, 1, 0:TILES * n_e].rearrange("p (t e) -> p t e", e=n_e)).then_inc(step, 1)
                dve.wait_ge(step, 1)
                n = one_hot_of_max(nc, dve, st, "top1", logits, n_e, pick1, scratch, eq, top1, rev, step, 1)
                nc.vector.scalar_tensor_tensor(rest[:, :, :], pick1[:, :, :], -3.0e38, logits[:, :, :],
                                               ALU.mult, ALU.add).then_inc(step, 1)
                dve.wait_ge(step, n + 1)
                n = one_hot_of_max(nc, dve, st, "top2", rest, n_e, pick2, scratch, eq, top2, rev, step, n + 1)
                nc.vector.tensor_tensor(gap[:, :], top2[:, :], top1[:, :], ALU.subtract).then_inc(gap_ready, 1)
                dve.wait_ge(exp_ready, 1)
                nc.vector.tensor_scalar(p1[:, :], e2[:, :], 1.0, None, ALU.add).then_inc(step, 1)
                dve.wait_ge(step, n + 1)
                nc.vector.reciprocal(p1[:, :], p1[:, :]).then_inc(step, 1)
                dve.wait_ge(step, n + 2)
                nc.vector.tensor_tensor(p2[:, :], e2[:, :], p1[:, :], ALU.mult).then_inc(step, 1)
                dve.wait_ge(step, n + 3)
                nc.vector.tensor_tensor(pick1[:, :, :], pick1[:, :, :], wide(p1), ALU.mult).then_inc(step, 1)
                nc.vector.tensor_tensor(pick2[:, :, :], pick2[:, :, :], wide(p2), ALU.mult).then_inc(step, 1)
                dve.wait_ge(step, n + 5)
                nc.vector.tensor_tensor(share[:, :, :], pick1[:, :, :], pick2[:, :, :], ALU.add).then_inc(step, 1)
        w12 = t["L2_ffn_w12"].rearrange("e h d -> (e h) d")
        w3 = t["L2_ffn_w3"].rearrange("e d h -> (e d) h")
        experts_stage(nc, per, "L2_experts", n_e, per.x_cols, share,
                      lambda e: (w12[span(e * 4 * C, 4 * C), :],), lambda e: w3[span(e * C, C), :], flip=True)
    norm_stage(nc, per, "L2_norm1", per.acc, per.x_rows)


def experts_stage(nc, per, name, n_e, cols_in, share, w_up, w_down, flip):
    IN = 2 * C
    with Stage(nc, name) as st:
        up = [st.sb(f"up{k}", [C, 2 * IN]) for k in range(2)]
        down = [st.sb(f"down{k}", [P, 2, C]) for k in range(2)]
        if flip:
            up_raw = st.sb("up_raw", [P, 4, C])
            down_raw = st.sb("down_raw", [C, IN])
        gated = st.sb("gated", [P, 2, HALF])
        hidden = [st.sb(f"hidden{k}", [P, 2, HALF]) for k in range(2)]
        mine = [st.sb(f"mine{k}", [P, TILES]) for k in range(2)]
        pair_ps = st.ps("pair_ps", [P, 2, 2, HALF])
        rows_ps = st.ps("rows_ps", [P, 2, HALF])
        flip_ps = st.ps("flip_ps", [P, 2, HALF])
        w_in = [st.sem(f"w_in{k}") for k in range(2)]
        w_ready, flipped = st.sem("w_ready"), st.sem("flipped")
        pair_done, silu_done, hidden_ready = st.sem("pair_done"), st.sem("silu_done"), st.sem("hidden_ready")
        rows_done, rows_added, mine_ready = st.sem("rows_done"), st.sem("rows_added"), st.sem("mine_ready")
        n_w = 2 if flip else 3
        block = st.begin()

        def experts(eng, body):
            body(0)
            if n_e > 4:
                with eng.Fori(1, n_e // 2 - 1) as i:
                    body(i)
            if n_e > 2:
                body(n_e // 2 - 1)

        pair = range(min(n_e, 2))

        def at(i, k, each, plus=0):
            return i * (2 * each) + (each * k + plus)

        def at_least(eng, sem, value):
            if not isinstance(value, int) or value > 0:
                eng.wait_ge(sem, value)

        @block.gpsimd
        def _(pool):
            def load(i, k):
                if flip:
                    at_least(pool, flipped, at(i, k, 1))
                else:
                    at_least(pool, rows_done, at(i, k, 4, -4))
                e = i * 2 + k
                if flip:
                    pool.dma_start(up_raw[:, :, :], w_up(e)[0].rearrange("(a p) d -> p a d", p=P)).then_inc(w_in[k], 16)
                    pool.dma_start(down_raw[:, :], w_down(e)).then_inc(w_in[k], 16)
                else:
                    for g in range(2):
                        pool.dma_start(up[k][:, g * IN:(g + 1) * IN], w_up(e)[g]).then_inc(w_in[k], 16)
                    pool.dma_start(down[k][:, :, :], w_down(e).rearrange("(a p) c -> p a c", p=P)).then_inc(w_in[k], 16)

            experts(pool, lambda i: [load(i, k) for k in pair])

        @block.tensor
        def _(pe):
            def rows_of(i, k, c):
                s = 4 * k + c
                pe.wait_ge(hidden_ready, at(i, k, 8, 2 * c + 2))
                at_least(pe, rows_added, at(i, k, 4, c - 1))
                for j in range(4):
                    for h in range(2):
                        last = nc.tensor.matmul(rows_ps[:, s % 2, j * C:(j + 1) * C],
                                                hidden[s % 2][:, h, j * P:(j + 1) * P], down[k][:, h, :],
                                                start=h == 0, stop=h == 1)
                last.then_inc(rows_done, 1)

            def step(i, k):
                if flip:
                    pe.wait_ge(w_in[k], i * (16 * n_w) + 16 * n_w)
                    at_least(pe, w_ready, at(i, k, 2))
                    for a in range(4):
                        nc.tensor.transpose(flip_ps[:, 0, a * P:(a + 1) * P], up_raw[:, a, :], per.ident[:, :])
                    for a in range(2):
                        last = nc.tensor.transpose(flip_ps[:, 1, a * P:(a + 1) * P], down_raw[:, a * P:(a + 1) * P],
                                                   per.ident[:, :])
                    last.then_inc(flipped, 1)
                    pe.wait_ge(w_ready, at(i, k, 2, 2))
                else:
                    pe.wait_ge(w_in[k], i * (16 * n_w) + 16 * n_w)
                for c in range(CHUNKS):
                    for h in range(2):
                        n = 8 * k + 2 * c + h
                        at_least(pe, hidden_ready, at(i, k, 8, 2 * c + h - 1))
                        for g in range(2):
                            last = nc.tensor.matmul(pair_ps[:, n % 2, g, :], up[k][:, g * IN + h * P:g * IN + (h + 1) * P],
                                                    cols_in[:, c * HALF:(c + 1) * HALF], start=True, stop=True)
                        last.then_inc(pair_done, 1)
                    if c:
                        rows_of(i, k, c - 1)
                    elif k:
                        rows_of(i, 0, CHUNKS - 1)
                    elif not (isinstance(i, int) and i == 0):
                        rows_of(i - 1, 1, CHUNKS - 1)

            experts(pe, lambda i: [step(i, k) for k in pair])
            rows_of((n_e - 1) // 2, (n_e - 1) % 2, CHUNKS - 1)

        @block.scalar
        def _(act):
            def copies(i, k):
                act.wait_ge(flipped, at(i, k, 1, 1))
                at_least(act, rows_done, at(i, k, 4, -4))
                nc.scalar.activation(up[k][:, :], flip_ps[:, 0, :], ACT.Copy).then_inc(w_ready, 1)
                nc.scalar.activation(down[k][:, :, :], flip_ps[:, 1, 0:IN].rearrange("p (a c) -> p a c", c=C),
                                     ACT.Copy).then_inc(w_ready, 1)

            def step(i, k):
                if flip:
                    copies(i, k)
                for n in range(8):
                    act.wait_ge(pair_done, at(i, k, 8, n + 1))
                    at_least(act, hidden_ready, at(i, k, 8, n - 1))
                    nc.scalar.activation(gated[:, n % 2, :], pair_ps[:, n % 2, 0, :], ACT.Silu).then_inc(silu_done, 1)

            experts(act, lambda i: [step(i, k) for k in pair])

        @block.vector
        def _(dve):
            def my_share(i, k):
                if share is not None:
                    src = share[:, :, span(i * 2 + k, 1)].rearrange("p t a -> p (t a)")
                    nc.vector.tensor_scalar(mine[k][:, :], src, 1.0, None, ALU.mult).then_inc(mine_ready, 1)

            def add_rows(i, k, c):
                s = 4 * k + c
                dve.wait_ge(rows_done, at(i, k, 4, c + 1))
                if share is not None:
                    dve.wait_ge(mine_ready, at(i, k, 1, 1))
                at_least(dve, rows_added, at(i, k, 4, c))
                for j in range(4):
                    tile = 4 * c + j
                    psum = rows_ps[:, s % 2, j * C:(j + 1) * C]
                    if share is not None:
                        last = nc.vector.scalar_tensor_tensor(per.acc[:, tile, :], psum, mine[k][:, tile:tile + 1],
                                                              per.acc[:, tile, :], ALU.mult, ALU.add)
                    else:
                        last = nc.vector.tensor_tensor(per.acc[:, tile, :], psum, per.acc[:, tile, :], ALU.add)
                last.then_inc(rows_added, 1)

            def step(i, k):
                for c in range(CHUNKS):
                    for h in range(2):
                        n = 2 * c + h
                        dve.wait_ge(silu_done, at(i, k, 8, n + 1))
                        at_least(dve, rows_done, at(i, k, 4, c - 1))
                        nc.vector.tensor_tensor(hidden[c % 2][:, h, :], pair_ps[:, n % 2, 1, :], gated[:, n % 2, :],
                                                ALU.mult).then_inc(hidden_ready, 1)
                    if c:
                        add_rows(i, k, c - 1)
                    elif k:
                        add_rows(i, 0, CHUNKS - 1)
                    elif not (isinstance(i, int) and i == 0):
                        add_rows(i - 1, 1, CHUNKS - 1)
                    if c == 0:
                        my_share(i, k)

            experts(dve, lambda i: [step(i, k) for k in pair])
            add_rows((n_e - 1) // 2, (n_e - 1) % 2, CHUNKS - 1)


def layer3_ffn(nc, per, t):
    HID = 4 * C
    HB = HID // P
    with ExitStack() as ctx:
        held = Held(nc, ctx, "L3_held")
        w_t = {n: held.sb(n, [P, k, m]) for n, k, m in
               (("w1", 1, HID), ("w2", 1, HID), ("h1", HB, HID), ("h2", HB, HID), ("w3", HB, C))}
        s_cols = held.sb("s_cols", [P, 4, HB])
        s3_bc = held.sb("s3_bc", [P, C])
        with Stage(nc, "L3_weights") as st:
            raw = {n: st.sb(n + "_raw", [P, k, m]) for n, k, m in
                   (("w1", HB, C), ("w2", HB, C), ("h1", HB, HID), ("h2", HB, HID), ("w3", 1, HID))}
            tr = st.ps("tr", [P, 4, HALF])
            loaded = {n: st.sem("loaded_" + n) for n in raw}
            scales_in, flipped, copied = st.sem("scales_in"), st.sem("flipped"), st.sem("copied")
            groups = []
            for n in ("w1", "w2"):
                groups.append((n, [(o, 0) for o in range(HB)], w_t[n][:, 0, :]))
            for n in ("h1", "h2"):
                groups += [(n, [(o, i) for o in range(HB)], w_t[n][:, i, :]) for i in range(HB)]
            groups.append(("w3", [(0, i) for i in range(HB)], w_t["w3"][:, :, :].rearrange("p k m -> p (k m)")))
            block = st.begin()

            @block.sync
            def _(sp):
                for n, r in raw.items():
                    sp.dma_start(r[:, :, :], t[f"L3_ffn_{n}_w"].rearrange("(a p) i -> p a i", p=P)).then_inc(loaded[n], 16)

            @block.gpsimd
            def _(pool):
                for k, n in enumerate(("w1", "w2", "h1", "h2")):
                    pool.dma_start(s_cols[:, k, :], t[f"L3_ffn_{n}_s"].rearrange("(a p) -> p a", p=P),
                                   allow_slow_non_contiguous=True).then_inc(scales_in, 16)
                pool.dma_start(s3_bc[:, :], t["L3_ffn_w3_s"].rearrange("(a c) -> a c", a=1).partition_broadcast(P)
                               .rearrange("p a c -> p (a c)")).then_inc(scales_in, 16)
                pool.wait_ge(scales_in, 80)

            @block.tensor
            def _(pe):
                for g, (n, blocks, _) in enumerate(groups):
                    pe.wait_ge(loaded[n], 16)
                    if g >= 4:
                        pe.wait_ge(copied, g - 3)
                    for j, (o, i) in enumerate(blocks):
                        last = nc.tensor.transpose(tr[:, g % 4, j * P:(j + 1) * P], raw[n][:, o, i * P:(i + 1) * P],
                                                   per.ident[:, :])
                    last.then_inc(flipped, 1)

            @block.scalar
            def _(act):
                for g, (_, _, place) in enumerate(groups):
                    act.wait_ge(flipped, g + 1)
                    nc.scalar.activation(place, tr[:, g % 4, :], ACT.Copy).then_inc(copied, 1)

        with Stage(nc, "L3_ffn") as st:
            h_a = st.sb("h_a", [P, HB, TOKENS])
            h_b = st.sb("h_b", [P, HB, TOKENS])
            gated = st.sb("gated", [P, 2, HALF])
            scaled = st.sb("scaled", [P, 2, HALF])
            bank = st.ps("bank", [P, 8, HALF])
            filled, gate_done, made = st.sem("filled"), st.sem("gate_done"), st.sem("made")
            gelu_done, scaled_ready, added = st.sem("gelu_done"), st.sem("scaled_ready"), st.sem("added")
            N1 = CHUNKS * HB
            block = st.begin()

            @block.tensor
            def _(pe):
                def cols(c):
                    return slice(c * HALF, (c + 1) * HALF)
                for n in range(N1):
                    c, o = divmod(n, HB)
                    if n >= 4:
                        pe.wait_ge(made, n - 3)
                    for g, w in enumerate(("w1", "w2")):
                        last = nc.tensor.matmul(bank[:, 2 * (n % 4) + g, :], w_t[w][:, 0, o * P:(o + 1) * P],
                                                per.x_cols[:, cols(c)], start=True, stop=True)
                    last.then_inc(filled, 1)
                for layer, (w, src) in enumerate((("h1", h_a), ("h2", h_b))):
                    for n in range(N1):
                        c, o = divmod(n, HB)
                        m = layer * N1 + n
                        if layer == 0:
                            pe.wait_ge(made, HB * (c + 1) if m >= 8 else N1)
                        else:
                            pe.wait_ge(gelu_done, HB * (c + 1))
                        if m >= 8:
                            pe.wait_ge(gelu_done, m - 7)
                        for i in range(HB):
                            last = nc.tensor.matmul(bank[:, m % 8, :], w_t[w][:, i, o * P:(o + 1) * P],
                                                    src[:, i, cols(c)], start=i == 0, stop=i == HB - 1)
                        last.then_inc(filled, 1)
                for c in range(CHUNKS):
                    pe.wait_ge(gelu_done, N1 + HB * (c + 1))
                    if c == 0:
                        pe.wait_ge(gelu_done, 2 * N1)
                    for j in range(4):
                        for i in range(HB):
                            last = nc.tensor.matmul(bank[:, c, j * C:(j + 1) * C],
                                                    h_a[:, i, c * HALF + j * P:c * HALF + (j + 1) * P],
                                                    w_t["w3"][:, i, :], start=i == 0, stop=i == HB - 1)
                    last.then_inc(filled, 1)

            @block.scalar
            def _(act):
                for n in range(N1):
                    c, o = divmod(n, HB)
                    act.wait_ge(filled, n + 1)
                    if n >= 2:
                        act.wait_ge(made, n - 1)
                    nc.scalar.activation(gated[:, n % 2, :], bank[:, 2 * (n % 4), :], ACT.Silu,
                                         scale=s_cols[:, 0, o:o + 1]).then_inc(gate_done, 1)
                for layer, dst in enumerate((h_b, h_a)):
                    for n in range(N1):
                        c, o = divmod(n, HB)
                        m = layer * N1 + n
                        act.wait_ge(filled, N1 + m + 1)
                        nc.scalar.activation(dst[:, o, c * HALF:(c + 1) * HALF], bank[:, m % 8, :], ACT.Gelu,
                                             scale=s_cols[:, 2 + layer, o:o + 1]).then_inc(gelu_done, 1)

            @block.vector
            def _(dve):
                for n in range(N1):
                    c, o = divmod(n, HB)
                    dve.wait_ge(gate_done, n + 1)
                    nc.vector.scalar_tensor_tensor(h_a[:, o, c * HALF:(c + 1) * HALF], bank[:, 2 * (n % 4) + 1, :],
                                                   s_cols[:, 1, o:o + 1], gated[:, n % 2, :],
                                                   ALU.mult, ALU.mult).then_inc(made, 1)
                for c in range(CHUNKS):
                    dve.wait_ge(filled, 3 * N1 + c + 1)
                    if c >= 2:
                        dve.wait_ge(added, c - 1)
                    tiles = slice(4 * c, 4 * c + 4)
                    nc.vector.tensor_tensor(scaled[:, c % 2, :].rearrange("p (t c) -> p t c", c=C),
                                            bank[:, c, :].rearrange("p (t c) -> p t c", c=C),
                                            s3_bc[:, :].unsqueeze(1).to_broadcast([P, 4, C]), ALU.mult).then_inc(scaled_ready, 1)
                    dve.wait_ge(scaled_ready, c + 1)
                    nc.vector.tensor_tensor(per.acc[:, tiles, :], scaled[:, c % 2, :].rearrange("p (t c) -> p t c", c=C),
                                            per.x_rows[:, tiles, :], ALU.add).then_inc(added, 1)
    norm_stage(nc, per, "L3_norm1", per.acc, per.x_rows, to_cols=False)



def build_network(nc, t, out, upto=8, start=0):
    with ExitStack() as ctx:
        per = Persistent(nc, ctx)
        load_stage(nc, per, t["L0_attn_x"], t["ident"])
        parts = [
            lambda: layer0_attention(nc, per, t),
            lambda: layer0_ffn(nc, per, t),
            lambda: layer1_attention(nc, per, t),
            lambda: layer1_ffn(nc, per, t),
            lambda: layer2_attention(nc, per, t),
            lambda: layer2_ffn(nc, per, t),
            lambda: layer3_attention(nc, per, t),
            lambda: layer3_ffn(nc, per, t),
        ]
        for part in parts[start:upto]:
            part()
        store_stage(nc, per, out)


def layer0_attention(nc, per, t):
    with ExitStack() as ctx:
        heads = SmallHeads(nc, Held(nc, ctx, "L0"))
        small_qkv_stage(nc, per, "L0_qkv", heads, t["L0_attn_W_qkv"], None, t["L0_attn_b_qkv"],
                        (t["rotation"], t["cos"], t["sin"]))
        attention_stage(nc, per, "L0_attn", "small", H8, D8, D8 ** -0.5,
                        t["L0_attn_W_out"].rearrange("(h d) o -> d h o", d=D8), heads=heads)
    norm_stage(nc, per, "L0_norm0", per.acc, per.x_rows, bias=t["L0_attn_b_out"])


def layer1_attention(nc, per, t):
    with ExitStack() as ctx:
        heads = SmallHeads(nc, Held(nc, ctx, "L1"))
        small_qkv_stage(nc, per, "L1_qkv", heads, t["L1_attn_w_qkv"], t["L1_attn_w_out"], None, None)
        window_attention_stage(nc, per, "L1_attn", "small", H8, D8, D8 ** -0.5, heads.w_out, heads=heads,
                        masks=(t["mask_t"], t["mask_q"]), windowed=True)
    norm_stage(nc, per, "L1_norm0", per.acc, per.x_rows)


def layer2_attention(nc, per, t):
    w_q, w_kv = t["L2_attn_Wq"], t["L2_attn_Wkv"]
    norm_stage(nc, per, "L2_norm_in", per.x_rows, per.acc, affine=(t["L2_attn_norm_w"], t["L2_attn_norm_b"]))
    attention_stage(nc, per, "L2_attn", "mqa", 8, 64, 64 ** -0.5,
                    t["L2_attn_Wo"].rearrange("(h d) o -> d h o", d=64),
                    weights=(lambda i: w_q[:, span(i * 64, 64)], lambda i: w_kv[:, 0:64],
                             lambda i: w_kv[:, 64:128]), x_init=False)
    norm_stage(nc, per, "L2_norm_out", per.acc, per.acc, affine=(t["L2_attn_out_norm_w"], t["L2_attn_out_norm_b"]),
               plus=per.x_rows, to_cols=False)
    norm_stage(nc, per, "L2_norm0", per.acc, per.x_rows)


def layer3_attention(nc, per, t):
    w = [t[f"L3_attn_W{n}"].rearrange("h d e -> (h d) e") for n in "qkv"]
    attention_stage(nc, per, "L3_attn", "full", 16, 64, 64 ** -0.5,
                    t["L3_attn_Wp"].rearrange("(e h) o -> e h o", h=16),
                    weights=[lambda i, m=m: m[span(i * C, C), :] for m in w])
    norm_stage(nc, per, "L3_norm0", per.acc, per.x_rows, bias=t["L3_attn_bp"])


class Held:

    def __init__(self, nc, ctx, name):
        self.nc, self.ctx, self.name = nc, ctx, name

    def sb(self, name, shape, dt=F32):
        return self.ctx.enter_context(self.nc.sbuf_tensor(f"{self.name}_{name}", shape, dt))


def constants():
    d = np.arange(P)
    rotation = np.zeros((P, P), np.float32)
    for o in range(P):
        h, r = divmod(o, D8)
        if r < D8 // 2:
            rotation[h * D8 + r + D8 // 2, o] = -1.0
        else:
            rotation[h * D8 + r - D8 // 2, o] = 1.0
    inv = (np.float32(1.0) / np.power(np.float32(10000.0), np.arange(0, D8, 2, dtype=np.float32) / np.float32(D8))
           ).astype(np.float32)
    angle = (np.arange(SEQ, dtype=np.float32)[None, :] * inv[d % (D8 // 2)][:, None]).astype(np.float32)
    p, q = np.arange(P)[:, None], np.arange(P)[None, :]
    own = (p <= q) & (q - p < WINDOW)
    before = q + P - p < WINDOW
    ok = np.zeros((P, 3, SEQ), bool)
    for j in range(QB):
        cols = slice(j * P, (j + 1) * P)
        ok[:, 0, cols] = (p <= q) if j == 0 else True
        ok[:, 1, cols] = own & ((p >= PREFIX) | (j > 0))
        ok[:, 2, cols] = before
    mask_t = np.where(ok, 0.0, MASKED).astype(np.float32)
    ok_q = np.zeros((P, 2, 2 * P + PREFIX), bool)
    for j in range(2):
        ok_q[:, j, 0:P] = before.T
        ok_q[:, j, P:2 * P] = ok[:, 1, j * P:(j + 1) * P].T
        ok_q[:, j, 2 * P:] = ok[0:PREFIX, 0, j * P:(j + 1) * P].T
    mask_q = np.where(ok_q, 0.0, MASKED).astype(np.float32)
    return {"ident": np.eye(P, dtype=np.float32), "rotation": rotation,
            "cos": np.cos(angle).astype(np.float32), "sin": np.sin(angle).astype(np.float32),
            "mask_t": mask_t, "mask_q": mask_q,
            "reversed": np.tile(np.arange(32, 0, -1, dtype=np.float32), (P, 1))}


def kernel(**inputs):
    import concourse.bacc as bacc
    from concourse.bass_utils import run_bass_kernel_spmd

    nc = bacc.Bacc("TRN2", target_bir_lowering=False, num_devices=1)
    arrays, t = {}, {}
    for name, a in {**inputs, **constants()}.items():
        arrays[name] = np.ascontiguousarray(a)
        t[name] = nc.dram_tensor(name, arrays[name].shape, mybir.dt.from_np(arrays[name].dtype),
                                 kind="ExternalInput").ap()
    out = nc.dram_tensor("out", (BATCH, SEQ, C), F32, kind="ExternalOutput").ap()
    build_network(nc, t, out)
    return run_bass_kernel_spmd(nc, [arrays], core_ids=[0]).results[0]["out"]
```

```python
import numpy as np
from contextlib import ExitStack

import concourse.bass as bass
from concourse import mybir

F32 = mybir.dt.float32
F32R = mybir.dt.float32r
I32 = mybir.dt.int32
ALU = mybir.AluOpType
ACT = mybir.ActivationFunctionType
AX = mybir.AxisListType

P = 128
BATCH = 2
SEQ = 1024
C = 128
TOKENS = BATCH * SEQ
TILES = TOKENS // P
QB = SEQ // P
HALF = 512
CHUNKS = TOKENS // HALF
EPS = 1e-5
MASKED = -1e9
WINDOW = 64
PREFIX = 16


class Stage:

    def __init__(self, nc, name):
        self.nc, self.name = nc, name
        self.ctx, self.sems = ExitStack(), []

    def __enter__(self):
        return self

    def sb(self, name, shape, dt=F32):
        return self.ctx.enter_context(self.nc.sbuf_tensor(f"{self.name}_{name}", shape, dt))

    def ps(self, name, shape):
        return self.ctx.enter_context(self.nc.psum_tensor(f"{self.name}_{name}", shape, F32))

    def sem(self, name):
        self.sems.append(self.nc.alloc_semaphore(f"{self.name}_{name}"))
        return self.sems[-1]

    def begin(self):
        self.guard = self.nc.Block()
        return self.guard.__enter__()

    def __exit__(self, *e):
        if e[0] is not None:
            return False
        self.guard.__exit__(None, None, None)
        self.nc.clear_and_free_semaphores(self.sems)
        self.nc.all_engine_barrier()
        self.ctx.close()
        return False


class Persistent:

    def __init__(self, nc, ctx):
        def sb(name, shape, dt=F32):
            return ctx.enter_context(nc.sbuf_tensor(name, shape, dt))
        self.x_rows = sb("x_rows", [P, TILES, C])
        self.x_cols = sb("x_cols", [C, TOKENS])
        self.acc = sb("acc", [P, TILES, C])
        self.ident = sb("identity", [P, P])
        self.ones_row = sb("ones_row", [1, P])


def span(start, n):
    return slice(start, start + n) if isinstance(start, int) else bass.ds(start, n)


def tile_bcast(row_bc):
    return row_bc[:, :].unsqueeze(1).to_broadcast([P, TILES, C])



def load_stage(nc, per, x, ident):
    with Stage(nc, "load") as st:
        tr = st.ps("tr", [P, CHUNKS, HALF])
        x_in, id_in = st.sem("x_in"), st.sem("id_in")
        transposed, ones_set, copied = st.sem("transposed"), st.sem("ones_set"), st.sem("copied")
        block = st.begin()

        @block.sync
        def _(sp):
            sp.dma_start(per.ident[:, :], ident).then_inc(id_in, 16)
            xv = x.rearrange("b (q p) c -> p (b q) c", p=P)
            sp.dma_start(per.x_rows[:, :, :], xv).then_inc(x_in, 16)

        @block.vector
        def _(dve):
            nc.vector.memset(per.ones_row[:, :], 1.0).then_inc(ones_set, 1)

        @block.tensor
        def _(pe):
            pe.wait_ge(id_in, 16)
            pe.wait_ge(x_in, 16)
            for t in range(TILES):
                nc.tensor.transpose(tr[:, t // 4, (t % 4) * P:(t % 4 + 1) * P], per.x_rows[:, t, :],
                                    per.ident[:, :]).then_inc(transposed, 1)

        @block.scalar
        def _(act):
            for c in range(CHUNKS):
                act.wait_ge(transposed, 4 * c + 4)
                nc.scalar.activation(per.x_cols[:, c * HALF:(c + 1) * HALF], tr[:, c, :],
                                     ACT.Copy).then_inc(copied, 1)


def norm_stage(nc, per, name, src, dst, bias=None, affine=None, plus=None, to_cols=True):
    with Stage(nc, name) as st:
        stats = st.sb("stats", [P, TILES, 6])
        moments = st.sb("moments", [P, TILES, 2])
        var = st.sb("var", [P, TILES])
        power = st.sb("power", [P, TILES])
        rstd = st.sb("rstd", [P, TILES])
        rows_bc = st.sb("rows_bc", [P, 3, C])
        tr = st.ps("tr", [P, CHUNKS, HALF])
        rows_in = st.sem("rows_in")
        biased, stats_done = st.sem("biased"), st.sem("stats_done")
        moments_ready, rstd_ready = st.sem("moments_ready"), st.sem("rstd_ready")
        var_ready, power_set = st.sem("var_ready"), st.sem("power_set")
        normed, scaled = st.sem("normed"), st.sem("scaled")
        transposed, copied = st.sem("transposed"), st.sem("copied")
        block = st.begin()
        rows = [r for r in ([bias] if bias is not None else []) + list(affine or [])]

        @block.sync
        def _(sp):
            for k, r in enumerate(rows):
                sp.dma_start(rows_bc[:, k, :],
                             r.rearrange("(a c) -> a c", a=1).partition_broadcast(P)
                             .rearrange("p a c -> p (a c)")).then_inc(rows_in, 16)

        @block.vector
        def _(dve):
            if rows:
                dve.wait_ge(rows_in, 16 * len(rows))
            if bias is not None:
                nc.vector.tensor_tensor(src[:, :, :], src[:, :, :], tile_bcast(rows_bc[:, 0, :]),
                                        ALU.add).then_inc(biased, 1)
                dve.wait_ge(biased, 1)
            for t in range(TILES):
                nc.vector.bn_stats(stats[:, t, :], src[:, t, :]).then_inc(stats_done, 1)
            for t in range(TILES):
                dve.wait_ge(stats_done, t + 1)
                nc.vector.bn_aggr(moments[:, t, :], stats[:, t, :]).then_inc(moments_ready, 1)
            dve.wait_ge(moments_ready, TILES)
            nc.vector.tensor_scalar(var[:, :], moments[:, :, 1], EPS, None, ALU.add).then_inc(var_ready, 1)
            dve.wait_ge(rstd_ready, 1)
            for t in range(TILES):
                nc.vector.tensor_scalar(dst[:, t, :], src[:, t, :], moments[:, t, 0:1],
                                        rstd[:, t:t + 1], ALU.subtract, ALU.mult).then_inc(normed, 1)
            if affine is not None:
                k = len(rows) - 2
                dve.wait_ge(normed, TILES)
                nc.vector.tensor_tensor(dst[:, :, :], dst[:, :, :], tile_bcast(rows_bc[:, k, :]),
                                        ALU.mult).then_inc(scaled, 1)
                dve.wait_ge(scaled, 1)
                nc.vector.tensor_tensor(dst[:, :, :], dst[:, :, :], tile_bcast(rows_bc[:, k + 1, :]),
                                        ALU.add).then_inc(scaled, 1)
                if plus is not None:
                    dve.wait_ge(scaled, 2)
                    nc.vector.tensor_tensor(dst[:, :, :], dst[:, :, :], plus[:, :, :],
                                            ALU.add).then_inc(scaled, 1)

        @block.gpsimd
        def _(pool):
            nc.gpsimd.memset(power[:, :], -0.5).then_inc(power_set, 1)
            pool.wait_ge(power_set, 1)
            pool.wait_ge(var_ready, 1)
            nc.gpsimd.tensor_tensor(rstd[:, :], var[:, :], power[:, :], ALU.pow).then_inc(rstd_ready, 1)

        if to_cols:
            @block.tensor
            def _(pe):
                if affine is not None:
                    pe.wait_ge(scaled, 2)
                for t in range(TILES):
                    pe.wait_ge(normed, t + 1)
                    nc.tensor.transpose(tr[:, t // 4, (t % 4) * P:(t % 4 + 1) * P], dst[:, t, :],
                                        per.ident[:, :]).then_inc(transposed, 1)

            @block.scalar
            def _(act):
                for c in range(CHUNKS):
                    act.wait_ge(transposed, 4 * c + 4)
                    nc.scalar.activation(per.x_cols[:, c * HALF:(c + 1) * HALF], tr[:, c, :],
                                         ACT.Copy).then_inc(copied, 1)


def store_stage(nc, per, out):
    with Stage(nc, "store") as st:
        stored = st.sem("stored")
        block = st.begin()

        @block.sync
        def _(sp):
            sp.dma_start(out.rearrange("b (q p) c -> p (b q) c", p=P),
                         per.x_rows[:, :, :]).then_inc(stored, 16)
            sp.wait_ge(stored, 16)



D8 = 8
H8 = 16


class SmallHeads:

    def __init__(self, nc, st):
        self.stacks = {x: nc.dram_tensor(f"{st.name}_stack_{x}", (BATCH * H8 * 4 * D8, SEQ), F32).ap() for x in "qk"}
        self.v_rows = st.sb("v_rows", [P, TILES, H8 * (D8 + 1)])
        self.w_out = st.sb("w_out_flipped", [C, C])


def small_qkv_stage(nc, per, name, heads, w_in, w_out, bias, rope):
    w_transposed = w_out is not None
    with Stage(nc, name) as st:
        w_raw = st.sb("w_raw", [P, 4, P])
        w = st.sb("w", [P, 3, P])
        acc_ps = st.ps("acc_ps", [P, 4, HALF])
        rot_ps = st.ps("rot_ps", [P, 4, HALF])
        parts = {n: st.sb(n, [P, TOKENS], F32R) for n in ("qh", "ql", "kh", "kl")}
        flat = st.sb("flat", [P, 2, HALF])
        t_cos = st.sb("t_cos", [P, 2, HALF])
        t_sin = st.sb("t_sin", [P, 2, HALF])
        roped = st.sb("roped", [P, 2, HALF])
        b_cols = st.sb("b_cols", [P, 2])
        b_row = st.sb("b_row", [1, C])
        rot = st.sb("rot", [P, P])
        cos = st.sb("cos", [P, SEQ])
        sin = st.sb("sin", [P, SEQ])
        loaded, w_flipped, w_ready = st.sem("loaded"), st.sem("w_flipped"), st.sem("w_ready")
        proj_done, flat_ready, rot_done = st.sem("proj_done"), st.sem("flat_ready"), st.sem("rot_done")
        cos_done, sin_done, roped_ready = st.sem("cos_done"), st.sem("sin_done"), st.sem("roped_ready")
        high_ready, low_ready, stacked = st.sem("high_ready"), st.sem("low_ready"), st.sem("stacked")
        v_done, v_copied, ones_set = st.sem("v_done"), st.sem("v_copied"), st.sem("ones_set")
        n_loads = 1 + w_transposed + (3 if bias is not None else 0) + (3 if rope is not None else 0)
        steps = [(x, c) for x in range(2) for c in range(CHUNKS)]
        stacked_act = st.sem("stacked_act")
        block = st.begin()

        def send_parts(eng, n, blocks, signal):
            x, c = steps[n]
            cols = slice(c * HALF, (c + 1) * HALF)
            at = slice((c % 2) * HALF, (c % 2 + 1) * HALF)
            stack = heads.stacks["qk"[x]].rearrange("(b h r d) t -> b h r d t", b=BATCH, r=4, d=D8)[c // 2]
            eng.wait_ge(low_ready, n + 1)
            for r in blocks:
                part = ("hhll", "hlhl")[x][r]
                eng.dma_start(stack[:, r, :, at], parts["qk"[x] + part][:, cols].bitcast(F32)).then_inc(signal, 16)

        @block.sync
        def _(sp):
            if w_transposed:
                sp.dma_start(w_raw[:, 0:3, :], w_in.rearrange("(a o) i -> o a i", a=3)).then_inc(loaded, 16)
                sp.dma_start(w_raw[:, 3, :], w_out).then_inc(loaded, 16)
            else:
                sp.dma_start(w[:, :, :], w_in.rearrange("i (a o) -> i a o", a=3)).then_inc(loaded, 16)
            if bias is not None:
                for x in range(2):
                    sp.dma_start(b_cols[:, x:x + 1],
                                 bias[x * C:(x + 1) * C].rearrange("(p a) -> p a", a=1)).then_inc(loaded, 16)
                sp.dma_start(b_row[:, :], bias[2 * C:3 * C].rearrange("(a c) -> a c", a=1)).then_inc(loaded, 16)
            if rope is not None:
                for dst, src in zip((rot, cos, sin), rope):
                    sp.dma_start(dst[:, :], src).then_inc(loaded, 16)
            for n in range(len(steps)):
                send_parts(sp, n, (0, 1), stacked)
            sp.wait_ge(stacked, 16 * 2 * len(steps))

        @block.tensor
        def _(pe):
            pe.wait_ge(loaded, 16 * n_loads)
            if w_transposed:
                for a in range(4):
                    nc.tensor.transpose(acc_ps[:, 0, a * P:(a + 1) * P], w_raw[:, a, :],
                                        per.ident[:, :]).then_inc(w_flipped, 1)
                pe.wait_ge(w_ready, 2)

            def rotate(n):
                pe.wait_ge(flat_ready, n + 1)
                if n >= 4:
                    pe.wait_ge(sin_done, n - 3)
                nc.tensor.matmul(rot_ps[:, n % 4, :], rot[:, :], flat[:, n % 2, :],
                                 start=True, stop=True).then_inc(rot_done, 1)

            for n, (x, c) in enumerate(steps):
                if n >= 4:
                    pe.wait_ge(flat_ready if rope is not None else low_ready, n - 3)
                nc.tensor.matmul(acc_ps[:, n % 4, :], w[:, x, :], per.x_cols[:, c * HALF:(c + 1) * HALF],
                                 start=True, stop=True).then_inc(proj_done, 1)
                if rope is not None and n >= 1:
                    rotate(n - 1)
            if rope is not None:
                rotate(len(steps) - 1)
            pe.wait_ge(flat_ready if rope is not None else low_ready, len(steps))
            for t in range(TILES):
                if bias is not None:
                    nc.tensor.matmul(acc_ps[:, t // 4, (t % 4) * P:(t % 4 + 1) * P], per.ones_row[:, :],
                                     b_row[:, :], start=True, stop=False)
                nc.tensor.matmul(acc_ps[:, t // 4, (t % 4) * P:(t % 4 + 1) * P],
                                 per.x_cols[:, t * P:(t + 1) * P], w[:, 2, :],
                                 start=bias is None, stop=True).then_inc(v_done, 1)

        @block.scalar
        def _(act):
            if w_transposed:
                act.wait_ge(w_flipped, 4)
                nc.scalar.activation(heads.w_out[:, :], acc_ps[:, 0, 3 * P:4 * P], ACT.Copy).then_inc(w_ready, 1)
                nc.scalar.activation(w[:, :, :], acc_ps[:, 0, 0:3 * P].rearrange("p (a o) -> p a o", a=3),
                                     ACT.Copy).then_inc(w_ready, 1)
            LAG = 3
            if rope is not None:
                for n, (x, c) in enumerate(steps):
                    act.wait_ge(proj_done, n + 1)
                    if n >= 2:
                        act.wait_ge(rot_done, n - 1)
                        act.wait_ge(cos_done, n - 1)
                    nc.scalar.activation(flat[:, n % 2, :], acc_ps[:, n % 4, :], ACT.Identity,
                                         bias=b_cols[:, x:x + 1]).then_inc(flat_ready, 1)
                    if n >= LAG:
                        send_parts(act, n - LAG, (2, 3), stacked_act)
            for n in range(len(steps) - LAG if rope is not None else 0, len(steps)):
                send_parts(act, n, (2, 3), stacked_act)
            act.wait_ge(ones_set, 1)
            for c in range(CHUNKS):
                act.wait_ge(v_done, 4 * c + 4)
                nc.scalar.activation(
                    heads.v_rows[:, 4 * c:4 * c + 4, :].rearrange("p t (h d) -> p t h d", d=D8 + 1)[:, :, :, 0:D8],
                    acc_ps[:, c, :].rearrange("p (t h d) -> p t h d", t=4, d=D8), ACT.Copy).then_inc(v_copied, 1)
            act.wait_ge(stacked_act, 16 * 2 * len(steps))

        @block.gpsimd
        def _(pool):
            nc.gpsimd.memset(heads.v_rows[:, :, :], 1.0).then_inc(ones_set, 1)
            if rope is not None:
                for n, (x, c) in enumerate(steps):
                    pool.wait_ge(flat_ready, n + 1)
                    if n >= 2:
                        pool.wait_ge(roped_ready, n - 1)
                    at = (c % 2) * HALF
                    nc.gpsimd.tensor_tensor(t_cos[:, n % 2, :], flat[:, n % 2, :], cos[:, at:at + HALF],
                                            ALU.mult).then_inc(cos_done, 1)

        @block.vector
        def _(dve):
            for n, (x, c) in enumerate(steps):
                high, low = [parts["qk"[x] + s][:, c * HALF:(c + 1) * HALF] for s in "hl"]
                if rope is not None:
                    at = (c % 2) * HALF
                    dve.wait_ge(rot_done, n + 1)
                    nc.vector.tensor_tensor(t_sin[:, n % 2, :], rot_ps[:, n % 4, :], sin[:, at:at + HALF],
                                            ALU.mult).then_inc(sin_done, 1)
                    dve.wait_ge(sin_done, n + 1)
                    dve.wait_ge(cos_done, n + 1)
                    nc.vector.tensor_tensor(roped[:, n % 2, :], t_cos[:, n % 2, :], t_sin[:, n % 2, :],
                                            ALU.add).then_inc(roped_ready, 1)
                    dve.wait_ge(roped_ready, n + 1)
                    value = roped[:, n % 2, :]
                else:
                    dve.wait_ge(proj_done, n + 1)
                    value = acc_ps[:, n % 4, :]
                nc.vector.tensor_copy(high, value).then_inc(high_ready, 1)
                dve.wait_ge(high_ready, n + 1)
                nc.vector.tensor_tensor(low, value, high.bitcast(F32), ALU.subtract).then_inc(low_ready, 1)



class Jobs:

    def __init__(self, next_uses, out_uses, prologue_uses):
        self.r = out_uses
        self.per = next_uses + out_uses
        self.u0 = prologue_uses + next_uses

    def first(self, i, b):
        return isinstance(i, int) and i == 0 and b == 0

    def use(self, i, b, k):
        fixed = self.u0 + self.per * b + k - (0 if self.first(i, b) else self.r)
        return i * (2 * self.per) + fixed, fixed % 2

    def job(self, i, b, each=1, plus=0):
        return i * (2 * each) + (each * b + plus)


def attention_stage(nc, per, name, kind, n_heads, dim, scale, w_o, *, heads=None, weights=None, x_init=True):
    small = kind == "small"
    full = kind == "full"
    rows = 2 * 2 * D8 if small else 2 * dim
    steps = QB
    v_width = 32 if small else dim
    group = P // v_width
    n_parts = group
    PART = SEQ // n_parts
    units = steps
    pre_uses = 6 if kind == "mqa" else 0
    half_maxima = [("max", k) for k in range(2 * QB)]
    plan = [("pair" if full else "query", h) for h in range(0 if small else 2)]
    n_split = len(plan)
    plan += half_maxima[:QB] + [("values", 0)] * full + half_maxima[QB:]
    values_place = n_split + (QB if full else 12)
    places = 3 * steps
    rows_place = places - (4 if small else 3)
    FIRST_MAX, LAST_MAX = {"small": (0, 19), "mqa": (4, 20), "full": (6, 20)}[kind]

    def place_of(n):
        if n < n_split:
            return n
        return FIRST_MAX + -(-(n - n_split + 1) * (LAST_MAX - FIRST_MAX) // (len(plan) - n_split)) - 1
    r_uses = 3
    J = Jobs(len(plan) + 1, r_uses, pre_uses)
    OUT = C + 1
    last_i = n_heads - 1
    max_at = 64 if small else dim
    k_rows = max_at + 1 if small else P
    v_used = dim + 1
    with Stage(nc, name) as st:
        keys = [st.sb(f"keys{b}", [k_rows, SEQ], F32R) for b in range(2)]
        queries = [st.sb(f"queries{b}", [k_rows, SEQ], F32R) for b in range(2)]
        if small:
            keys_m = [st.sb(f"keys_m{b}", [max_at, SEQ], F32R) for b in range(2)]
            queries_m = [st.sb(f"queries_m{b}", [max_at, SEQ], F32R) for b in range(2)]
        else:
            keys_m, queries_m = keys, queries
            keys_b = [st.sb(f"keys_b{b}", [dim + 1, SEQ], F32R) for b in range(2)]
            queries_b = [st.sb(f"queries_b{b}", [dim + 1, SEQ], F32R) for b in range(2)]
            w_qk = st.sb("w_qk", [P, 4, dim])
            w_v = st.sb("w_v", [P, dim])
            prob_sum = [st.sb(f"prob_sum{b}", [P, SEQ]) for b in range(2)]
            ones_col = st.sb("ones_col", [P, 1])
        values = [st.sb(f"values{b}", [P, QB, v_width]) for b in range(2)]
        probs = st.sb("probs", [P, steps, SEQ])
        out_cols = [st.sb(f"out_cols{b}", [P, SEQ]) for b in range(2)]
        w_out = st.sb("w_out_heads", [P, n_heads * OUT])
        part_max = st.sb("part_max", [P, QB, 2])
        neg_max = st.sb("neg_max", [P, QB], F32R)
        max_rows = st.sb("max_rows", [QB, P])
        w_head = [st.sb(f"w_head{b}", [P, OUT]) for b in range(2)]
        recip = st.sb("recip", [P, 2, QB])
        work = st.ps("work", [P, 2, HALF])
        scores = st.ps("scores", [P, 2, SEQ])
        outs = st.ps("outs", [P, SEQ])

        work_filled, work_drained = st.sem("work_filled"), st.sem("work_drained")
        scores_ready, exp_done = st.sem("scores_ready"), st.sem("exp_done")
        values_done, out_saved, acc_set = st.sem("values_done"), st.sem("out_saved"), st.sem("acc_set")
        rounded, recip_done = st.sem("rounded"), st.sem("recip_done")
        max_joined, max_loaded = st.sem("max_joined"), st.sem("max_loaded")
        operands_in = [st.sem(f"operands_in{b}") for b in range(2)]
        max_operands_in = [st.sem(f"max_operands_in{b}") for b in range(2)]
        weights_in, probs_added = st.sem("weights_in"), st.sem("probs_added")
        values_in, keys_b_ready, queries_ready = st.sem("values_in"), st.sem("keys_b_ready"), st.sem("queries_ready")
        consts_in, consts_set, w_out_in = st.sem("consts_in"), st.sem("consts_set"), st.sem("w_out_in")
        w_head_ready, rows_cleared = st.sem("w_head_ready"), st.sem("rows_cleared")
        block = st.begin()

        def iterations(eng, body):
            body(0)
            with eng.Fori(1, last_i) as i:
                body(i)
            body(last_i)

        def is_last(i, b):
            return isinstance(i, int) and i == last_i and b == 1

        def after(i, b):
            return (i, 1) if b == 0 else (i + 1, 0)

        def before(i, b):
            return (i, 0) if b else (i - 1, 1)

        def at_least(eng, sem, value):
            if not isinstance(value, int) or value > 0:
                eng.wait_ge(sem, value)

        first_unit_step = group + 1 if small else group

        def unit_at(t):
            u = t - first_unit_step
            return divmod(u, n_parts) if 0 <= u < units else None

        save_steps = (0, 1) if group == 2 else (3, 5)
        n_weights = {"small": 0, "mqa": 2, "full": 3}[kind]
        n_consts = (group if small else 1) + 2 + 2 * (2 if small else 1)

        @block.sync
        def _(sp):
            def stacked(i, b, to_keys, to_queries, signal):
                for dst, x in ((to_keys, "k"), (to_queries, "q")):
                    sp.dma_start(dst[0:rows, :].bitcast(F32),
                                 heads.stacks[x][span(i * rows + b * (H8 * rows), rows), :]).then_inc(signal, 16)

            def operands(i, b):
                stacked(i, b, keys[b], queries[b], operands_in[b])

            def max_operands(i, b):
                stacked(i, b, keys_m[b], queries_m[b], max_operands_in[b])

            def head_projections(i):
                for k in range(2):
                    sp.dma_start(w_qk[:, k, :], weights[k if full else 0](i)).then_inc(weights_in, 16)
                if full:
                    sp.dma_start(w_v[:, :], weights[2](i)).then_inc(weights_in, 16)

            def maxima(b, use):
                sp.wait_ge(work_drained, use + 1)
                row = (queries if small else queries_b)[b][max_at:max_at + 1, :]
                sp.dma_start(row.bitcast(F32), max_rows[:, :]).then_inc(max_loaded, 16)

            if small:
                max_operands(0, 0)
                operands(0, 0)
                max_operands(0, 1)
            else:
                if kind == "mqa":
                    for k in range(2):
                        sp.dma_start(w_qk[:, 2 + k, :], weights[1](0)).then_inc(consts_in, 16)
                    sp.dma_start(w_v[:, :], weights[2](0)).then_inc(consts_in, 16)
                head_projections(0)
            maxima(0, J.u0 - 1)

            def slot(i, b):
                if is_last(i, b):
                    return
                ni, nb = after(i, b)
                if small:
                    at_least(sp, scores_ready, J.job(i, b, steps))
                    operands(ni, nb)
                    if not (isinstance(i, int) and i == last_i):
                        sp.wait_ge(work_filled, J.use(i, b, 0)[0])
                        max_operands(i + 1, b)
                elif b == 0 and not (isinstance(i, int) and i == last_i):
                    last_use = plan.index(("values", 0)) if full else n_split - 1
                    sp.wait_ge(work_filled, J.use(i, b, last_use)[0] + 1)
                    head_projections(i + 1)
                maxima(nb, J.use(i, b, len(plan))[0])

            iterations(sp, lambda i: (slot(i, 0), slot(i, 1)))

        @block.gpsimd
        def _(pool):
            wv = w_out[:, :].rearrange("p (h c) -> p h c", c=OUT)
            done = 0

            def filled(op):
                nonlocal done
                op.then_inc(consts_set, 1)
                done += 1
                pool.wait_ge(consts_set, done)

            filled(nc.gpsimd.memset(w_out[:, :], 0.0))
            filled(nc.gpsimd.memset(wv[:, :, C:OUT], 1.0 if small else 0.0))
            if small:
                for j in range(group):
                    part = wv[j * v_width:(j + 1) * v_width, :, C:OUT]
                    filled(nc.gpsimd.affine_select(out=part, in_=part, compare_op=ALU.is_equal, fill=0.0,
                                                   base=-dim, pattern=[[0, n_heads], [0, 1]], channel_multiplier=1))
            else:
                filled(nc.gpsimd.memset(ones_col[:, :], 1.0))
            for b in range(2):
                filled(nc.gpsimd.memset((keys if small else keys_b)[b][max_at:max_at + 1, :].bitcast(F32), 1.0))
                if small:
                    filled(nc.gpsimd.memset(values[b][:, :, :], 0.0))
            assert done == n_consts
            for j in range(group):
                pool.dma_start(wv[j * v_width:j * v_width + dim, :, 0:C], w_o).then_inc(w_out_in, 16)
            if x_init:
                nc.gpsimd.tensor_copy(per.acc[:, :, :], per.x_rows[:, :, :]).then_inc(acc_set, 1)
            else:
                nc.gpsimd.memset(per.acc[:, :, :], 0.0).then_inc(acc_set, 1)

            def slot(i, b):
                pool.wait_ge(work_filled, J.use(i, b, 0)[0])
                for k in range(1, steps):
                    pool.wait_ge(exp_done, J.job(i, b, steps, k + 1))
                    at_least(pool, probs_added, J.job(i, b, steps - 1, k - 1))
                    nc.gpsimd.tensor_tensor(prob_sum[b][:, :], probs[:, 0, :] if k == 1 else prob_sum[b][:, :],
                                            probs[:, k, :], ALU.add).then_inc(probs_added, 1)

            if not small:
                iterations(pool, lambda i: (slot(i, 0), slot(i, 1)))

        @block.tensor
        def _(pe):
            def fill(use):
                at_least(pe, work_drained, use - 1)

            def project(b, h, w, bank):
                nc.tensor.matmul(work[:, bank, :], w_qk[:, w:w + 2, :].rearrange("p a d -> p (a d)"),
                                 per.x_cols[:, b * SEQ + h * HALF:b * SEQ + (h + 1) * HALF],
                                 start=True, stop=True).then_inc(work_filled, 1)

            def project_values(b, bank):
                for t in range(QB):
                    last = nc.tensor.matmul(work[:, bank, t * dim:(t + 1) * dim],
                                            per.x_cols[:, b * SEQ + t * P:b * SEQ + (t + 1) * P], w_v[:, :],
                                            start=True, stop=True)
                last.then_inc(work_filled, 1)

            def next_job_use(b, n, u, bank, job_count):
                what, k = plan[n]
                if full and (what, k) == ("max", 0):
                    pe.wait_ge(queries_ready, job_count)
                if what in ("query", "pair"):
                    fill(u)
                    project(b, k, 0, bank)
                elif what == "values":
                    fill(u)
                    project_values(b, bank)
                else:
                    at_least(pe, work_drained, u if k == 0 and n_split else u - 1)
                    q, h = divmod(k, 2)
                    nc.tensor.matmul(work[:, bank, :], queries_m[b][0:(max_at if small else P), q * P:(q + 1) * P],
                                     keys_m[b][0:(max_at if small else P), h * HALF:(h + 1) * HALF],
                                     start=True, stop=True).then_inc(work_filled, 1)

            def max_rows_use(u, bank, job_count):
                fill(u)
                pe.wait_ge(max_joined, job_count)
                nc.tensor.transpose(work[0:QB, bank, 0:P], neg_max[:, :].bitcast(F32),
                                    per.ident[:, :]).then_inc(work_filled, 1)

            def half_scores(i, b, k, h):
                bank = k % 2
                cols = slice(h * HALF, (h + 1) * HALF)
                if h == 0:
                    at_least(pe, exp_done, J.job(i, b, steps, k - 1))
                last = nc.tensor.matmul(scores[:, bank, cols], keys[b][:, k * P:(k + 1) * P],
                                        queries[b][:, cols], start=True, stop=small)
                if not small:
                    last = nc.tensor.matmul(scores[:, bank, cols], keys_b[b][:, k * P:(k + 1) * P],
                                            queries_b[b][:, cols], start=False, stop=True)
                if h:
                    last.then_inc(scores_ready, 1)

            def value_unit(i, b, g, c):
                pe.wait_ge(exp_done, J.job(i, b, steps, group * (g + 1)))
                h, opens = c * 2 // n_parts, c % (n_parts // 2) == 0
                if g == 0 and opens:
                    at_least(pe, out_saved, J.job(i, b, 2, h - 1))
                    if small and h == 0:
                        pe.wait_ge(values_in, J.job(i, b, 1, 1))
                cols = slice(c * PART, (c + 1) * PART)
                for j in range(group):
                    last = nc.tensor.matmul(outs[j * v_width:(j + 1) * v_width, cols], values[b][:, group * g + j, :],
                                            probs[:, group * g + j, cols], start=g == 0 and opens,
                                            stop=group * (g + 1) == steps, skip_group_check=True)
                last.then_inc(values_done, 1)

            def output_use(i, b, k, u, bank):
                if k == 0:
                    pe.wait_ge(out_saved, J.job(i, b, 2, 2))
                    pe.wait_ge(w_head_ready, J.job(i, b, 1, 1))
                    if not small:
                        pe.wait_ge(probs_added, J.job(i, b, steps - 1, steps - 1))
                fill(u)
                wide = OUT if small else C
                for n, j in enumerate(range(3 * k, min(3 * k + 3, QB))):
                    last = nc.tensor.matmul(work[:, bank, n * OUT:n * OUT + wide], out_cols[b][:, j * P:(j + 1) * P],
                                            w_head[b][:, 0:wide], start=True, stop=True)
                    if not small:
                        last = nc.tensor.matmul(work[:, bank, n * OUT + C:(n + 1) * OUT],
                                                prob_sum[b][:, j * P:(j + 1) * P], ones_col[:, :],
                                                start=True, stop=True)
                last.then_inc(work_filled, 1)

            pe.wait_ge(consts_set, n_consts)
            if small:
                pe.wait_ge(rows_cleared, 8)
                pe.wait_ge(max_operands_in[0], 32)
            elif kind == "mqa":
                pe.wait_ge(consts_in, 16 * 3)
                for b in range(2):
                    for h in range(2):
                        fill(3 * b + h)
                        project(b, h, 2, (3 * b + h) % 2)
                    fill(3 * b + 2)
                    project_values(b, (3 * b + 2) % 2)
            if not small:
                pe.wait_ge(weights_in, 16 * n_weights)
            for n in range(len(plan)):
                next_job_use(0, n, pre_uses + n, (pre_uses + n) % 2, 1)
            max_rows_use(J.u0 - 1, (J.u0 - 1) % 2, 1)

            def slot(i, b):
                last_slot, first_slot = is_last(i, b), J.first(i, b)
                ni, nb = after(i, b)
                r0 = 0 if last_slot else len(plan) + 1

                def between(place):
                    if not last_slot:
                        if place == 0 and small:
                            pe.wait_ge(max_operands_in[nb], ni * 32 + 32)
                        elif place == 0 and nb == 0:
                            pe.wait_ge(weights_in, ni * (16 * n_weights) + 16 * n_weights)
                        for n in range(len(plan)):
                            if place_of(n) == place:
                                next_job_use(nb, n, *J.use(i, b, n), J.job(i, b, 1, 2))
                        if place == rows_place:
                            max_rows_use(*J.use(i, b, len(plan)), J.job(i, b, 1, 2))
                    if place >= places - 3 and not first_slot:
                        k = place - (places - 3)
                        output_use(*before(i, b), k, *J.use(i, b, r0 + k))

                pe.wait_ge(max_loaded, J.job(i, b, 16, 16))
                if small:
                    pe.wait_ge(operands_in[b], i * 32 + 32)
                elif full:
                    pe.wait_ge(keys_b_ready, J.job(i, b, 1, 1))
                elif first_slot:
                    pe.wait_ge(keys_b_ready, 2)
                for k in range(steps):
                    for h in range(2):
                        half_scores(i, b, k, h)
                        between(3 * k + h)
                    if unit_at(k):
                        value_unit(i, b, *unit_at(k))
                    elif not first_slot:
                        value_unit(*before(i, b), *unit_at(k + steps))
                    between(3 * k + 2)

            iterations(pe, lambda i: (slot(i, 0), slot(i, 1)))
            for k in range(steps):
                if unit_at(k + steps):
                    value_unit(last_i, 1, *unit_at(k + steps))
            for k in range(3):
                output_use(last_i, 1, k, *J.use(last_i, 1, r_uses + k))

        @block.scalar
        def _(act):
            def save(i, b, h):
                act.wait_ge(values_done, J.job(i, b, units, units - (1 - h) * (n_parts // 2)))
                cols = slice(h * HALF, (h + 1) * HALF)
                nc.scalar.activation(out_cols[b][:, cols], outs[:, cols], ACT.Copy).then_inc(out_saved, 1)

            def high_keys(b, use):
                act.wait_ge(work_drained, use + 1)
                high = slice(dim, P) if full else slice(0, dim)
                nc.scalar.activation(keys_b[b][0:dim, :], keys[b][high, :].bitcast(F32),
                                     ACT.Copy).then_inc(keys_b_ready, 1)

            def round_part(whole, h, u, bank):
                act.wait_ge(work_filled, u + 1)
                nc.scalar.activation(whole[:, h * HALF:(h + 1) * HALF], work[:, bank, :], ACT.Copy).then_inc(rounded, 1)

            def round_pair(b, h, u, bank):
                act.wait_ge(work_filled, u + 1)
                cols = slice(h * HALF, (h + 1) * HALF)
                nc.scalar.activation(queries[b][0:dim, cols], work[0:dim, bank, :], ACT.Copy)
                nc.scalar.activation(keys[b][dim:P, cols], work[dim:P, bank, :], ACT.Copy).then_inc(rounded, 1)

            def round_next(b, h, u, bank):
                if full:
                    round_pair(b, h, u, bank)
                else:
                    round_part(queries[b], h, u, bank)

            if kind == "mqa":
                for b in range(2):
                    for h in range(2):
                        round_part(keys[b], h, 3 * b + h, (3 * b + h) % 2)
            for h in range(n_split):
                round_next(0, h, pre_uses + h, (pre_uses + h) % 2)
            if full:
                high_keys(0, 1)
            if kind == "mqa":
                for b in range(2):
                    high_keys(b, 3 * b + 1)

            def slot(i, b):
                for k in range(steps):
                    if k == 0 and n_split and not is_last(i, b):
                        at_least(act, scores_ready, J.job(i, b, steps))
                        round_next(1 - b, 0, *J.use(i, b, 0))
                    act.wait_ge(scores_ready, J.job(i, b, steps, k + 1))
                    at_least(act, values_done, J.job(i, b, units, n_parts * (k // group + 1) - units))
                    if not small:
                        at_least(act, probs_added, J.job(i, b, steps - 1, max(k, 1) - (steps - 1)))
                    nc.scalar.activation(probs[:, k, :], scores[:, k % 2, :], ACT.Exp, scale=scale).then_inc(exp_done, 1)
                    if k == 0 and n_split and not is_last(i, b):
                        round_next(1 - b, 1, *J.use(i, b, 1))
                    if k == 3 and full and not is_last(i, b):
                        high_keys(1 - b, J.use(i, b, 1)[0])
                    if k in save_steps and not J.first(i, b):
                        save(*before(i, b), save_steps.index(k))

            iterations(act, lambda i: (slot(i, 0), slot(i, 1)))
            for h in range(2):
                save(last_i, 1, h)

        @block.vector
        def _(dve):
            pre_splits = 4 if kind == "mqa" else 0

            def split(whole, low, part, b, h, u, bank, s):
                cols = slice(h * HALF, (h + 1) * HALF)
                dve.wait_ge(rounded, s + 1)
                nc.vector.tensor_tensor(low[part, cols], work[part, bank, :], whole[part, cols].bitcast(F32),
                                        ALU.subtract).then_inc(work_drained, 1)

            def split_key(b, h, u, bank, s):
                split(keys[b], keys[b], slice(dim, 2 * dim), b, h, u, bank, s)

            def copy_values(b, u, bank):
                dve.wait_ge(work_filled, u + 1)
                nc.vector.tensor_copy(values[b][:, :, :],
                                      work[:, bank, :].rearrange("p (t d) -> p t d", d=dim)).then_inc(work_drained, 1)

            def next_job_use(b, n, u, bank, s0):
                what, k = plan[n]
                if what == "query":
                    split(queries[b], queries_b[b], slice(0, dim), b, k, u, bank, s0 + k)
                elif what == "pair":
                    cols = slice(k * HALF, (k + 1) * HALF)
                    dve.wait_ge(rounded, s0 + k + 1)
                    nc.vector.tensor_tensor(queries_b[b][0:dim, cols], work[0:dim, bank, :],
                                            queries[b][0:dim, cols].bitcast(F32), ALU.subtract)
                    nc.vector.tensor_tensor(keys[b][0:dim, cols], work[dim:P, bank, :],
                                            keys[b][dim:P, cols].bitcast(F32), ALU.subtract).then_inc(work_drained, 1)
                    if k:
                        nc.vector.tensor_copy(queries[b][dim:P, :],
                                              queries[b][0:dim, :].bitcast(F32)).then_inc(queries_ready, 1)
                elif what == "values":
                    copy_values(b, u, bank)
                else:
                    dve.wait_ge(work_filled, u + 1)
                    nc.vector.tensor_reduce(part_max[:, k // 2, k % 2:k % 2 + 1], work[:, bank, :], AX.X,
                                            ALU.max).then_inc(work_drained, 1)

            def join_max(u, bank, dma_value):
                dve.wait_ge(work_drained, u)
                nc.vector.tensor_reduce(neg_max[:, :], part_max[:, :, :], AX.X, ALU.max,
                                        negate=True).then_inc(max_joined, 1)
                dve.wait_ge(work_filled, u + 1)
                at_least(dve, max_loaded, dma_value)
                nc.vector.tensor_copy(max_rows[:, :], work[0:QB, bank, 0:P]).then_inc(work_drained, 1)

            def output_use(b, k, u, bank, r0):
                n = min(3, QB - 3 * k)
                dve.wait_ge(work_filled, u + 1)
                at = work[:, bank, 0:n * OUT].rearrange("p (j c) -> p j c", c=OUT)
                nc.vector.reciprocal(recip[:, b, 3 * k:3 * k + n], at[:, :, C]).then_inc(recip_done, 1)
                dve.wait_ge(recip_done, r0 + k + 1)
                for j in range(n):
                    t = b * QB + 3 * k + j
                    last = nc.vector.scalar_tensor_tensor(per.acc[:, t, :], at[:, j, 0:C],
                                                          recip[:, b, 3 * k + j:3 * k + j + 1], per.acc[:, t, :],
                                                          ALU.mult, ALU.add)
                last.then_inc(work_drained, 1)

            def head_weights(i, b):
                nc.vector.tensor_scalar(w_head[b][:, :], w_out[:, span(i * OUT, OUT)], 1.0, None,
                                        ALU.mult).then_inc(w_head_ready, 1)

            def head_values(i, b):
                nc.vector.tensor_scalar(values[b][:, :, 0:v_used],
                                        heads.v_rows[:, b * QB:(b + 1) * QB, span(i * v_used, v_used)], 1.0, None,
                                        ALU.mult).then_inc(values_in, 1)

            if small:
                for x in keys_m + queries_m + keys + queries:
                    nc.vector.memset(x[rows:max_at, :].bitcast(F32), 0.0).then_inc(rows_cleared, 1)
            dve.wait_ge(consts_set, n_consts)
            dve.wait_ge(w_out_in, 16 * group)
            if small:
                head_values(0, 0)
            if kind == "mqa":
                for b in range(2):
                    for h in range(2):
                        split_key(b, h, 3 * b + h, (3 * b + h) % 2, 2 * b + h)
                    copy_values(b, 3 * b + 2, (3 * b + 2) % 2)
            for n in range(len(plan)):
                next_job_use(0, n, pre_uses + n, (pre_uses + n) % 2, pre_splits)
            join_max(J.u0 - 1, (J.u0 - 1) % 2, 0)

            def slot(i, b):
                last_slot, first_slot = is_last(i, b), J.first(i, b)
                ni, nb = after(i, b)
                r0 = 0 if last_slot else len(plan) + 1
                dve.wait_ge(work_filled, J.use(i, b, 0)[0])
                head_weights(i, b)
                if not last_slot:
                    at_least(dve, scores_ready, J.job(i, b, steps))
                    for n in range(len(plan)):
                        if n == values_place:
                            at_least(dve, values_done, J.job(i, b, units))
                            if small:
                                head_values(ni, nb)
                        next_job_use(nb, n, *J.use(i, b, n), J.job(i, b, n_split, n_split + pre_splits))
                    join_max(*J.use(i, b, len(plan)), J.job(i, b, 16, 16))
                if not first_slot:
                    for k in range(3):
                        output_use(1 - b, k, *J.use(i, b, r0 + k), J.job(i, b, 3, -3))

            dve.wait_ge(acc_set, 1)
            iterations(dve, lambda i: (slot(i, 0), slot(i, 1)))
            for k in range(3):
                output_use(1, k, *J.use(last_i, 1, r_uses + k), 3 * (2 * n_heads - 1))



def window_attention_stage(nc, per, name, heads, masks, scale):
    G = 4
    JOBS = BATCH * H8
    BANKS = QB // 2
    AHEAD_SCORES, AHEAD_EXP = 4, 2
    rows = 2 * 2 * D8
    k_rows = 64
    W = 2 * P
    CELLS = PREFIX + W
    SUMS = 3 * 32
    with Stage(nc, name) as st:
        keys = [st.sb(f"keys{k}", [k_rows, SEQ], F32R) for k in range(2)]
        queries = [st.sb(f"queries{k}", [k_rows, SEQ], F32R) for k in range(2)]
        mask = st.sb("mask", [P, 2, HALF])
        masked = [st.sb(f"masked{k}", [P, QB, CELLS]) for k in range(2)]
        probs = [st.sb(f"probs{r}", [P, QB, CELLS]) for r in range(G)]
        prefix_probs = [st.sb(f"prefix_probs{r}", [P, QB * PREFIX]) for r in range(G)]
        turned = [st.sb(f"turned{k}", [P, BANKS, HALF]) for k in range(2)]
        values = [st.sb(f"values{r}", [P, QB + 1, 32]) for r in range(G)]
        prefix_values = [st.sb(f"prefix_values{r}", [P, QB, 32]) for r in range(G)]
        prefix_all = st.sb("prefix_all", [P, QB, BATCH, H8 * (D8 + 1)])
        out_cols = st.sb("out_cols", [SUMS, JOBS // G, SEQ])
        w_groups = st.sb("w_groups", [SUMS, G, C])
        block_max = [st.sb(f"block_max{k}", [P, QB]) for k in range(2)]
        neg_max = [st.sb(f"neg_max{k}", [P, QB]) for k in range(2)]
        sums = [st.sb(f"sums{k}", [P, QB]) for k in range(2)]
        inverse = [st.sb(f"inverse{k}", [P, QB]) for k in range(2)]
        scores = st.ps("scores", [P, BANKS, HALF])
        turn = st.ps("turn", [P, 2, HALF])
        outs = st.ps("outs", [P, SEQ])

        operands_in = [st.sem(f"operands_in{k}") for k in range(2)]
        consts_in, consts_set, prefix_in = st.sem("consts_in"), st.sem("consts_set"), st.sem("prefix_in")
        scores_ready, cells_masked, maxima_ready = st.sem("scores_ready"), st.sem("cells_masked"), st.sem("maxima_ready")
        neg_max_ready, exp_done = st.sem("neg_max_ready"), st.sem("exp_done")
        inverse_ready, normed_step = st.sem("inverse_ready"), st.sem("normed_step")
        turn_filled, turn_drained = st.sem("turn_filled"), st.sem("turn_drained")
        values_in, values_done, out_saved = st.sem("values_in"), st.sem("values_done"), st.sem("out_saved")
        rows_done, added = st.sem("rows_done"), st.sem("added")
        n_fills = 2 * 2 + G * 2 + 2 * 2 + 1
        NORMS = 1 + BANKS
        block = st.begin()

        def groups(eng, job):
            def body(b, g):
                for r in range(G):
                    job(b, g, r)
            body(0, 0)
            with eng.Fori(1, H8 // G) as g:
                body(0, g)
            with eng.Fori(0, H8 // G - 1) as g:
                body(1, g)
            body(1, H8 // G - 1)

        def at(b, g, r, each=1, plus=0):
            return g * (G * each) + ((H8 * b + r) * each + plus)

        def at_least(eng, sem, value):
            if not isinstance(value, int) or value > 0:
                eng.wait_ge(sem, value)

        def exists(b, g, r, ahead):
            n = at(b, g, r, 1, ahead)
            return not isinstance(n, int) or n < JOBS

        def score_cells(j):
            return slice(0, P) if j == 0 else slice((j % 2) * W, (j % 2 + 1) * W)

        def prefix_scores(j):
            return slice(P + (j - 2) * PREFIX, P + (j - 1) * PREFIX)

        @block.sync
        def _(sp):
            sp.dma_start(mask[:, :, :], masks).then_inc(consts_in, 16)
            for g in range(G):
                for k in range(3):
                    sp.dma_start(w_groups[32 * k:32 * (k + 1), g, :], heads.w_out[32 * g:32 * (g + 1), :]).then_inc(consts_in, 16)
            sp.wait_ge(consts_set, n_fills)
            for j in range(2, QB):
                for b in range(BATCH):
                    sp.dma_start(prefix_all[j * PREFIX:(j + 1) * PREFIX, j, b, :],
                                 heads.v_rows[0:PREFIX, b * QB, :]).then_inc(prefix_in, 16)

            def job(b, g, r):
                at_least(sp, scores_ready, at(b, g, r, BANKS, -BANKS))
                for dst, x in ((keys[r % 2], "k"), (queries[r % 2], "q")):
                    sp.dma_start(dst[0:rows, :].bitcast(F32),
                                 heads.stacks[x][span(at(b, g, r, rows), rows), :]).then_inc(operands_in[r % 2], 16)

            groups(sp, job)

        @block.gpsimd
        def _(pool):
            fills = [(x[rows:k_rows, :].bitcast(F32), 0.0) for x in keys + queries]
            fills += [(x[:, :, :], 0.0) for x in values + prefix_values]
            fills += [(x[:, 0, 0:PREFIX + P], MASKED) for x in masked]
            fills += [(x[:, 1, 0:PREFIX], MASKED) for x in masked]
            fills += [(prefix_all[:, :, :, :], 0.0)]
            assert len(fills) == n_fills
            for done, (x, value) in enumerate(fills):
                nc.gpsimd.memset(x, value).then_inc(consts_set, 1)
                pool.wait_ge(consts_set, done + 1)

            def job(b, g, r):
                def scale_cells(to, cols, j0, j1):
                    cells = probs[r][:, j0:j1, cols]
                    by = inverse[r % 2][:, j0:j1].unsqueeze(2).to_broadcast([P, j1 - j0, cells.shape[-1]])
                    nc.gpsimd.tensor_tensor(cells if to is None else to, cells, by, ALU.mult).then_inc(normed_step, 1)
                pool.wait_ge(inverse_ready, at(b, g, r, 1, 1))
                scale_cells(prefix_probs[r][:, :].rearrange("p (j k) -> p j k", k=PREFIX), slice(0, PREFIX), 0, QB)
                for m in range(BANKS):
                    scale_cells(None, slice(PREFIX, CELLS), 2 * m, 2 * m + 2)

            groups(pool, job)

        @block.tensor
        def _(pe):
            def scores_of(b, g, r, m):
                k = r % 2
                if m == 0:
                    pe.wait_ge(operands_in[k], g * (16 * G) + (8 * b + r // 2) * 32 + 32)
                at_least(pe, cells_masked, at(b, g, r, BANKS, m + 1 - BANKS))
                for j in (2 * m, 2 * m + 1):
                    last = nc.tensor.matmul(scores[:, m, score_cells(j)], queries[k][:, j * P:(j + 1) * P],
                                            keys[k][:, max(j - 1, 0) * P:(j + 1) * P],
                                            start=True, stop=True, skip_group_check=True)
                if m == 0:
                    for j in range(2, QB):
                        last = nc.tensor.matmul(scores[:, 0, prefix_scores(j)], queries[k][:, j * P:(j + 1) * P],
                                                keys[k][:, 0:PREFIX], start=True, stop=True, skip_group_check=True)
                last.then_inc(scores_ready, 1)

            def turn_bank(b, g, r, m):
                pe.wait_ge(normed_step, at(b, g, r, NORMS, 2 + m))
                at_least(pe, turn_drained, at(b, g, r, BANKS, m - 1))
                for q in range(4):
                    if (m, q) == (0, 1):
                        cells = prefix_probs[r][:, :]
                    else:
                        own = (m, q) == (0, 0) or q % 2
                        cells = probs[r][:, 2 * m + q // 2, (PREFIX + P if own else PREFIX):(CELLS if own else PREFIX + P)]
                    last = nc.tensor.transpose(turn[:, m % 2, q * P:(q + 1) * P], cells, per.ident[:, :])
                last.then_inc(turn_filled, 1)

            def value_products(b, g, r, m):
                pe.wait_ge(turn_drained, at(b, g, r, BANKS, m + 1))
                if m == 0:
                    pe.wait_ge(values_in, at(b, g, r, 1, 1))
                    if r == 0:
                        at_least(pe, out_saved, g + b * (H8 // G))
                t = turned[r % 2]
                for j in (2 * m, 2 * m + 1):
                    own = 0 if j == 0 else (j % 2) * W + P
                    parts = ((prefix_values[r][:, j, :], t[:, 0, P:W]),
                             (values[r][:, j, :], t[:, m, own:own + P]),
                             (values[r][:, j - 1 if j else QB, :], t[:, m, max(own - P, 0):max(own - P, 0) + P]))
                    for k, (v, p) in enumerate(parts):
                        last = nc.tensor.matmul(outs[32 * k:32 * (k + 1), j * P:(j + 1) * P], v, p,
                                                start=r == 0 and j % 4 == 0, stop=r == G - 1, skip_group_check=True)
                last.then_inc(values_done, 1)

            pe.wait_ge(consts_set, n_fills)
            for n in range(AHEAD_SCORES):
                for m in range(BANKS):
                    scores_of(0, 0, n, m)

            def job(b, g, r):
                for m in range(BANKS):
                    turn_bank(b, g, r, m)
                    if m:
                        value_products(b, g, r, m - 1)
                    if exists(b, g, r, AHEAD_SCORES):
                        n = r + AHEAD_SCORES
                        scores_of(b, g + n // G, n % G, m)
                value_products(b, g, r, BANKS - 1)

            groups(pe, job)
            pe.wait_ge(consts_in, 16 * (1 + 3 * G))
            pe.wait_ge(out_saved, JOBS // G)
            for c in range(CHUNKS):
                for j in range(4):
                    q = (c % 2) * 4 + j
                    for g in range(G):
                        last = nc.tensor.matmul(scores[:, c, j * P:(j + 1) * P],
                                                out_cols[:, (c // 2) * G + g, q * P:(q + 1) * P],
                                                w_groups[:, g, :], start=g == 0, stop=g == G - 1)
                last.then_inc(rows_done, 1)

        @block.scalar
        def _(act):
            def exponentials(b, g, r, blocks):
                k = r % 2
                if 0 in blocks:
                    act.wait_ge(neg_max_ready, at(b, g, r, 1, 1))
                    at_least(act, turn_filled, at(b, g, r, BANKS, -3 * BANKS))
                    at_least(act, inverse_ready, at(b, g, r, 1, -1))
                for j in blocks:
                    last = nc.scalar.activation(probs[r][:, j, :], masked[k][:, j, :], ACT.Exp, scale=scale,
                                                bias=neg_max[k][:, j:j + 1], accum_out=sums[k][:, j:j + 1])
                if QB - 1 in blocks:
                    last.then_inc(exp_done, 1)

            act.wait_ge(consts_set, n_fills)
            for n in range(AHEAD_EXP):
                exponentials(0, 0, n, range(QB))

            def job(b, g, r):
                for m in range(BANKS):
                    act.wait_ge(turn_filled, at(b, g, r, BANKS, m + 1))
                    if m == 0:
                        at_least(act, values_done, at(b, g, r, BANKS, -BANKS))
                    nc.scalar.activation(turned[r % 2][:, m, :], turn[:, m % 2, :], ACT.Copy).then_inc(turn_drained, 1)
                    if exists(b, g, r, AHEAD_EXP):
                        n = r + AHEAD_EXP
                        exponentials(b, g + n // G, n % G, (2 * m, 2 * m + 1))

            groups(act, job)

        @block.vector
        def _(dve):
            def take_values(b, g, r):
                at_least(dve, values_done, at(b, g, r, BANKS, -3 * BANKS))
                head = span(g * (G * (D8 + 1)) + r * (D8 + 1), D8)
                mine = slice(r * D8, (r + 1) * D8)
                nc.vector.tensor_scalar(values[r][:, 0:QB, mine], heads.v_rows[:, b * QB:(b + 1) * QB, head], 1.0, None,
                                        ALU.mult)
                nc.vector.tensor_scalar(prefix_values[r][:, :, mine], prefix_all[:, :, b, head], 1.0, None,
                                        ALU.mult).then_inc(values_in, 1)

            def save(b, g):
                dve.wait_ge(values_done, at(b, g, G - 1, BANKS, BANKS))
                where = out_cols[:, span(g + b * (H8 // G), 1), :].rearrange("p a t -> p (a t)")
                nc.vector.tensor_scalar(where, outs[0:SUMS, :], 1.0, None, ALU.mult).then_inc(out_saved, 1)

            def invert(k, count):
                dve.wait_ge(exp_done, count)
                at_least(dve, normed_step, count * NORMS - 2 * NORMS)
                nc.vector.reciprocal(inverse[k][:, :], sums[k][:, :]).then_inc(inverse_ready, 1)

            def job(b, g, r):
                k = r % 2
                n_before = at(b, g, r, 1, -1)
                if not isinstance(n_before, int) or n_before > 0:
                    invert(k, n_before)
                for m in range(BANKS):
                    dve.wait_ge(scores_ready, at(b, g, r, BANKS, m + 1))
                    if m == 0:
                        nc.vector.tensor_tensor(masked[k][:, 0, PREFIX + P:CELLS], scores[:, 0, 0:P], mask[:, 0, 0:P],
                                                ALU.add)
                        nc.vector.tensor_copy(masked[k][:, 2:QB, 0:PREFIX],
                                              scores[:, 0, P:P + (QB - 2) * PREFIX].rearrange("p (j k) -> p j k", k=PREFIX))
                        last = nc.vector.tensor_tensor(masked[k][:, 1, PREFIX:CELLS], scores[:, 0, W:2 * W],
                                                       mask[:, 0, W:2 * W], ALU.add)
                    else:
                        last = nc.vector.tensor_tensor(masked[k][:, 2 * m:2 * m + 2, PREFIX:CELLS],
                                                       scores[:, m, :].rearrange("p (j k) -> p j k", k=W),
                                                       mask[:, 1, :].rearrange("p (j k) -> p j k", k=W), ALU.add)
                    last.then_inc(cells_masked, 1)
                dve.wait_ge(cells_masked, at(b, g, r, BANKS, BANKS))
                nc.vector.tensor_reduce(block_max[k][:, :], masked[k][:, :, :], AX.X, ALU.max).then_inc(maxima_ready, 1)
                dve.wait_ge(maxima_ready, at(b, g, r, 1, 1))
                nc.vector.tensor_scalar(neg_max[k][:, :], block_max[k][:, :], -scale, None,
                                        ALU.mult).then_inc(neg_max_ready, 1)
                take_values(b, g, r)
                if r == G - 2 and not (isinstance(g, int) and (b, g) == (0, 0)):
                    save(b, g - 1)

            dve.wait_ge(consts_in, 16 * (1 + 3 * G))
            dve.wait_ge(consts_set, n_fills)
            dve.wait_ge(prefix_in, 16 * BATCH * (QB - 2))
            groups(dve, job)
            for n in (JOBS - 1, JOBS):
                invert((n - 1) % 2, n)
            save(1, H8 // G - 1)
            for c in range(CHUNKS):
                tiles = slice(4 * c, 4 * c + 4)
                dve.wait_ge(rows_done, c + 1)
                nc.vector.tensor_tensor(per.acc[:, tiles, :], scores[:, c, :].rearrange("p (t c) -> p t c", c=C),
                                        per.x_rows[:, tiles, :], ALU.add).then_inc(added, 1)



def layer0_ffn(nc, per, t):
    with Stage(nc, "L0_ffn") as st:
        w = st.sb("w", [C, C])
        a1 = st.sb("a1", [C, C])
        a2 = st.sb("a2", [C, C])
        b_row = st.sb("b_row", [1, C])
        w_t = st.sb("w_t", [C, C])
        a1_t = st.sb("a1_t", [C, C])
        a12 = st.sb("a12", [C, C])
        wa = st.sb("wa", [C, C])
        act_out = st.sb("act_out", [P, TILES, C])
        small_ps = st.ps("small_ps", [P, 4, HALF])
        out_ps = st.ps("out_ps", [P, CHUNKS, HALF])
        loaded = st.sem("loaded")
        product, copied = st.sem("product"), st.sem("copied")
        rows_done, tanh_done, added = st.sem("rows_done"), st.sem("tanh_done"), st.sem("added")
        block = st.begin()

        @block.sync
        def _(sp):
            for dst, name in ((w, "weight"), (a1, "aux_weight1"), (a2, "aux_weight2")):
                sp.dma_start(dst[:, :], t["L0_ffn_" + name]).then_inc(loaded, 16)
            sp.dma_start(b_row[:, :], t["L0_ffn_bias"].rearrange("(a c) -> a c", a=1)).then_inc(loaded, 16)

        @block.tensor
        def _(pe):
            pe.wait_ge(loaded, 64)
            nc.tensor.transpose(small_ps[:, 0, 0:C], w[:, :], per.ident[:, :]).then_inc(product, 1)
            nc.tensor.transpose(small_ps[:, 1, 0:C], a1[:, :], per.ident[:, :]).then_inc(product, 1)
            pe.wait_ge(copied, 2)
            nc.tensor.matmul(small_ps[:, 2, 0:C], a1_t[:, :], a2[:, :], start=True, stop=True).then_inc(product, 1)
            pe.wait_ge(copied, 3)
            nc.tensor.matmul(small_ps[:, 3, 0:C], w_t[:, :], a12[:, :], start=True, stop=True).then_inc(product, 1)
            pe.wait_ge(copied, 4)
            for k in range(TILES):
                cols = slice((k % 4) * C, (k % 4 + 1) * C)
                nc.tensor.matmul(out_ps[:, k // 4, cols], per.ones_row[:, :], b_row[:, :], start=True, stop=False)
                nc.tensor.matmul(out_ps[:, k // 4, cols], per.x_cols[:, k * P:(k + 1) * P], wa[:, :],
                                 start=False, stop=True).then_inc(rows_done, 1)

        @block.scalar
        def _(act):
            for k, dst in enumerate((w_t, a1_t, a12, wa)):
                act.wait_ge(product, k + 1)
                nc.scalar.activation(dst[:, :], small_ps[:, k, 0:C], ACT.Copy).then_inc(copied, 1)
            for c in range(CHUNKS):
                act.wait_ge(rows_done, 4 * c + 4)
                nc.scalar.activation(act_out[:, 4 * c:4 * c + 4, :],
                                     out_ps[:, c, :].rearrange("p (t c) -> p t c", c=C), ACT.Tanh).then_inc(tanh_done, 1)

        @block.vector
        def _(dve):
            for c in range(CHUNKS):
                dve.wait_ge(tanh_done, c + 1)
                part = slice(4 * c, 4 * c + 4)
                nc.vector.tensor_tensor(per.acc[:, part, :], per.x_rows[:, part, :], act_out[:, part, :],
                                        ALU.add).then_inc(added, 1)
    norm_stage(nc, per, "L0_norm1", per.acc, per.x_rows)


def one_hot_of_max(nc, dve, scores, n, one_hot, scratch, eq, top, rev, step, at):
    def wide(a):
        return a[:, :].unsqueeze(2).to_broadcast([P, TILES, n])
    nc.vector.tensor_reduce(top[:, :], scores[:, :, :], AX.X, ALU.max).then_inc(step, 1)
    dve.wait_ge(step, at + 1)
    nc.vector.tensor_tensor(eq[:, :, :], scores[:, :, :], wide(top), ALU.is_equal).then_inc(step, 1)
    dve.wait_ge(step, at + 2)
    nc.vector.tensor_tensor(eq[:, :, :], eq[:, :, :], rev[:, 0:n].unsqueeze(1).to_broadcast([P, TILES, n]),
                            ALU.mult).then_inc(step, 1)
    dve.wait_ge(step, at + 3)
    nc.vector.tensor_reduce(scratch[:, :], eq[:, :, :], AX.X, ALU.max).then_inc(step, 1)
    dve.wait_ge(step, at + 4)
    nc.vector.tensor_tensor(one_hot[:, :, :], eq[:, :, :], wide(scratch), ALU.is_equal).then_inc(step, 1)
    dve.wait_ge(step, at + 5)
    return at + 5


N_ROUTED = 32
SORTED_TILES = -(-(TILES + N_ROUTED - 1) // 4) * 4


def layer1_ffn(nc, per, t):
    sorted_x = nc.dram_tensor("L1_sorted_x", (SORTED_TILES * P, C), F32).ap()
    sorted_y = nc.dram_tensor("L1_sorted_y", (SORTED_TILES * P, C), F32).ap()
    with ExitStack() as ctx:
        held = Held(nc, ctx, "L1_routed")
        places = held.sb("places", [P, TILES], I32)
        weight_rows = held.sb("weight_rows", [1, SORTED_TILES], I32)
        routing_stage(nc, per, t, sorted_x, places, weight_rows)
        shared = [t["L1_ffn_shared_" + n] for n in ("gate_w", "up_w", "down_w")]
        experts_stage(nc, per, "L1_shared", 1, per.x_cols, None,
                      lambda e: (shared[0], shared[1]), lambda e: shared[2], flip=False)
        routed = [t["L1_ffn_routed_" + n].rearrange("e a b -> (e a) b") for n in ("gate_w", "up_w", "down_w")]
        sorted_experts_stage(nc, per, "L1_experts", sorted_x, sorted_y, weight_rows, routed)
        gather_stage(nc, per, "L1_gather", sorted_y, places)
    norm_stage(nc, per, "L1_norm1", per.acc, per.x_rows)


def routing_stage(nc, per, t, sorted_x, places, weight_rows):
    n_e = N_ROUTED
    with Stage(nc, "L1_router") as st:
        w = st.sb("w", [C, n_e])
        rev = st.sb("rev", [P, n_e])
        below = st.sb("below", [P, P])
        ones = st.sb("ones", [P, P])
        zeros = st.sb("zeros", [P, C])
        tile_starts = st.sb("tile_starts", [P, TILES])
        up_to = st.sb("up_to", [P, n_e, n_e])
        tile_numbers = st.sb("tile_numbers", [1, SORTED_TILES])
        pick = st.sb("pick", [P, TILES, n_e])
        logits = st.sb("logits", [P, TILES, n_e])
        eq = st.sb("eq", [P, TILES, n_e])
        top = st.sb("top", [P, TILES])
        scratch = st.sb("scratch", [P, TILES])
        score = st.sb("score", [P, TILES])
        scaled = st.sb("scaled", [P, TILES, C])
        earlier = st.sb("earlier", [P, TILES + 1, n_e])
        counts = st.sb("counts", [P, n_e])
        over = st.sb("over", [P, n_e, TILES])
        n_tiles = st.sb("n_tiles", [P, n_e])
        products = st.sb("products", [P, n_e, n_e])
        ends = st.sb("ends", [P, n_e])
        starts = st.sb("starts", [P, n_e])
        row = st.sb("row", [P, TILES, n_e])
        place = st.sb("place", [P, TILES])
        passed = st.sb("passed", [1, SORTED_TILES, n_e])
        expert = st.sb("expert", [1, SORTED_TILES])
        logit_ps = st.ps("logit_ps", [P, HALF])
        rank_ps = st.ps("rank_ps", [P, HALF])
        count_ps = st.ps("count_ps", [P, n_e])
        loaded, logits_done, zeros_set = st.sem("loaded"), st.sem("logits_done"), st.sem("zeros_set")
        cleared, scattered = st.sem("cleared"), st.sem("scattered")
        step, score_ready, scaled_ready = st.sem("step"), st.sem("score_ready"), st.sem("scaled_ready")
        earlier_ready, ranks_done, sorting = st.sem("earlier_ready"), st.sem("ranks_done"), st.sem("sorting")
        places_ready, acc_set = st.sem("places_ready"), st.sem("acc_set")
        block = st.begin()

        @block.sync
        def _(sp):
            for dst, name in ((rev, "reversed"), (below, "below"), (tile_starts, "tile_starts")):
                sp.dma_start(dst[:, :], t[name]).then_inc(loaded, 16)
            sp.dma_start(w[:, :], t["L1_ffn_gate_w"]).then_inc(loaded, 16)
            sp.dma_start(up_to[:, :, :], t["up_to"]).then_inc(loaded, 16)
            sp.dma_start(tile_numbers[:, :], t["tile_numbers"]).then_inc(loaded, 16)
            sp.wait_ge(zeros_set, 1)
            sp.dma_start(sorted_x.rearrange("(k p) c -> p k c", p=P),
                         zeros[:, :].unsqueeze(1).to_broadcast([P, SORTED_TILES, C])).then_inc(cleared, 16)

        @block.tensor
        def _(pe):
            pe.wait_ge(loaded, 16 * 6)
            for k in range(TILES):
                nc.tensor.matmul(logit_ps[:, k * n_e:(k + 1) * n_e], per.x_cols[:, k * P:(k + 1) * P], w[:, :],
                                 start=True, stop=True).then_inc(logits_done, 1)
            pe.wait_ge(zeros_set, 2)
            pe.wait_ge(earlier_ready, TILES + 1)
            nc.tensor.matmul(count_ps[:, :], ones[:, :], earlier[:, TILES, :], start=True, stop=True).then_inc(ranks_done, 1)
            nc.tensor.matmul(rank_ps[:, :], ones[:, :], earlier[:, 0:TILES, :].rearrange("p t e -> p (t e)"),
                             start=True, stop=False)
            nc.tensor.matmul(rank_ps[:, :], below[:, :], pick[:, :, :].rearrange("p t e -> p (t e)"),
                             start=False, stop=True).then_inc(ranks_done, 1)

        @block.scalar
        def _(act):
            act.wait_ge(step, 2)
            nc.scalar.activation(score[:, :], top[:, :], ACT.Sigmoid).then_inc(score_ready, 1)
            act.wait_ge(score_ready, 1)
            for k in range(TILES):
                nc.scalar.activation(scaled[:, k, :], per.x_rows[:, k, :], ACT.Copy,
                                     scale=score[:, k:k + 1]).then_inc(scaled_ready, 1)

        @block.vector
        def _(dve):
            def chain(sem, count, op):
                op.then_inc(sem, 1)
                dve.wait_ge(sem, count)
                return count + 1
            dve.wait_ge(loaded, 16 * 6)
            dve.wait_ge(logits_done, TILES)
            nc.vector.tensor_copy(logits[:, :, :], logit_ps[:, :].rearrange("p (t e) -> p t e", e=n_e)).then_inc(step, 1)
            dve.wait_ge(step, 1)
            one_hot_of_max(nc, dve, logits, n_e, pick, scratch, eq, top, rev, step, 1)
            n = chain(earlier_ready, 1, nc.vector.memset(earlier[:, 0, :], 0.0))
            for k in range(TILES):
                n = chain(earlier_ready, n, nc.vector.tensor_tensor(earlier[:, k + 1, :], earlier[:, k, :], pick[:, k, :],
                                                                   ALU.add))
            dve.wait_ge(ranks_done, 1)
            n = chain(sorting, 1, nc.vector.tensor_copy(counts[:, :], count_ps[:, :]))
            n = chain(sorting, n, nc.vector.tensor_tensor(
                over[:, :, :], counts[:, :].unsqueeze(2).to_broadcast([P, n_e, TILES]),
                tile_starts[:, :].unsqueeze(1).to_broadcast([P, n_e, TILES]), ALU.is_gt))
            n = chain(sorting, n, nc.vector.tensor_reduce(n_tiles[:, :], over[:, :, :], AX.X, ALU.add))
            n = chain(sorting, n, nc.vector.tensor_tensor(
                products[:, :, :], up_to[:, :, :], n_tiles[:, :].unsqueeze(1).to_broadcast([P, n_e, n_e]), ALU.mult))
            n = chain(sorting, n, nc.vector.tensor_reduce(ends[:, :], products[:, :, :], AX.X, ALU.add))
            n = chain(sorting, n, nc.vector.tensor_tensor(starts[:, :], ends[:, :], n_tiles[:, :], ALU.subtract))
            n = chain(sorting, n, nc.vector.tensor_scalar(starts[:, :], starts[:, :], float(P), None, ALU.mult))
            dve.wait_ge(ranks_done, 2)
            n = chain(sorting, n, nc.vector.tensor_tensor(
                row[:, :, :], rank_ps[:, :].rearrange("p (t e) -> p t e", e=n_e),
                starts[:, :].unsqueeze(1).to_broadcast([P, TILES, n_e]), ALU.add))
            n = chain(sorting, n, nc.vector.tensor_tensor(row[:, :, :], row[:, :, :], pick[:, :, :], ALU.mult))
            n = chain(sorting, n, nc.vector.tensor_reduce(place[:, :], row[:, :, :], AX.X, ALU.add))
            nc.vector.tensor_copy(places[:, :], place[:, :]).then_inc(places_ready, 1)
            n = chain(sorting, n, nc.vector.tensor_tensor(
                passed[:, :, :], ends[0:1, :].unsqueeze(1).to_broadcast([1, SORTED_TILES, n_e]),
                tile_numbers[:, :].unsqueeze(2).to_broadcast([1, SORTED_TILES, n_e]), ALU.is_le))
            n = chain(sorting, n, nc.vector.tensor_reduce(expert[:, :], passed[:, :, :], AX.X, ALU.add))
            n = chain(sorting, n, nc.vector.tensor_scalar(expert[:, :], expert[:, :], float(n_e - 1), None, ALU.min))
            nc.vector.tensor_scalar(weight_rows[:, :], expert[:, :], float(C), None, ALU.mult).then_inc(places_ready, 1)

        @block.gpsimd
        def _(pool):
            nc.gpsimd.memset(zeros[:, :], 0.0).then_inc(zeros_set, 1)
            nc.gpsimd.memset(ones[:, :], 1.0).then_inc(zeros_set, 1)
            nc.gpsimd.tensor_copy(per.acc[:, :, :], per.x_rows[:, :, :]).then_inc(acc_set, 1)
            pool.wait_ge(places_ready, 1)
            pool.wait_ge(cleared, 16)
            for k in range(TILES):
                pool.wait_ge(scaled_ready, k + 1)
                pool.indirect_dma_start(out=sorted_x, out_offset=bass.IndirectOffsetOnAxis(ap=places[:, k:k + 1], axis=0),
                                        in_=scaled[:, k, :], in_offset=None).then_inc(scattered, 16)
            pool.wait_ge(scattered, 16 * TILES)


def gather_stage(nc, per, name, sorted_y, places):
    with Stage(nc, name) as st:
        mine = st.sb("mine", [P, TILES, C])
        gathered, added = [st.sem(f"gathered{c}") for c in range(CHUNKS)], st.sem("added")
        block = st.begin()

        @block.gpsimd
        def _(pool):
            for k in range(TILES):
                pool.indirect_dma_start(out=mine[:, k, :], out_offset=None, in_=sorted_y,
                                        in_offset=bass.IndirectOffsetOnAxis(ap=places[:, k:k + 1], axis=0)
                                        ).then_inc(gathered[k // 4], 16)

        @block.vector
        def _(dve):
            for c in range(CHUNKS):
                tiles = slice(4 * c, 4 * c + 4)
                dve.wait_ge(gathered[c], 64)
                nc.vector.tensor_tensor(per.acc[:, tiles, :], per.acc[:, tiles, :], mine[:, tiles, :],
                                        ALU.add).then_inc(added, 1)


def sorted_experts_stage(nc, per, name, sorted_x, sorted_y, weight_rows, w):
    U = 4
    IN = 2 * C
    with Stage(nc, name) as st:
        up = [st.sb(f"up{k}", [C, 2 * IN]) for k in range(U)]
        down = [st.sb(f"down{k}", [P, 2, C]) for k in range(U)]
        x_tile = [st.sb(f"x_tile{k}", [P, C]) for k in range(U)]
        x_t = [st.sb(f"x_t{k}", [C, P]) for k in range(2)]
        gated = [st.sb(f"gated{k}", [P, IN]) for k in range(2)]
        hidden = [st.sb(f"hidden{k}", [P, IN]) for k in range(2)]
        y_tile = [st.sb(f"y_tile{k}", [P, C]) for k in range(U)]
        turn = st.ps("turn", [P, 2, HALF])
        pair = st.ps("pair", [P, 2, HALF])
        rows = st.ps("rows", [P, 2, HALF])
        w_in = [st.sem(f"w_in{k}") for k in range(U)]
        x_in = [st.sem(f"x_in{k}") for k in range(U)]
        stored = [st.sem(f"stored{k}") for k in range(U)]
        turned, x_ready, pair_done = st.sem("turned"), st.sem("x_ready"), st.sem("pair_done")
        silu_done, hidden_ready = st.sem("silu_done"), st.sem("hidden_ready")
        rows_done, y_ready = st.sem("rows_done"), st.sem("y_ready")
        last_i = SORTED_TILES // U - 1
        block = st.begin()

        def tiles(eng, body):
            for k in range(U):
                body(0, k)
            with eng.Fori(1, last_i) as i:
                for k in range(U):
                    body(i, k)
            for k in range(U):
                body(last_i, k)

        def at(i, k, plus=0):
            return i * U + (k + plus)

        def at_least(eng, sem, value):
            if not isinstance(value, int) or value > 0:
                eng.wait_ge(sem, value)

        @block.sync
        def _(sp):
            def load(i, k):
                first = sp.value_load(weight_rows[0:1, span(at(i, k), 1)], min_val=0, max_val=(N_ROUTED - 1) * C)
                at_least(sp, rows_done, at(i, k, 1 - U))
                for g in range(2):
                    sp.dma_start(up[k][:, g * IN:(g + 1) * IN], w[g][bass.ds(first, C), :]).then_inc(w_in[k], 16)
                sp.dma_start(down[k][:, :, :],
                             w[2][bass.ds(first * 2, IN), :].rearrange("(a p) c -> p a c", p=P)).then_inc(w_in[k], 16)

            tiles(sp, load)

        @block.tensor
        def _(pe):
            def turn_tile(i, k):
                pe.wait_ge(x_in[k], i * 16 + 16)
                at_least(pe, x_ready, at(i, k, -1))
                nc.tensor.transpose(turn[:, k % 2, 0:P], x_tile[k][:, :], per.ident[:, :]).then_inc(turned, 1)

            def rows_of(i, k):
                pe.wait_ge(hidden_ready, at(i, k, 1))
                at_least(pe, y_ready, at(i, k, -1))
                for h in range(2):
                    last = nc.tensor.matmul(rows[:, k % 2, 0:C], hidden[k % 2][:, h * P:(h + 1) * P], down[k][:, h, :],
                                            start=h == 0, stop=h == 1)
                last.then_inc(rows_done, 1)

            def tile(i, k):
                if not (isinstance(i, int) and (i, k) == (last_i, U - 1)):
                    turn_tile(i + (k + 1) // U, (k + 1) % U)
                pe.wait_ge(w_in[k], i * 48 + 48)
                pe.wait_ge(x_ready, at(i, k, 1))
                at_least(pe, hidden_ready, at(i, k, -1))
                for g in range(2):
                    for h in range(2):
                        last = nc.tensor.matmul(pair[:, k % 2, (2 * g + h) * P:(2 * g + h + 1) * P],
                                                up[k][:, g * IN + h * P:g * IN + (h + 1) * P], x_t[k % 2][:, :],
                                                start=True, stop=True)
                last.then_inc(pair_done, 1)
                if not (isinstance(i, int) and (i, k) == (0, 0)):
                    rows_of(i if k else i - 1, (k - 1) % U)

            turn_tile(0, 0)
            tiles(pe, tile)
            rows_of(last_i, U - 1)

        @block.scalar
        def _(act):
            def load_rows(i, k):
                at_least(act, turned, at(i, k, 1 - U))
                act.dma_start(x_tile[k][:, :], sorted_x[span(at(i, k) * P, P), :]).then_inc(x_in[k], 16)

            def copy_x(i, k):
                act.wait_ge(turned, at(i, k, 1))
                at_least(act, pair_done, at(i, k, -1))
                nc.scalar.activation(x_t[k % 2][:, :], turn[:, k % 2, 0:P], ACT.Copy).then_inc(x_ready, 1)

            def tile(i, k):
                if not (isinstance(i, int) and i == last_i and k):
                    load_rows(i + (k + U - 1) // U, (k + U - 1) % U)
                if not (isinstance(i, int) and (i, k) == (last_i, U - 1)):
                    copy_x(i + (k + 1) // U, (k + 1) % U)
                act.wait_ge(pair_done, at(i, k, 1))
                at_least(act, hidden_ready, at(i, k, -1))
                nc.scalar.activation(gated[k % 2][:, :], pair[:, k % 2, 0:IN], ACT.Silu).then_inc(silu_done, 1)

            for k in range(U - 1):
                load_rows(0, k)
            copy_x(0, 0)
            tiles(act, tile)

        @block.vector
        def _(dve):
            def copy_rows(i, k):
                dve.wait_ge(rows_done, at(i, k, 1))
                at_least(dve, stored[k], i * 16)
                nc.vector.tensor_copy(y_tile[k][:, :], rows[:, k % 2, 0:C]).then_inc(y_ready, 1)

            def tile(i, k):
                dve.wait_ge(silu_done, at(i, k, 1))
                at_least(dve, rows_done, at(i, k, -1))
                nc.vector.tensor_tensor(hidden[k % 2][:, :], pair[:, k % 2, IN:2 * IN], gated[k % 2][:, :],
                                        ALU.mult).then_inc(hidden_ready, 1)
                if not (isinstance(i, int) and (i, k) == (0, 0)):
                    copy_rows(i if k else i - 1, (k - 1) % U)

            tiles(dve, tile)
            copy_rows(last_i, U - 1)

        @block.gpsimd
        def _(pool):
            def store(i, k):
                pool.wait_ge(y_ready, at(i, k, 1))
                pool.dma_start(sorted_y[span(at(i, k) * P, P), :], y_tile[k][:, :]).then_inc(stored[k], 16)

            tiles(pool, store)
            for k in range(U):
                pool.wait_ge(stored[k], 16 * (last_i + 1))


def layer2_ffn(nc, per, t):
    n_e = 8
    with ExitStack() as ctx:
        held = Held(nc, ctx, "L2_routed")
        share = held.sb("share", [P, TILES, n_e])
        with Stage(nc, "L2_router") as st:
            w = st.sb("w", [n_e, C])
            w_t = st.sb("w_t", [C, n_e])
            rev = st.sb("rev", [P, 32])
            logits = st.sb("logits", [P, TILES, n_e])
            rest = st.sb("rest", [P, TILES, n_e])
            eq = st.sb("eq", [P, TILES, n_e])
            pick1 = st.sb("pick1", [P, TILES, n_e])
            pick2 = st.sb("pick2", [P, TILES, n_e])
            top1 = st.sb("top1", [P, TILES])
            top2 = st.sb("top2", [P, TILES])
            scratch = st.sb("scratch", [P, TILES])
            gap = st.sb("gap", [P, TILES])
            e2 = st.sb("e2", [P, TILES])
            p1 = st.sb("p1", [P, TILES])
            p2 = st.sb("p2", [P, TILES])
            ps = st.ps("ps", [P, 2, HALF])
            loaded, flipped, w_ready = st.sem("loaded"), st.sem("flipped"), st.sem("w_ready")
            logits_done, step, exp_ready = st.sem("logits_done"), st.sem("step"), st.sem("exp_ready")
            gap_ready, acc_set = st.sem("gap_ready"), st.sem("acc_set")
            block = st.begin()

            @block.sync
            def _(sp):
                sp.dma_start(w[:, :], t["L2_ffn_gate_w"]).then_inc(loaded, 16)
                sp.dma_start(rev[:, :], t["reversed"]).then_inc(loaded, 16)

            @block.gpsimd
            def _(pool):
                nc.gpsimd.tensor_copy(per.acc[:, :, :], per.x_rows[:, :, :]).then_inc(acc_set, 1)

            @block.tensor
            def _(pe):
                pe.wait_ge(loaded, 32)
                nc.tensor.transpose(ps[:, 0, 0:n_e], w[:, :], per.ident[0:n_e, 0:n_e]).then_inc(flipped, 1)
                pe.wait_ge(w_ready, 1)
                for k in range(TILES):
                    nc.tensor.matmul(ps[:, 1, k * n_e:(k + 1) * n_e], per.x_cols[:, k * P:(k + 1) * P], w_t[:, :],
                                     start=True, stop=True).then_inc(logits_done, 1)

            @block.scalar
            def _(act):
                act.wait_ge(flipped, 1)
                nc.scalar.activation(w_t[:, :], ps[:, 0, 0:n_e], ACT.Copy).then_inc(w_ready, 1)
                act.wait_ge(gap_ready, 1)
                nc.scalar.activation(e2[:, :], gap[:, :], ACT.Exp).then_inc(exp_ready, 1)

            @block.vector
            def _(dve):
                def wide(a):
                    return a[:, :].unsqueeze(2).to_broadcast([P, TILES, n_e])
                dve.wait_ge(loaded, 32)
                dve.wait_ge(logits_done, TILES)
                nc.vector.tensor_copy(logits[:, :, :],
                                      ps[:, 1, 0:TILES * n_e].rearrange("p (t e) -> p t e", e=n_e)).then_inc(step, 1)
                dve.wait_ge(step, 1)
                n = one_hot_of_max(nc, dve, logits, n_e, pick1, scratch, eq, top1, rev, step, 1)
                nc.vector.scalar_tensor_tensor(rest[:, :, :], pick1[:, :, :], -3.0e38, logits[:, :, :],
                                               ALU.mult, ALU.add).then_inc(step, 1)
                dve.wait_ge(step, n + 1)
                n = one_hot_of_max(nc, dve, rest, n_e, pick2, scratch, eq, top2, rev, step, n + 1)
                nc.vector.tensor_tensor(gap[:, :], top2[:, :], top1[:, :], ALU.subtract).then_inc(gap_ready, 1)
                dve.wait_ge(exp_ready, 1)
                nc.vector.tensor_scalar(p1[:, :], e2[:, :], 1.0, None, ALU.add).then_inc(step, 1)
                dve.wait_ge(step, n + 1)
                nc.vector.reciprocal(p1[:, :], p1[:, :]).then_inc(step, 1)
                dve.wait_ge(step, n + 2)
                nc.vector.tensor_tensor(p2[:, :], e2[:, :], p1[:, :], ALU.mult).then_inc(step, 1)
                dve.wait_ge(step, n + 3)
                nc.vector.tensor_tensor(pick1[:, :, :], pick1[:, :, :], wide(p1), ALU.mult).then_inc(step, 1)
                nc.vector.tensor_tensor(pick2[:, :, :], pick2[:, :, :], wide(p2), ALU.mult).then_inc(step, 1)
                dve.wait_ge(step, n + 5)
                nc.vector.tensor_tensor(share[:, :, :], pick1[:, :, :], pick2[:, :, :], ALU.add).then_inc(step, 1)
        w12 = t["L2_ffn_w12"].rearrange("e h d -> (e h) d")
        w3 = t["L2_ffn_w3"].rearrange("e d h -> (e d) h")
        experts_stage(nc, per, "L2_experts", n_e, per.x_cols, share,
                      lambda e: (w12[span(e * 4 * C, 4 * C), :],), lambda e: w3[span(e * C, C), :], flip=True)
    norm_stage(nc, per, "L2_norm1", per.acc, per.x_rows)


def experts_stage(nc, per, name, n_e, cols_in, share, w_up, w_down, flip):
    IN = 2 * C
    with Stage(nc, name) as st:
        up = [st.sb(f"up{k}", [C, 2 * IN], F32R if flip else F32) for k in range(2)]
        down = [st.sb(f"down{k}", [P, 2, C]) for k in range(2)]
        if flip:
            up_low = [st.sb(f"up_low{k}", [C, 2 * IN], F32R) for k in range(2)]
            x_high = st.sb("x_high", [C, TOKENS], F32R)
            x_low = st.sb("x_low", [C, TOKENS], F32R)
            up_raw = st.sb("up_raw", [P, 4, C])
            down_raw = st.sb("down_raw", [C, IN])
        gated = st.sb("gated", [P, 2, HALF])
        hidden = [st.sb(f"hidden{k}", [P, 2, HALF]) for k in range(2)]
        mine = [st.sb(f"mine{k}", [P, TILES]) for k in range(2)]
        pair_ps = st.ps("pair_ps", [P, 2, 2, HALF])
        rows_ps = st.ps("rows_ps", [P, 2, HALF])
        flip_ps = st.ps("flip_ps", [P, 2, HALF])
        w_in = [st.sem(f"w_in{k}") for k in range(2)]
        w_ready, flipped = st.sem("w_ready"), st.sem("flipped")
        pair_done, silu_done, hidden_ready = st.sem("pair_done"), st.sem("silu_done"), st.sem("hidden_ready")
        rows_done, rows_added, mine_ready = st.sem("rows_done"), st.sem("rows_added"), st.sem("mine_ready")
        x_rounded, x_split, up_split = st.sem("x_rounded"), st.sem("x_split"), st.sem("up_split")
        n_w = 2 if flip else 3
        block = st.begin()

        def experts(eng, body):
            body(0)
            if n_e > 4:
                with eng.Fori(1, n_e // 2 - 1) as i:
                    body(i)
            if n_e > 2:
                body(n_e // 2 - 1)

        pair = range(min(n_e, 2))

        TURN_AT = 1

        def following(i, k):
            if k == 0:
                return (i, 1)
            return None if isinstance(i, int) and i == n_e // 2 - 1 else (i + 1, 0)

        def at(i, k, each, plus=0):
            return i * (2 * each) + (each * k + plus)

        def at_least(eng, sem, value):
            if not isinstance(value, int) or value > 0:
                eng.wait_ge(sem, value)

        @block.gpsimd
        def _(pool):
            def load(i, k):
                if flip:
                    at_least(pool, flipped, at(i, k, 1))
                else:
                    at_least(pool, rows_done, at(i, k, 4, -4))
                e = i * 2 + k
                if flip:
                    pool.dma_start(up_raw[:, :, :], w_up(e)[0].rearrange("(a p) d -> p a d", p=P)).then_inc(w_in[k], 16)
                    pool.dma_start(down_raw[:, :], w_down(e)).then_inc(w_in[k], 16)
                else:
                    for g in range(2):
                        pool.dma_start(up[k][:, g * IN:(g + 1) * IN], w_up(e)[g]).then_inc(w_in[k], 16)
                    pool.dma_start(down[k][:, :, :], w_down(e).rearrange("(a p) c -> p a c", p=P)).then_inc(w_in[k], 16)

            experts(pool, lambda i: [load(i, k) for k in pair])

        @block.tensor
        def _(pe):
            def rows_of(i, k, c):
                s = 4 * k + c
                pe.wait_ge(hidden_ready, at(i, k, 8, 2 * c + 2))
                at_least(pe, rows_added, at(i, k, 4, c - 1))
                for j in range(4):
                    for h in range(2):
                        last = nc.tensor.matmul(rows_ps[:, s % 2, j * C:(j + 1) * C],
                                                hidden[s % 2][:, h, j * P:(j + 1) * P], down[k][:, h, :],
                                                start=h == 0, stop=h == 1)
                last.then_inc(rows_done, 1)

            def turn_weights(i, k):
                pe.wait_ge(w_in[k], i * (16 * n_w) + 16 * n_w)
                at_least(pe, w_ready, at(i, k, 2))
                at_least(pe, up_split, at(i, k, 1))
                for a in range(4):
                    nc.tensor.transpose(flip_ps[:, 0, a * P:(a + 1) * P], up_raw[:, a, :], per.ident[:, :])
                for a in range(2):
                    last = nc.tensor.transpose(flip_ps[:, 1, a * P:(a + 1) * P], down_raw[:, a * P:(a + 1) * P],
                                               per.ident[:, :])
                last.then_inc(flipped, 1)

            def step(i, k):
                if flip:
                    pe.wait_ge(w_ready, at(i, k, 2, 2))
                    pe.wait_ge(up_split, at(i, k, 1, 1))
                else:
                    pe.wait_ge(w_in[k], i * (16 * n_w) + 16 * n_w)
                for c in range(CHUNKS):
                    for h in range(2):
                        n = 8 * k + 2 * c + h
                        at_least(pe, hidden_ready, at(i, k, 8, 2 * c + h - 1))
                        cols = slice(c * HALF, (c + 1) * HALF)
                        for g in range(2):
                            w_cols = slice(g * IN + h * P, g * IN + (h + 1) * P)
                            parts = ([(up[k], x_high), (up_low[k], x_high), (up[k], x_low)] if flip
                                     else [(up[k], cols_in)])
                            for m, (w, x) in enumerate(parts):
                                last = nc.tensor.matmul(pair_ps[:, n % 2, g, :], w[:, w_cols], x[:, cols],
                                                        start=m == 0, stop=m == len(parts) - 1)
                        last.then_inc(pair_done, 1)
                    if flip and c == TURN_AT and following(i, k):
                        turn_weights(*following(i, k))
                    if c:
                        rows_of(i, k, c - 1)
                    elif k:
                        rows_of(i, 0, CHUNKS - 1)
                    elif not (isinstance(i, int) and i == 0):
                        rows_of(i - 1, 1, CHUNKS - 1)

            if flip:
                turn_weights(0, 0)
                pe.wait_ge(x_split, CHUNKS)
            experts(pe, lambda i: [step(i, k) for k in pair])
            rows_of((n_e - 1) // 2, (n_e - 1) % 2, CHUNKS - 1)

        @block.scalar
        def _(act):
            def copies(i, k):
                act.wait_ge(flipped, at(i, k, 1, 1))
                at_least(act, rows_done, at(i, k, 4, -4))
                nc.scalar.activation(up[k][:, :], flip_ps[:, 0, :], ACT.Copy).then_inc(w_ready, 1)
                nc.scalar.activation(down[k][:, :, :], flip_ps[:, 1, 0:IN].rearrange("p (a c) -> p a c", c=C),
                                     ACT.Copy).then_inc(w_ready, 1)

            def step(i, k):
                for n in range(8):
                    if flip and n == 2 * TURN_AT + 2 and following(i, k):
                        copies(*following(i, k))
                    act.wait_ge(pair_done, at(i, k, 8, n + 1))
                    at_least(act, hidden_ready, at(i, k, 8, n - 1))
                    nc.scalar.activation(gated[:, n % 2, :], pair_ps[:, n % 2, 0, :], ACT.Silu).then_inc(silu_done, 1)

            if flip:
                for c in range(CHUNKS):
                    cols = slice(c * HALF, (c + 1) * HALF)
                    nc.scalar.activation(x_high[:, cols], cols_in[:, cols], ACT.Copy).then_inc(x_rounded, 1)
                copies(0, 0)
            experts(act, lambda i: [step(i, k) for k in pair])

        @block.vector
        def _(dve):
            def my_share(i, k):
                if share is not None:
                    src = share[:, :, span(i * 2 + k, 1)].rearrange("p t a -> p (t a)")
                    nc.vector.tensor_scalar(mine[k][:, :], src, 1.0, None, ALU.mult).then_inc(mine_ready, 1)

            def add_rows(i, k, c):
                s = 4 * k + c
                dve.wait_ge(rows_done, at(i, k, 4, c + 1))
                if share is not None:
                    dve.wait_ge(mine_ready, at(i, k, 1, 1))
                at_least(dve, rows_added, at(i, k, 4, c))
                for j in range(4):
                    tile = 4 * c + j
                    psum = rows_ps[:, s % 2, j * C:(j + 1) * C]
                    if share is not None:
                        last = nc.vector.scalar_tensor_tensor(per.acc[:, tile, :], psum, mine[k][:, tile:tile + 1],
                                                              per.acc[:, tile, :], ALU.mult, ALU.add)
                    else:
                        last = nc.vector.tensor_tensor(per.acc[:, tile, :], psum, per.acc[:, tile, :], ALU.add)
                last.then_inc(rows_added, 1)

            def low_weights(i, k):
                dve.wait_ge(w_ready, at(i, k, 2, 1))
                nc.vector.tensor_tensor(up_low[k][:, :], flip_ps[:, 0, :], up[k][:, :].bitcast(F32),
                                        ALU.subtract).then_inc(up_split, 1)

            def step(i, k):
                for c in range(CHUNKS):
                    if flip and c == TURN_AT + 1 and following(i, k):
                        low_weights(*following(i, k))
                    for h in range(2):
                        n = 2 * c + h
                        dve.wait_ge(silu_done, at(i, k, 8, n + 1))
                        at_least(dve, rows_done, at(i, k, 4, c - 1))
                        nc.vector.tensor_tensor(hidden[c % 2][:, h, :], pair_ps[:, n % 2, 1, :], gated[:, n % 2, :],
                                                ALU.mult).then_inc(hidden_ready, 1)
                    if c:
                        add_rows(i, k, c - 1)
                    elif k:
                        add_rows(i, 0, CHUNKS - 1)
                    elif not (isinstance(i, int) and i == 0):
                        add_rows(i - 1, 1, CHUNKS - 1)
                    if c == 0:
                        my_share(i, k)

            if flip:
                for c in range(CHUNKS):
                    cols = slice(c * HALF, (c + 1) * HALF)
                    dve.wait_ge(x_rounded, c + 1)
                    nc.vector.tensor_tensor(x_low[:, cols], cols_in[:, cols], x_high[:, cols].bitcast(F32),
                                            ALU.subtract).then_inc(x_split, 1)
                low_weights(0, 0)
            experts(dve, lambda i: [step(i, k) for k in pair])
            add_rows((n_e - 1) // 2, (n_e - 1) % 2, CHUNKS - 1)


def layer3_ffn(nc, per, t):
    HID = 4 * C
    HB = HID // P
    with ExitStack() as ctx:
        held = Held(nc, ctx, "L3_held")
        w_t = {n: held.sb(n, [P, k, m]) for n, k, m in
               (("w1", 1, HID), ("w2", 1, HID), ("h1", HB, HID), ("h2", HB, HID), ("w3", HB, C))}
        s_cols = held.sb("s_cols", [P, 4, HB])
        s3_bc = held.sb("s3_bc", [P, C])
        with Stage(nc, "L3_weights") as st:
            raw = {n: st.sb(n + "_raw", [P, k, m]) for n, k, m in
                   (("w1", HB, C), ("w2", HB, C), ("h1", HB, HID), ("h2", HB, HID), ("w3", 1, HID))}
            tr = st.ps("tr", [P, 4, HALF])
            loaded = {n: st.sem("loaded_" + n) for n in raw}
            scales_in, flipped, copied = st.sem("scales_in"), st.sem("flipped"), st.sem("copied")
            groups = []
            for n in ("w1", "w2"):
                groups.append((n, [(o, 0) for o in range(HB)], w_t[n][:, 0, :]))
            for n in ("h1", "h2"):
                groups += [(n, [(o, i) for o in range(HB)], w_t[n][:, i, :]) for i in range(HB)]
            groups.append(("w3", [(0, i) for i in range(HB)], w_t["w3"][:, :, :].rearrange("p k m -> p (k m)")))
            block = st.begin()

            @block.sync
            def _(sp):
                for n, r in raw.items():
                    sp.dma_start(r[:, :, :], t[f"L3_ffn_{n}_w"].rearrange("(a p) i -> p a i", p=P)).then_inc(loaded[n], 16)

            @block.gpsimd
            def _(pool):
                for k, n in enumerate(("w1", "w2", "h1", "h2")):
                    pool.dma_start(s_cols[:, k, :], t[f"L3_ffn_{n}_s"].rearrange("(a p) -> p a", p=P),
                                   allow_slow_non_contiguous=True).then_inc(scales_in, 16)
                pool.dma_start(s3_bc[:, :], t["L3_ffn_w3_s"].rearrange("(a c) -> a c", a=1).partition_broadcast(P)
                               .rearrange("p a c -> p (a c)")).then_inc(scales_in, 16)
                pool.wait_ge(scales_in, 80)

            @block.tensor
            def _(pe):
                for g, (n, blocks, _) in enumerate(groups):
                    pe.wait_ge(loaded[n], 16)
                    if g >= 4:
                        pe.wait_ge(copied, g - 3)
                    for j, (o, i) in enumerate(blocks):
                        last = nc.tensor.transpose(tr[:, g % 4, j * P:(j + 1) * P], raw[n][:, o, i * P:(i + 1) * P],
                                                   per.ident[:, :])
                    last.then_inc(flipped, 1)

            @block.scalar
            def _(act):
                for g, (_, _, place) in enumerate(groups):
                    act.wait_ge(flipped, g + 1)
                    nc.scalar.activation(place, tr[:, g % 4, :], ACT.Copy).then_inc(copied, 1)

        with Stage(nc, "L3_ffn") as st:
            h_a = st.sb("h_a", [P, HB, TOKENS])
            h_b = st.sb("h_b", [P, HB, TOKENS])
            gated = st.sb("gated", [P, 2, HALF])
            scaled = st.sb("scaled", [P, 2, HALF])
            bank = st.ps("bank", [P, 8, HALF])
            filled, gate_done, made = st.sem("filled"), st.sem("gate_done"), st.sem("made")
            gelu_done, scaled_ready, added = st.sem("gelu_done"), st.sem("scaled_ready"), st.sem("added")
            N1 = CHUNKS * HB
            block = st.begin()

            @block.tensor
            def _(pe):
                def cols(c):
                    return slice(c * HALF, (c + 1) * HALF)
                for n in range(N1):
                    c, o = divmod(n, HB)
                    if n >= 4:
                        pe.wait_ge(made, n - 3)
                    for g, w in enumerate(("w1", "w2")):
                        last = nc.tensor.matmul(bank[:, 2 * (n % 4) + g, :], w_t[w][:, 0, o * P:(o + 1) * P],
                                                per.x_cols[:, cols(c)], start=True, stop=True)
                    last.then_inc(filled, 1)
                for layer, (w, src) in enumerate((("h1", h_a), ("h2", h_b))):
                    for n in range(N1):
                        c, o = divmod(n, HB)
                        m = layer * N1 + n
                        if layer == 0:
                            pe.wait_ge(made, HB * (c + 1) if m >= 8 else N1)
                        else:
                            pe.wait_ge(gelu_done, HB * (c + 1))
                        if m >= 8:
                            pe.wait_ge(gelu_done, m - 7)
                        for i in range(HB):
                            last = nc.tensor.matmul(bank[:, m % 8, :], w_t[w][:, i, o * P:(o + 1) * P],
                                                    src[:, i, cols(c)], start=i == 0, stop=i == HB - 1)
                        last.then_inc(filled, 1)
                for c in range(CHUNKS):
                    pe.wait_ge(gelu_done, N1 + HB * (c + 1))
                    if c == 0:
                        pe.wait_ge(gelu_done, 2 * N1)
                    for j in range(4):
                        for i in range(HB):
                            last = nc.tensor.matmul(bank[:, c, j * C:(j + 1) * C],
                                                    h_a[:, i, c * HALF + j * P:c * HALF + (j + 1) * P],
                                                    w_t["w3"][:, i, :], start=i == 0, stop=i == HB - 1)
                    last.then_inc(filled, 1)

            @block.scalar
            def _(act):
                for n in range(N1):
                    c, o = divmod(n, HB)
                    act.wait_ge(filled, n + 1)
                    if n >= 2:
                        act.wait_ge(made, n - 1)
                    nc.scalar.activation(gated[:, n % 2, :], bank[:, 2 * (n % 4), :], ACT.Silu,
                                         scale=s_cols[:, 0, o:o + 1]).then_inc(gate_done, 1)
                for layer, dst in enumerate((h_b, h_a)):
                    for n in range(N1):
                        c, o = divmod(n, HB)
                        m = layer * N1 + n
                        act.wait_ge(filled, N1 + m + 1)
                        nc.scalar.activation(dst[:, o, c * HALF:(c + 1) * HALF], bank[:, m % 8, :], ACT.Gelu,
                                             scale=s_cols[:, 2 + layer, o:o + 1]).then_inc(gelu_done, 1)

            @block.vector
            def _(dve):
                for n in range(N1):
                    c, o = divmod(n, HB)
                    dve.wait_ge(gate_done, n + 1)
                    nc.vector.scalar_tensor_tensor(h_a[:, o, c * HALF:(c + 1) * HALF], bank[:, 2 * (n % 4) + 1, :],
                                                   s_cols[:, 1, o:o + 1], gated[:, n % 2, :],
                                                   ALU.mult, ALU.mult).then_inc(made, 1)
                for c in range(CHUNKS):
                    dve.wait_ge(filled, 3 * N1 + c + 1)
                    if c >= 2:
                        dve.wait_ge(added, c - 1)
                    tiles = slice(4 * c, 4 * c + 4)
                    nc.vector.tensor_tensor(scaled[:, c % 2, :].rearrange("p (t c) -> p t c", c=C),
                                            bank[:, c, :].rearrange("p (t c) -> p t c", c=C),
                                            s3_bc[:, :].unsqueeze(1).to_broadcast([P, 4, C]), ALU.mult).then_inc(scaled_ready, 1)
                    dve.wait_ge(scaled_ready, c + 1)
                    nc.vector.tensor_tensor(per.acc[:, tiles, :], scaled[:, c % 2, :].rearrange("p (t c) -> p t c", c=C),
                                            per.x_rows[:, tiles, :], ALU.add).then_inc(added, 1)
    norm_stage(nc, per, "L3_norm1", per.acc, per.x_rows, to_cols=False)



def build_network(nc, t, out, upto=8, start=0):
    with ExitStack() as ctx:
        per = Persistent(nc, ctx)
        load_stage(nc, per, t["L0_attn_x"], t["ident"])
        parts = [
            lambda: layer0_attention(nc, per, t),
            lambda: layer0_ffn(nc, per, t),
            lambda: layer1_attention(nc, per, t),
            lambda: layer1_ffn(nc, per, t),
            lambda: layer2_attention(nc, per, t),
            lambda: layer2_ffn(nc, per, t),
            lambda: layer3_attention(nc, per, t),
            lambda: layer3_ffn(nc, per, t),
        ]
        for part in parts[start:upto]:
            part()
        store_stage(nc, per, out)


def layer0_attention(nc, per, t):
    with ExitStack() as ctx:
        heads = SmallHeads(nc, Held(nc, ctx, "L0"))
        small_qkv_stage(nc, per, "L0_qkv", heads, t["L0_attn_W_qkv"], None, t["L0_attn_b_qkv"],
                        (t["rotation"], t["cos"], t["sin"]))
        attention_stage(nc, per, "L0_attn", "small", H8, D8, D8 ** -0.5,
                        t["L0_attn_W_out"].rearrange("(h d) o -> d h o", d=D8), heads=heads)
    norm_stage(nc, per, "L0_norm0", per.acc, per.x_rows, bias=t["L0_attn_b_out"])


def layer1_attention(nc, per, t):
    with ExitStack() as ctx:
        heads = SmallHeads(nc, Held(nc, ctx, "L1"))
        small_qkv_stage(nc, per, "L1_qkv", heads, t["L1_attn_w_qkv"], t["L1_attn_w_out"], None, None)
        window_attention_stage(nc, per, "L1_attn", heads, t["mask"], D8 ** -0.5)
    norm_stage(nc, per, "L1_norm0", per.acc, per.x_rows)


def layer2_attention(nc, per, t):
    w_q, w_kv = t["L2_attn_Wq"], t["L2_attn_Wkv"]
    norm_stage(nc, per, "L2_norm_in", per.x_rows, per.acc, affine=(t["L2_attn_norm_w"], t["L2_attn_norm_b"]))
    attention_stage(nc, per, "L2_attn", "mqa", 8, 64, 64 ** -0.5,
                    t["L2_attn_Wo"].rearrange("(h d) o -> d h o", d=64),
                    weights=(lambda i: w_q[:, span(i * 64, 64)], lambda i: w_kv[:, 0:64],
                             lambda i: w_kv[:, 64:128]), x_init=False)
    norm_stage(nc, per, "L2_norm_out", per.acc, per.acc, affine=(t["L2_attn_out_norm_w"], t["L2_attn_out_norm_b"]),
               plus=per.x_rows, to_cols=False)
    norm_stage(nc, per, "L2_norm0", per.acc, per.x_rows)


def layer3_attention(nc, per, t):
    w = [t[f"L3_attn_W{n}"].rearrange("h d e -> (h d) e") for n in "qkv"]
    attention_stage(nc, per, "L3_attn", "full", 16, 64, 64 ** -0.5,
                    t["L3_attn_Wp"].rearrange("(e h) o -> e h o", h=16),
                    weights=[lambda i, m=m: m[span(i * C, C), :] for m in w])
    norm_stage(nc, per, "L3_norm0", per.acc, per.x_rows, bias=t["L3_attn_bp"])


class Held:

    def __init__(self, nc, ctx, name):
        self.nc, self.ctx, self.name = nc, ctx, name

    def sb(self, name, shape, dt=F32):
        return self.ctx.enter_context(self.nc.sbuf_tensor(f"{self.name}_{name}", shape, dt))


def constants():
    d = np.arange(P)
    rotation = np.zeros((P, P), np.float32)
    for o in range(P):
        h, r = divmod(o, D8)
        if r < D8 // 2:
            rotation[h * D8 + r + D8 // 2, o] = -1.0
        else:
            rotation[h * D8 + r - D8 // 2, o] = 1.0
    inv = (np.float32(1.0) / np.power(np.float32(10000.0), np.arange(0, D8, 2, dtype=np.float32) / np.float32(D8))
           ).astype(np.float32)
    angle = (np.arange(SEQ, dtype=np.float32)[None, :] * inv[d % (D8 // 2)][:, None]).astype(np.float32)
    q, p = np.arange(P)[:, None], np.arange(P)[None, :]
    own = (p <= q) & (q - p < WINDOW)
    before = q + P - p < WINDOW
    ok = np.zeros((P, 2, HALF), bool)
    ok[:, 0, 0:P] = own | (p < PREFIX) & (p <= q)
    ok[:, 0, 2 * P:3 * P] = before | (p < PREFIX)
    ok[:, 0, 3 * P:] = own
    ok[:, 1, :] = np.concatenate([before, own] * 2, axis=1)
    return {"ident": np.eye(P, dtype=np.float32), "rotation": rotation,
            "cos": np.cos(angle).astype(np.float32), "sin": np.sin(angle).astype(np.float32),
            "mask": np.where(ok, 0.0, MASKED).astype(np.float32),
            "below": np.triu(np.ones((P, P), np.float32), 1),
            "up_to": np.tile(np.tril(np.ones((N_ROUTED, N_ROUTED), np.float32)), (P, 1, 1)),
            "tile_starts": np.tile(np.arange(TILES, dtype=np.float32) * P, (P, 1)),
            "tile_numbers": np.arange(SORTED_TILES, dtype=np.float32)[None, :],
            "reversed": np.tile(np.arange(32, 0, -1, dtype=np.float32), (P, 1))}


def kernel(**inputs):
    import concourse.bacc as bacc
    from concourse.bass_utils import run_bass_kernel_spmd

    nc = bacc.Bacc("TRN2", target_bir_lowering=False, num_devices=1)
    arrays, t = {}, {}
    for name, a in {**inputs, **constants()}.items():
        arrays[name] = np.ascontiguousarray(a)
        t[name] = nc.dram_tensor(name, arrays[name].shape, mybir.dt.from_np(arrays[name].dtype),
                                 kind="ExternalInput").ap()
    out = nc.dram_tensor("out", (BATCH, SEQ, C), F32, kind="ExternalOutput").ap()
    build_network(nc, t, out)
    return run_bass_kernel_spmd(nc, [arrays], core_ids=[0]).results[0]["out"]
```
